# Optimizing a Trainium2 kernel written in Bass

```python
import numpy as np
import jax
import jax.numpy as jnp

def _softmax(x, axis=-1):
    return jax.nn.softmax(x, axis=axis)

def _gelu(x):
    return jax.nn.gelu(x, approximate=True)

def _silu(x):
    return jax.nn.silu(x)

def _sigmoid(x):
    return jax.nn.sigmoid(x)

def _layernorm(x, axis=-1, eps=1e-05):
    m = jnp.mean(x, axis=axis, keepdims=True)
    v = jnp.var(x, axis=axis, keepdims=True)
    return (x - m) / jnp.sqrt(v + eps)

def _scatter_add(tgt, idx, src, axis=0):
    return tgt.at[idx].add(src)

def _segment_sum(src, seg, n):
    return jax.ops.segment_sum(src, seg, n)
kernel_name = 'mk_xattn_ffn_d1_seqx_r8_8a40aa'

def setup_inputs(seed: int=0):
    np.random.seed(seed)
    _w = jnp.asarray

    def _rec_inputs():
        import jax
        import jax.numpy as jnp
        _rk = jax.random.key(seed)
        x = 7.22e-05 + 1 * jax.random.normal(jax.random.fold_in(_rk, 1), (4, 256, 128), jnp.float32)
        _lenS = 256 - jax.random.randint(jax.random.fold_in(_rk, 7), (4,), 0, max(1, 256 // 4) + 1, jnp.int32)
        _lenS2 = 256 - jax.random.randint(jax.random.fold_in(_rk, 8), (4,), 0, max(1, 256 // 4) + 1, jnp.int32)
        _ctx_768P = jax.random.normal(jax.random.fold_in(_rk, 11), (4, 16, 96), jnp.float32)
        _ctx_768c = jax.random.dirichlet(jax.random.fold_in(_rk, 511), 0.3 * jnp.ones((16,), jnp.float32), (4, 256))
        _ctx_768t = jnp.einsum('bsk,bkd->bsd', _ctx_768c, _ctx_768P)
        _ctx_768t = _ctx_768t * jax.lax.rsqrt(jnp.mean(jnp.square(_ctx_768t)) + 1e-12) * 0.953939
        ctx_768 = 2.09791e-05 + 1.00001 * (_ctx_768t + 0.3 * jax.random.normal(jax.random.fold_in(_rk, 611), (4, 256, 96), jnp.float32))
        return (x, ctx_768)
    x, ctx_768 = _rec_inputs()

    def _L0_xattn_setup():
        import jax, jax.numpy as jnp
        import numpy as np
        NUM_HEADS = 16
        key = jax.random.key(seed)
        ks = jax.random.split(key, 8)
        dim, cond_dim = (128, 96)
        B, N, condN = (4, 256, 128)
        s = lambda k, shp, fan: jax.random.normal(k, shp, dtype=jnp.float32) * fan ** (-0.5)
        return {'x': jax.random.normal(ks[0], (B, N, dim), dtype=jnp.float32), 'cond': jax.random.normal(ks[1], (B, condN, cond_dim), dtype=jnp.float32), 'q_w': s(ks[2], (dim, dim), dim), 'q_b': jnp.zeros((dim,), jnp.float32), 'kv_w': s(ks[3], (cond_dim, 2 * dim), cond_dim), 'kv_b': jnp.zeros((2 * dim,), jnp.float32), 'proj_w': s(ks[4], (dim, dim), dim), 'proj_b': jnp.zeros((dim,), jnp.float32)}
    _L0_xattn_all = _L0_xattn_setup()
    _L0_xattn_in = {k: v for k, v in _L0_xattn_all.items() if k in ('q_w', 'q_b', 'kv_w', 'kv_b', 'proj_w', 'proj_b')}
    del _L0_xattn_all

    def _L0_ffn_setup():
        import jax, jax.numpy as jnp
        import numpy as np
        DIM = 128
        NQ = 16
        NKV = 4
        HD = DIM // NQ
        HID = 256
        E = 8
        B, S = (1, 128)
        EPS = 1e-06

        def rmsnorm(x, w):
            ms = jnp.mean(x * x, axis=-1, keepdims=True)
            return w * (x * jax.lax.rsqrt(ms + EPS))

        def rope_tables(seq_len, head_dim):
            inv_freq = 1.0 / 10000.0 ** (jnp.arange(0, head_dim, 2, dtype=jnp.float32) / head_dim)
            t = jnp.arange(seq_len, dtype=jnp.float32)
            freqs = jnp.einsum('i,j->ij', t, inv_freq)
            return (jnp.cos(freqs), jnp.sin(freqs))

        def apply_rope(x, cos, sin):
            c = cos[None, :, None, :]
            s = sin[None, :, None, :]
            half = x.shape[-1] // 2
            x1, x2 = (x[..., :half], x[..., half:])
            return jnp.concatenate([x1 * c - x2 * s, x1 * s + x2 * c], axis=-1)

        def _forward(x, ln1_w, ln2_w, Wq, bq, Wk, bk, Wv, bv, qn_w, kn_w, Wg, bg, Wo, bo, Wr, br, W1, b1, W2, b2):
            batch, seq, _ = x.shape
            cos, sin = rope_tables(seq, HD)
            h = rmsnorm(x, ln1_w)
            q = (h @ Wq + bq).reshape(batch, seq, NQ, HD)
            k = (h @ Wk + bk).reshape(batch, seq, NKV, HD)
            v = (h @ Wv + bv).reshape(batch, seq, NKV, HD)
            q = rmsnorm(apply_rope(q, cos, sin), qn_w)
            k = rmsnorm(apply_rope(k, cos, sin), kn_w)
            rep = NQ // NKV
            k = jnp.repeat(k, rep, axis=2)
            v = jnp.repeat(v, rep, axis=2)
            scores = jnp.einsum('bthd,bshd->bhts', q, k) / np.sqrt(HD)
            causal = jnp.tril(jnp.ones((seq, seq), dtype=bool))
            scores = jnp.where(causal[None, None], scores, -jnp.inf)
            attn = jax.nn.softmax(scores, axis=-1)
            out = jnp.einsum('bhts,bshd->bthd', attn, v)
            gate = jax.nn.sigmoid(out @ Wg + bg)
            out = (out * gate).reshape(batch, seq, DIM)
            x = x + out @ Wo + bo
            h2 = rmsnorm(x, ln2_w)
            logits = h2 @ Wr + br
            top1 = jnp.argmax(logits, axis=-1).reshape(-1)
            xt = h2.reshape(-1, DIM)
            u = jnp.einsum('td,edf->tef', xt, W1) + b1
            u1, u2 = (u[..., :HID], u[..., HID:])
            act = u1 * jax.nn.sigmoid(u2)
            y_all = jnp.einsum('teh,ehd->ted', act, W2) + b2
            y = jnp.take_along_axis(y_all, top1[:, None, None], axis=1)[:, 0, :]
            return x + y.reshape(batch, seq, DIM)
        key = jax.random.key(seed)
        ks = jax.random.split(key, 20)
        sc = lambda fan_in: 1.0 / np.sqrt(fan_in)
        d = {}
        d['x'] = jax.random.normal(ks[0], (B, S, DIM), dtype=jnp.float32)
        d['ln1_w'] = jnp.ones((DIM,), jnp.float32)
        d['ln2_w'] = jnp.ones((DIM,), jnp.float32)
        d['Wq'] = jax.random.normal(ks[1], (DIM, DIM), jnp.float32) * sc(DIM)
        d['bq'] = jnp.zeros((DIM,), jnp.float32)
        d['Wk'] = jax.random.normal(ks[2], (DIM, HD * NKV), jnp.float32) * sc(DIM)
        d['bk'] = jnp.zeros((HD * NKV,), jnp.float32)
        d['Wv'] = jax.random.normal(ks[3], (DIM, HD * NKV), jnp.float32) * sc(DIM)
        d['bv'] = jnp.zeros((HD * NKV,), jnp.float32)
        d['qn_w'] = jnp.ones((HD,), jnp.float32)
        d['kn_w'] = jnp.ones((HD,), jnp.float32)
        d['Wg'] = jax.random.normal(ks[4], (HD, HD), jnp.float32) * sc(HD)
        d['bg'] = jnp.zeros((HD,), jnp.float32)
        d['Wo'] = jax.random.normal(ks[5], (DIM, DIM), jnp.float32) * sc(DIM)
        d['bo'] = jnp.zeros((DIM,), jnp.float32)
        d['Wr'] = jax.random.normal(ks[6], (DIM, E), jnp.float32) * sc(DIM)
        d['br'] = jnp.zeros((E,), jnp.float32)
        d['W1'] = jax.random.normal(ks[7], (E, DIM, 2 * HID), jnp.float32) * sc(DIM)
        d['b1'] = jnp.zeros((E, 2 * HID), jnp.float32)
        d['W2'] = jax.random.normal(ks[8], (E, HID, DIM), jnp.float32) * sc(HID)
        d['b2'] = jnp.zeros((E, DIM), jnp.float32)
        return d
    _L0_ffn_all = _L0_ffn_setup()
    _L0_ffn_in = {k: v for k, v in _L0_ffn_all.items() if k in ('ln1_w', 'ln2_w', 'Wq', 'bq', 'Wk', 'bk', 'Wv', 'bv', 'qn_w', 'kn_w', 'Wg', 'bg', 'Wo', 'bo', 'Wr', 'br', 'W1', 'b1', 'W2', 'b2')}
    del _L0_ffn_all
    return {'x': x, 'ctx_768': ctx_768, 'L0_xattn_q_w': _L0_xattn_in['q_w'], 'L0_xattn_q_b': _L0_xattn_in['q_b'], 'L0_xattn_kv_w': _L0_xattn_in['kv_w'], 'L0_xattn_kv_b': _L0_xattn_in['kv_b'], 'L0_xattn_proj_w': _L0_xattn_in['proj_w'], 'L0_xattn_proj_b': _L0_xattn_in['proj_b'], 'L0_ffn_ln1_w': _L0_ffn_in['ln1_w'], 'L0_ffn_ln2_w': _L0_ffn_in['ln2_w'], 'L0_ffn_Wq': _L0_ffn_in['Wq'], 'L0_ffn_bq': _L0_ffn_in['bq'], 'L0_ffn_Wk': _L0_ffn_in['Wk'], 'L0_ffn_bk': _L0_ffn_in['bk'], 'L0_ffn_Wv': _L0_ffn_in['Wv'], 'L0_ffn_bv': _L0_ffn_in['bv'], 'L0_ffn_qn_w': _L0_ffn_in['qn_w'], 'L0_ffn_kn_w': _L0_ffn_in['kn_w'], 'L0_ffn_Wg': _L0_ffn_in['Wg'], 'L0_ffn_bg': _L0_ffn_in['bg'], 'L0_ffn_Wo': _L0_ffn_in['Wo'], 'L0_ffn_bo': _L0_ffn_in['bo'], 'L0_ffn_Wr': _L0_ffn_in['Wr'], 'L0_ffn_br': _L0_ffn_in['br'], 'L0_ffn_W1': _L0_ffn_in['W1'], 'L0_ffn_b1': _L0_ffn_in['b1'], 'L0_ffn_W2': _L0_ffn_in['W2'], 'L0_ffn_b2': _L0_ffn_in['b2']}

def reference(x, ctx_768, L0_xattn_q_w, L0_xattn_q_b, L0_xattn_kv_w, L0_xattn_kv_b, L0_xattn_proj_w, L0_xattn_proj_b, L0_ffn_ln1_w, L0_ffn_ln2_w, L0_ffn_Wq, L0_ffn_bq, L0_ffn_Wk, L0_ffn_bk, L0_ffn_Wv, L0_ffn_bv, L0_ffn_qn_w, L0_ffn_kn_w, L0_ffn_Wg, L0_ffn_bg, L0_ffn_Wo, L0_ffn_bo, L0_ffn_Wr, L0_ffn_br, L0_ffn_W1, L0_ffn_b1, L0_ffn_W2, L0_ffn_b2):
    import jax
    import jax.numpy as jnp

    def _L0_xattn_ref(x, cond, q_w, q_b, kv_w, kv_b, proj_w, proj_b):
        import jax, jax.numpy as jnp
        import numpy as np
        NUM_HEADS = 16
        B, N, C = x.shape
        condN = cond.shape[1]
        H = NUM_HEADS
        hd = C // H
        scale = hd ** (-0.5)
        q = (x @ q_w + q_b).reshape(B, N, H, hd).transpose(0, 2, 1, 3)
        kv = (cond @ kv_w + kv_b).reshape(B, condN, 2, H, hd)
        k = kv[:, :, 0].transpose(0, 2, 1, 3)
        v = kv[:, :, 1].transpose(0, 2, 1, 3)
        attn = jnp.einsum('bhnd,bhmd->bhnm', q * scale, k)
        attn = jax.nn.softmax(attn, axis=-1)
        out = jnp.einsum('bhnm,bhmd->bhnd', attn, v)
        out = out.transpose(0, 2, 1, 3).reshape(B, N, C)
        return out @ proj_w + proj_b

    def _L0_ffn_ref(x, ln1_w, ln2_w, Wq, bq, Wk, bk, Wv, bv, qn_w, kn_w, Wg, bg, Wo, bo, Wr, br, W1, b1, W2, b2):
        import jax, jax.numpy as jnp
        import numpy as np
        DIM = 128
        NQ = 16
        NKV = 4
        HD = DIM // NQ
        HID = 256
        E = 8
        B, S = (1, 128)
        EPS = 1e-06

        def rmsnorm(x, w):
            ms = jnp.mean(x * x, axis=-1, keepdims=True)
            return w * (x * jax.lax.rsqrt(ms + EPS))

        def rope_tables(seq_len, head_dim):
            inv_freq = 1.0 / 10000.0 ** (jnp.arange(0, head_dim, 2, dtype=jnp.float32) / head_dim)
            t = jnp.arange(seq_len, dtype=jnp.float32)
            freqs = jnp.einsum('i,j->ij', t, inv_freq)
            return (jnp.cos(freqs), jnp.sin(freqs))

        def apply_rope(x, cos, sin):
            c = cos[None, :, None, :]
            s = sin[None, :, None, :]
            half = x.shape[-1] // 2
            x1, x2 = (x[..., :half], x[..., half:])
            return jnp.concatenate([x1 * c - x2 * s, x1 * s + x2 * c], axis=-1)

        def _forward(x, ln1_w, ln2_w, Wq, bq, Wk, bk, Wv, bv, qn_w, kn_w, Wg, bg, Wo, bo, Wr, br, W1, b1, W2, b2):
            batch, seq, _ = x.shape
            cos, sin = rope_tables(seq, HD)
            h = rmsnorm(x, ln1_w)
            q = (h @ Wq + bq).reshape(batch, seq, NQ, HD)
            k = (h @ Wk + bk).reshape(batch, seq, NKV, HD)
            v = (h @ Wv + bv).reshape(batch, seq, NKV, HD)
            q = rmsnorm(apply_rope(q, cos, sin), qn_w)
            k = rmsnorm(apply_rope(k, cos, sin), kn_w)
            rep = NQ // NKV
            k = jnp.repeat(k, rep, axis=2)
            v = jnp.repeat(v, rep, axis=2)
            scores = jnp.einsum('bthd,bshd->bhts', q, k) / np.sqrt(HD)
            causal = jnp.tril(jnp.ones((seq, seq), dtype=bool))
            scores = jnp.where(causal[None, None], scores, -jnp.inf)
            attn = jax.nn.softmax(scores, axis=-1)
            out = jnp.einsum('bhts,bshd->bthd', attn, v)
            gate = jax.nn.sigmoid(out @ Wg + bg)
            out = (out * gate).reshape(batch, seq, DIM)
            x = x + out @ Wo + bo
            h2 = rmsnorm(x, ln2_w)
            logits = h2 @ Wr + br
            top1 = jnp.argmax(logits, axis=-1).reshape(-1)
            xt = h2.reshape(-1, DIM)
            u = jnp.einsum('td,edf->tef', xt, W1) + b1
            u1, u2 = (u[..., :HID], u[..., HID:])
            act = u1 * jax.nn.sigmoid(u2)
            y_all = jnp.einsum('teh,ehd->ted', act, W2) + b2
            y = jnp.take_along_axis(y_all, top1[:, None, None], axis=1)[:, 0, :]
            return x + y.reshape(batch, seq, DIM)
        return _forward(x, ln1_w, ln2_w, Wq, bq, Wk, bk, Wv, bv, qn_w, kn_w, Wg, bg, Wo, bo, Wr, br, W1, b1, W2, b2)
    x = x + _L0_xattn_ref(_layernorm(x, axis=-1), ctx_768, L0_xattn_q_w, L0_xattn_q_b, L0_xattn_kv_w, L0_xattn_kv_b, L0_xattn_proj_w, L0_xattn_proj_b)
    x = x + _L0_ffn_ref(_layernorm(x, axis=-1), L0_ffn_ln1_w, L0_ffn_ln2_w, L0_ffn_Wq, L0_ffn_bq, L0_ffn_Wk, L0_ffn_bk, L0_ffn_Wv, L0_ffn_bv, L0_ffn_qn_w, L0_ffn_kn_w, L0_ffn_Wg, L0_ffn_bg, L0_ffn_Wo, L0_ffn_bo, L0_ffn_Wr, L0_ffn_br, L0_ffn_W1, L0_ffn_b1, L0_ffn_W2, L0_ffn_b2)
    return x

_drawn_inputs = setup_inputs


def setup_inputs(seed=0):
    import zlib

    import numpy as np

    out = dict(_drawn_inputs(seed))
    spreads = {'L0_xattn_q_b': (0.0, 0.1),
     'L0_xattn_kv_b': (0.0, 0.1),
     'L0_xattn_proj_b': (0.0, 0.1),
     'L0_ffn_ln1_w': (1.0, 0.2),
     'L0_ffn_ln2_w': (1.0, 0.2),
     'L0_ffn_bq': (0.0, 0.1),
     'L0_ffn_bk': (0.0, 0.1),
     'L0_ffn_bv': (0.0, 0.1),
     'L0_ffn_qn_w': (1.0, 0.2),
     'L0_ffn_kn_w': (1.0, 0.2),
     'L0_ffn_bg': (0.0, 0.1),
     'L0_ffn_bo': (0.0, 0.1),
     'L0_ffn_br': (0.0, 0.1),
     'L0_ffn_b1': (0.0, 0.293),
     'L0_ffn_b2': (0.0, 0.1)}
    factors = {}
    for name, (base, spread) in spreads.items():
        noise = np.random.default_rng([zlib.crc32(name.encode()), seed]).standard_normal(out[name].shape)
        drawn = base * np.exp(spread * noise) if base else spread * noise
        out[name] = jnp.asarray(drawn.astype(out[name].dtype))
    for name, factor in factors.items():
        out[name] = (out[name] * factor).astype(out[name].dtype)
    return out
```

```python
import numpy as np
import concourse.bass as bass
from concourse import mybir
from contextlib import ExitStack

B, T, C = 4, 256, 128
CD = 96
H, HD = 16, 8
G = 4
E, HID = 8, 256
P = 128
TT = T // P
NT = B * TT
QKV = C + 2 * G * HD
NPART = 3
ROWS = NPART * NPART * HD
KROWS = 96
RING = 3
PRING = 4
UNITS, BEATS = 4, 8
SCALE = HD ** -0.5

C_QB, C_KB, C_LN1, C_LN2, C_QN, C_KN, C_BG, C_B1 = 0, 1, 2, 3, 4, 5, 6, 7
NCOL = C_B1 + E * 4
R_VB, R_PB, R_BQKV, R_BO, R_BR = 0, C, 2 * C, 2 * C + QKV, 3 * C + QKV
NROW = R_BR + E


def tuned(nc, x, ctxT, cols, rows, wq, wk, wv, wp, wqkv, wg, wo, wr, w1, w2, b2, ident, tri, rope,
          revs, ones_row, zero_row, parts_dram, out):
    fp32, bf16 = mybir.dt.float32, mybir.dt.bfloat16
    ALU, ACT, AX = mybir.AluOpType, mybir.ActivationFunctionType, mybir.AxisListType
    ctx = ExitStack()
    with ctx:
        def sb(name, shape, dt=fp32):
            return ctx.enter_context(nc.sbuf_tensor(name, shape, dt))

        def ps(name, cols):
            return ctx.enter_context(nc.psum_tensor(name, [P, cols], fp32))

        def sem(name):
            return ctx.enter_context(nc.semaphore(name))

        X = sb("X", [P, NT, C])
        CT = sb("CT", [CD, B * T])
        COL = sb("COL", [P, NCOL])
        ROW = sb("ROW", [P, NROW])
        WQ, WK, WV = sb("WQ", [C, C]), sb("WK", [CD, C]), sb("WV", [CD, C])
        WP, WQKV = sb("WP", [C, C]), sb("WQKV", [C, QKV])
        WG, WO, WR = sb("WG", [C, C]), sb("WO", [C, C]), sb("WR", [C, E])
        W1 = sb("W1", [C, E, 2 * HID])
        W2 = sb("W2", [P, E, 2, C])
        B2 = sb("B2", [E, C])
        ID = sb("ID", [P, P])
        IDB = sb("IDB", [P, P], bf16)
        TRI = sb("TRI", [P, P])
        TRIB = sb("TRIB", [P, 4, P], bf16)
        ROPE = sb("ROPE", [P, TT, 2, HD])
        REV = sb("REV", [P, E])
        NEGHALF = sb("NEGHALF", [P, 64])
        QBS = sb("QBS", [P, 1])
        QNS = sb("QNS", [P, 1])
        BGH = sb("BGH", [P, 1])
        XB = sb("XB", [P, NT, C])
        X1 = sb("X1", [P, NT, C])
        Z = sb("Z", [P, NT, C])
        ZB = sb("ZB", [P, NT, C])
        RR = sb("RR", [P, NT, C])
        MV1 = sb("MV1", [P, TT, 2])
        ST = sb("ST", [P, TT, 6])
        SM1 = sb("SM1", [P, 8, TT])
        XN = sb("XN", [P, TT, C])
        XNT = sb("XNT", [C, T])
        QKF = sb("QKF", [P, 2, T])
        R1 = sb("R1", [P, 2, T])
        PT = sb("PT", [P, NPART, 2, T], bf16)
        QA = [sb(f"QA{i}", [KROWS, H, T], bf16) for i in range(RING)]
        KA = [sb(f"KA{i}", [KROWS, H, T], bf16) for i in range(RING)]
        VA = [sb(f"VA{i}", [P, TT, H, 32]) for i in range(RING)]
        VB = [sb(f"VB{i}", [P, TT, G, 32]) for i in range(RING)]
        NEGM = sb("NEGM", [P, TT, H])
        MHL = sb("MHL", [P, 2, TT, H], bf16)
        MTS = sb("MTS", [2 * TT * H, P], bf16)
        EX = [sb(f"EX{i}", [P, 4 * T]) for i in range(PRING)]
        OS = sb("OS", [P, 2 * T])
        RC = sb("RC", [P, 16, 2])
        ON = sb("ON", [P, 16, 16])
        ONT = sb("ONT", [C, T])
        ST2 = sb("ST2", [P, TT, 6])
        MV2 = sb("MV2", [P, TT, 2])
        SM2 = sb("SM2", [P, 8, TT])
        HZ = sb("HZ", [P, TT, C])
        HT = sb("HT", [C, T])
        QKVS = sb("QKVS", [P, TT, QKV])
        NH2 = H + G
        SQ = sb("SQ", [P, TT, NH2 * HD])
        SSQ = sb("SSQ", [P, TT * NH2])
        RQ = sb("RQ", [P, TT * NH2])
        ROT = sb("ROT", [P, TT, NH2, HD])
        ROTS = sb("ROTS", [P, TT, NH2, HD])
        QN = sb("QN", [P, TT, NH2 * HD])
        TH = sb("TH", [C, T])
        GT = sb("GT", [C, T])
        XP = sb("XP", [P, TT, C])
        SQX = sb("SQX", [P, TT, C])
        SS3 = sb("SS3", [P, 4, TT])
        H2 = sb("H2", [P, TT, C])
        H2T = sb("H2T", [C, B * T])
        LG = sb("LG", [P, TT, E])
        MXL = sb("MXL", [P, 2, TT])
        EQ = sb("EQ", [P, TT, E])
        OH = sb("OH", [P, NT, E])
        OHT = sb("OHT", [E, B * T])
        SG = [sb(f"SG{i}", [P, 4 * P]) for i in range(2)]
        AC = [sb(f"AC{i}", [P, 2, 4 * P]) for i in range(2)]

        S = [ps(f"S{i}", 1024) for i in range(2)]
        MXX = ps("MXX", 1024)
        MX = [MXX[:, 512 * i:512 * i + 512] for i in range(2)]
        O = ps("O", 512)
        MS = ps("MS", 512)
        MSB = MS[:, :].bitcast(bf16)
        OHP = O[:, :]
        U = [S[0], S[1], MXX]
        Y = [O, MS]

        ld = {k: sem(f"ld_{k}") for k in ("x0", "x1", "ctx", "cols", "rows", "id", "wqk", "wv", "wp", "wqkv",
                                          "tri", "rope", "wg", "wo", "wr", "w1", "w2", "b2", "rev", "pad")}
        cst = sem("constants_ready")
        ocst = sem("scaled_wo_ready")
        xb_ready = sem("xb_ready")
        va_zero = sem("va_zero")
        dve_step = sem("dve_step")
        pool_step = sem("pool_step")
        act_step = sem("act_step")
        scores = sem("scores")
        probs = sem("probs")
        masked = sem("masked")
        pv = sem("pv")
        mx_scores = sem("mx_scores")
        mx_taken = sem("mx_taken")
        mhl = sem("mhl")
        m_t = sem("m_t")
        mts = sem("mts")
        m_rows = [sem(f"m_rows{i}") for i in range(RING)]
        m_sent = sem("m_sent")
        mv1 = sem("mv1")
        rstd1 = sem("rstd1")
        xn = sem("xn")
        xn_t = sem("xn_t")
        xnt = sem("xnt")
        qk_ps = sem("qk_ps")
        v_ps = sem("v_ps")
        va = sem("va")
        vb = sem("vb")
        qkf = sem("qkf")
        part1, rest1, part2, part3 = sem("part1"), sem("rest1"), sem("part2"), sem("part3")
        parts_out = sem("parts_out")
        stacked = [sem(f"stacked{i}") for i in range(RING)]
        o_sb = sem("o_sb")
        o_t = sem("o_t")
        on = sem("on")
        on_t = sem("on_t")
        ont = sem("ont")
        pj = sem("pj")
        mv2 = sem("mv2")
        rstd2 = sem("rstd2")
        hz = sem("hz")
        hz_t = sem("hz_t")
        ht = sem("ht")
        qkv_ps = sem("qkv_ps")
        qkvs = sem("qkvs")
        sq = sem("sq")
        ssq = sem("ssq")
        rq = sem("rq")
        qn = sem("qn")
        qn_t = sem("qn_t")
        gate_ps = sem("gate_ps")
        th = sem("th")
        gated = sem("gated")
        wo_ps = sem("wo_ps")
        xp = sem("xp")
        ss3 = sem("ss3")
        rstd3 = sem("rstd3")
        h2 = sem("h2")
        h2_t = sem("h2_t")
        h2t = sem("h2t")
        lg_ps = sem("lg_ps")
        oh = sem("oh")
        z_ready = sem("z_ready")
        rr = sem("rr")
        oh_t, oht = sem("oh_t"), sem("oht")
        u_ps, sg, ac, y_ps, acc = sem("u_ps"), sem("sg"), sem("ac"), sem("y_ps"), sem("acc")
        yb_ps, acc0, stored = sem("yb_ps"), sem("acc0"), sem("stored")
        block = ctx.enter_context(nc.Block())

        NE = 2 * B
        SLOTS = NE + 4

        def has(i, n=NE):
            return 0 <= i < n

        def nbanks(e):
            return 16 if e < B else 12

        def bank_of(e, k):
            if e < B:
                u, q, half = k // 4, k // 2 % 2, k % 2
                return range(4 * u + 2 * half, 4 * u + 2 * half + 2), q, T
            u, w = k // 3, k % 3
            if w == 0:
                return range(4 * u, 4 * u + 4), 0, P
            return range(4 * u + 2 * (w - 1), 4 * u + 2 * w), 1, T

        def banks_before(e):
            return sum(nbanks(i) for i in range(e))

        def ring_uses(e, per=1):
            return (e // RING + 1) * per

        @block.sync
        def _(sp):
            sp.dma_start(X[:, 0:TT, :], x[:, 0:TT, :]).then_inc(ld["x0"], 16)
            sp.dma_start(CT[:, :], ctxT).then_inc(ld["ctx"], 16)
            sp.dma_start(COL[:, :], cols).then_inc(ld["cols"], 16)
            sp.dma_start(WK[:, :], wk).then_inc(ld["wqk"], 16)
            sp.dma_start(WV[:, :], wv).then_inc(ld["wv"], 16)
            sp.dma_start(X[:, TT:NT, :], x[:, TT:NT, :]).then_inc(ld["x1"], 16)
            for i in range(RING):
                sp.dma_start(KA[i][ROWS:KROWS, :, :].rearrange("p h t -> p (h t)").bitcast(fp32),
                             ones_row.broadcast_to([KROWS - ROWS, H * T // 2])).then_inc(ld["pad"], 16)
                sp.dma_start(QA[i][ROWS:KROWS, :, :].rearrange("p h t -> p (h t)").bitcast(fp32),
                             zero_row.broadcast_to([KROWS - ROWS, H * T // 2])).then_inc(ld["pad"], 16)

            def stack(e):
                nk = H if e < B else G
                sp.wait_ge(part3, e + 1)
                sp.dma_start(parts_dram[e].rearrange("i p q t -> p i q t"), PT[:, :, :, :]).then_inc(parts_out, 16)
                sp.wait_ge(parts_out, 16 * (e + 1))
                if e >= RING:
                    sp.wait_ge(scores, BEATS * (e - RING + 1))
                for i in range(NPART):
                    for j in range(NPART):
                        r = HD * (NPART * i + j)
                        sp.dma_start(QA[e % RING][r:r + HD, :, :],
                                     parts_dram[e, i, :, 0, :].rearrange("(h d) t -> d h t", d=HD))\
                          .then_inc(stacked[e % RING], 16)
                        sp.dma_start(KA[e % RING][r:r + HD, 0:nk, :],
                                     parts_dram[e, j, 0:nk * HD, 1, :].rearrange("(h d) t -> d h t", d=HD))\
                          .then_inc(stacked[e % RING], 16)

            def max_rows(e):
                sp.wait_ge(mts, e + 1)
                for part in range(2):
                    for q in range(TT):
                        r = (part * TT + q) * H
                        sp.dma_start(QA[e % RING][ROWS + part:ROWS + part + 1, :, q * P:(q + 1) * P],
                                     MTS[r:r + H, :]).then_inc(m_rows[e % RING], 16)

            for k in range(SLOTS):
                if has(k, B):
                    stack(k)
                if B <= k < NE:
                    stack(k)
                if has(k - 1):
                    max_rows(k - 1)
            for hf in range(2):
                sp.wait_ge(acc, (hf + 1) * E)
                for t in range(4):
                    n = 4 * hf + t
                    sp.dma_start(out[n], RR[:, n, :]).then_inc(stored, 16)
            sp.wait_ge(stored, 16 * NT)

        @block.gpsimd
        def _(pool):
            n = [0]

            def link(ins):
                n[0] += 1
                ins.then_inc(pool_step, 1)
                pool.wait_ge(pool_step, n[0])

            def rsqrt(out_, in_, w, mult, eps):
                link(pool.tensor_scalar(out_, in_, mult, eps, ALU.mult, ALU.add))
                return pool.tensor_tensor(out_, out_, NEGHALF[:, 0:w], ALU.pow)

            link(pool.memset(NEGHALF[:, :], -0.5))
            pool.wait_ge(ld["cols"], 16)
            pool.tensor_scalar(QBS[:, :], COL[:, C_QB:C_QB + 1], SCALE, None, ALU.mult).then_inc(cst, 1)
            pool.tensor_scalar(QNS[:, :], COL[:, C_QN:C_QN + 1], SCALE, None, ALU.mult).then_inc(cst, 1)
            pool.tensor_scalar(BGH[:, :], COL[:, C_BG:C_BG + 1], 0.5, None, ALU.mult).then_inc(cst, 1)

            def ln1_rstd(b):
                pool.wait_ge(mv1, b + 1)
                if b:
                    pool.wait_ge(xn, b)
                rsqrt_last = rsqrt(SM1[:, 0, :], MV1[:, :, 1], TT, 1.0, 1e-5)
                rsqrt_last.then_inc(rstd1, 1)

            def split_rest(e):
                pool.wait_ge(part1, e + 1)
                pool.tensor_tensor(R1[:, :, :], QKF[:, :, :], PT[:, 0, :, :], ALU.subtract).then_inc(rest1, 1)
                pool.wait_ge(rest1, e + 1)
                pool.wait_ge(part2, e + 1)
                pool.tensor_tensor(PT[:, 2, :, :], R1[:, :, :], PT[:, 1, :, :], ALU.subtract).then_inc(part3, 1)

            ln1_rstd(0)
            pool.wait_ge(ld["id"], 16)
            pool.tensor_copy(IDB[:, :], ID[:, :]).then_inc(cst, 1)
            nv = 0
            for i in range(RING):
                for V_, nh in ((VA[i], H), (VB[i], G)):
                    link(pool.memset(V_[:, :, :, :], 0.0))
                    v = V_[:, :, :, :].rearrange("p k (r s j) c -> p (k r) s j c", s=2, j=nh // 4)
                    for s in range(2):
                        pool.memset(v[:, :, s, :, 16 + s:17 + s], 1.0).then_inc(va_zero, 1)
            split_rest(0)
            pool.wait_ge(ld["tri"], 16)
            for j in range(4):
                pool.tensor_copy(TRIB[:, j, :], TRI[:, :]).then_inc(cst, 1)
            pool.wait_ge(ld["x0"], 16)
            pool.wait_ge(ld["x1"], 16)
            pool.wait_ge(ld["rows"], 16)
            pool.tensor_tensor(XB[:, :, :], X[:, :, :],
                               ROW[:, None, R_PB:R_PB + C].broadcast_to([P, NT, C]), ALU.add).then_inc(xb_ready, 1)
            pool.wait_ge(ld["wo"], 16)
            pool.tensor_scalar(WO[:, :], WO[:, :], 0.5, None, ALU.mult).then_inc(ocst, 1)

            def ln2_rstd(b):
                pool.wait_ge(mv2, b + 1)
                if b:
                    pool.wait_ge(hz, b)
                link(rsqrt(SM2[:, 0, :], MV2[:, :, 1], TT, 1.0, 1e-5))
                link(pool.tensor_tensor(SM2[:, 1, :], SM2[:, 0, :], SM2[:, 0, :], ALU.mult))
                link(pool.tensor_tensor(SM2[:, 1, :], SM2[:, 1, :], MV2[:, :, 1], ALU.mult))
                link(rsqrt(SM2[:, 2, :], SM2[:, 1, :], TT, 1.0, 1e-6))
                pool.tensor_tensor(SM2[:, 3, :], SM2[:, 0, :], SM2[:, 2, :], ALU.mult).then_inc(rstd2, 1)
                for t in range(TT):
                    link(pool.tensor_scalar(Z[:, TT * b + t, :], X1[:, TT * b + t, :],
                                            MV2[:, t, 0:1], SM2[:, 0, t:t + 1], ALU.subtract, ALU.mult))
                pool.tensor_tensor(ZB[:, TT * b:TT * b + TT, :], Z[:, TT * b:TT * b + TT, :],
                                   ROW[:, None, R_BO:R_BO + C].broadcast_to([P, TT, C]), ALU.add)\
                    .then_inc(z_ready, 1)

            def head_squares(b):
                pool.wait_ge(qkvs, b + 1)
                if b:
                    pool.wait_ge(ssq, b)
                pool.tensor_tensor(SQ[:, :, :], QKVS[:, :, 0:NH2 * HD], QKVS[:, :, 0:NH2 * HD], ALU.mult)\
                    .then_inc(sq, 1)
                if b >= RING:
                    pool.wait_ge(pv, BEATS * (B + b - RING + 1))
                for s in range(2):
                    pool.tensor_copy(
                        VB[b % RING][:, :, :, 8 * s:8 * s + 8].rearrange("p k (r s) c -> p k r s c", s=2)[:, :, :, s, :],
                        QKVS[:, :, NH2 * HD:QKV].rearrange("p k (r s c) -> p k r s c", s=2, c=HD)[:, :, :, s, :])\
                        .then_inc(vb, 1)
                pool.wait_ge(ssq, b + 1)
                if b:
                    pool.wait_ge(qn, b)
                rsqrt(RQ[:, :], SSQ[:, :], TT * NH2, 1.0 / HD, 1e-6).then_inc(rq, 1)

            def rms3(b):
                pool.wait_ge(ss3, b + 1)
                if b:
                    pool.wait_ge(h2, b)
                rsqrt(SS3[:, 1, :], SS3[:, 0, :], TT, 1.0 / C, 1e-6).then_inc(rstd3, 1)

            def causal(e, i):
                u, kt = i // 2, i % 2
                w = T if kt == 0 else P
                g = BEATS * e + i
                pool.wait_ge(probs, g + 1)
                v = EX[g % PRING][:, 0:4 * w].rearrange("p (j t) -> p j t", j=4)[:, :, 0:P]
                pool.affine_select(out=v, in_=v, pattern=[[0, 4], [1, P]], compare_op=ALU.is_ge, fill=0.0,
                                   base=0, channel_multiplier=-1).then_inc(masked, 1)

            for k in range(SLOTS):
                for i in range(BEATS):
                    if i == 0 and has(k, B) and k:
                        ln1_rstd(k)
                    if i == 1 and has(k - 4, B):
                        head_squares(k - 4)
                    if B <= k - 2 < NE:
                        causal(k - 2, i)
                    if i == 1 and has(k, B) and k:
                        split_rest(k)
                    if i == 3 and has(k - 4, B):
                        split_rest(k)
                    if i == 5 and has(k - 3, B):
                        ln2_rstd(k - 3)
                    if i == 1 and has(k - 8, B):
                        b = k - 8
                        pool.wait_ge(xp, b + 1)
                        pool.tensor_tensor(RR[:, TT * b:TT * b + TT, :], X1[:, TT * b:TT * b + TT, :],
                                           XP[:, :, :], ALU.add).then_inc(rr, 1)
                        rms3(b)

        @block.scalar
        def _(act):
            n = [0]

            def link(ins):
                n[0] += 1
                ins.then_inc(act_step, 1)
                act.wait_ge(act_step, n[0])

            act.dma_start(ID[:, :], ident).then_inc(ld["id"], 16)
            act.dma_start(WQ[:, :], wq).then_inc(ld["wqk"], 16)
            act.dma_start(ROW[:, :], rows.broadcast_to([P, NROW])).then_inc(ld["rows"], 16)
            act.dma_start(TRI[:, :], tri).then_inc(ld["tri"], 16)
            act.dma_start(WP[:, :], wp).then_inc(ld["wp"], 16)
            act.dma_start(WQKV[:, :], wqkv).then_inc(ld["wqkv"], 16)
            act.dma_start(ROPE[:, :, :, :], rope).then_inc(ld["rope"], 16)
            act.dma_start(WG[:, :], wg).then_inc(ld["wg"], 16)
            act.dma_start(WO[:, :], wo).then_inc(ld["wo"], 16)
            act.dma_start(WR[:, :], wr).then_inc(ld["wr"], 16)
            act.dma_start(REV[:, :], revs.broadcast_to([P, E])).then_inc(ld["rev"], 16)
            act.dma_start(B2[:, :], b2).then_inc(ld["b2"], 16)
            act.dma_start(W1[:, :, :], w1).then_inc(ld["w1"], 16)
            act.dma_start(W2[:, :, :, :], w2).then_inc(ld["w2"], 16)

            def split(e):
                if e:
                    act.wait_ge(parts_out, 16 * e)
                act.wait_ge(qkf, e + 1)
                act.activation(PT[:, 0, :, :], QKF[:, :, :], ACT.Copy).then_inc(part1, 1)
                act.wait_ge(rest1, e + 1)
                act.activation(PT[:, 1, :, :], R1[:, :, :], ACT.Copy).then_inc(part2, 1)

            def qkf_free(e):
                if e:
                    act.wait_ge(rest1, e)
                    act.wait_ge(part1, e)

            for k in range(SLOTS):
                for i in range(BEATS):
                    if has(k - 2):
                        e = k - 2
                        g = BEATS * e + i
                        w = 4 * T if e < B or i % 2 == 0 else 4 * P
                        act.wait_ge(scores, g + 1)
                        if g >= PRING:
                            act.wait_ge(pv, g - PRING + 1)
                        act.activation(EX[g % PRING][:, 0:w], S[g % 2][:, 0:w], ACT.Exp).then_inc(probs, 1)
                    if i == 1 and has(k - 3):
                        act.wait_ge(pv, BEATS * (k - 2))
                        if k > 3:
                            act.wait_ge(o_t, k - 3)
                        act.activation(OS[:, :], O[:, :], ACT.Copy).then_inc(o_sb, 1)
                    if i == 0 and has(k, B):
                        act.wait_ge(xn_t, k + 1)
                        if k:
                            act.wait_ge(qk_ps, k)
                        act.activation(XNT[:, :], MS[:, 0:T], ACT.Copy).then_inc(xnt, 1)
                    if i == 1 and has(k, B):
                        act.wait_ge(qk_ps, k + 1)
                        act.wait_ge(cst, 1)
                        act.wait_ge(ld["cols"], 16)
                        qkf_free(k)
                        act.activation(QKF[:, 0, :], MS[:, 0:T], ACT.Identity, bias=QBS[:, :], scale=SCALE)
                        act.activation(QKF[:, 1, :], MS[:, T:2 * T], ACT.Identity,
                                       bias=COL[:, C_KB:C_KB + 1]).then_inc(qkf, 1)
                        split(k)
                    if i == 0 and has(k - 4, B):
                        act.wait_ge(hz_t, k - 3)
                        if k > 4:
                            act.wait_ge(qkv_ps, k - 4)
                        act.activation(HT[:, :], MS[:, 0:T], ACT.Copy, scale=COL[:, C_LN1:C_LN1 + 1]).then_inc(ht, 1)
                    if i == 3 and has(k - 4, B):
                        act.wait_ge(qn_t, k - 3)
                        qkf_free(k)
                        act.activation(QKF[:, 0, :], MS[:, 0:T], ACT.Copy, scale=QNS[:, :])
                        act.activation(QKF[0:G * HD, 1, :], MS[0:G * HD, T:2 * T], ACT.Copy,
                                       scale=COL[0:G * HD, C_KN:C_KN + 1]).then_inc(qkf, 1)
                        split(k)
                    if i == 4 and has(k - 3):
                        act.wait_ge(on_t, k - 2)
                        if 3 < k <= 7:
                            act.wait_ge(pj, k - 3)
                        elif k > 7:
                            act.wait_ge(gated, k - 7)
                            act.wait_ge(gate_ps, k - 7)
                        act.activation(ONT[:, :], MS[:, 0:T], ACT.Copy).then_inc(ont, 1)
                    if i == 5 and has(k - 7, B):
                        b = k - 7
                        act.wait_ge(gate_ps, b + 1)
                        if b:
                            act.wait_ge(gated, b)
                        act.activation(TH[:, :], MS[:, 0:T], ACT.Tanh, bias=BGH[:, :], scale=0.5).then_inc(th, 1)
                    if i == 0 and has(k - 8, B):
                        b = k - 8
                        act.wait_ge(xp, b + 1)
                        if b:
                            act.wait_ge(rstd3, b)
                        for t in range(TT):
                            last = act.activation(SQX[:, t, :], XP[:, t, :], ACT.Square,
                                                  accum_out=SS3[:, 0, t:t + 1])
                        last.then_inc(ss3, 1)
                    if i == 3 and has(k - 8, B):
                        b = k - 8
                        act.wait_ge(h2_t, b + 1)
                        act.activation(H2T[:, T * b:T * b + T], MS[:, 0:T], ACT.Copy,
                                       scale=COL[:, C_LN2:C_LN2 + 1]).then_inc(h2t, 1)
                    if i == 6 and has(k - 1):
                        act.wait_ge(m_t, k)
                        if k > 1:
                            act.wait_ge(m_rows[(k - 2) % RING], 64 * ring_uses(k - 2))
                        act.activation(MTS[:, :], MSB[0:2 * TT * H, 0:P], ACT.Copy).then_inc(mts, 1)

            for hf in range(2):
                act.wait_ge(oh_t, hf + 1)
                act.activation(OHT[:, 4 * P * hf:4 * P * hf + 4 * P], OHP[0:E, :], ACT.Copy).then_inc(oht, 1)
                for e in range(E):
                    for c in range(2):
                        m = 2 * (E * hf + e) + c
                        act.wait_ge(u_ps, m + 1)
                        if m >= 2:
                            act.wait_ge(ac, m - 1)
                        act.activation(SG[m % 2][:, :], U[m % 3][:, 512:1024], ACT.Sigmoid,
                                       bias=COL[:, C_B1 + 4 * e + 2 + c:C_B1 + 4 * e + 3 + c]).then_inc(sg, 1)

        @block.vector
        def _(dve):
            n = [0]

            def link(ins):
                n[0] += 1
                ins.then_inc(dve_step, 1)
                dve.wait_ge(dve_step, n[0])

            def statistics(src, st, mv):
                for t in range(TT):
                    last = dve.bn_stats(st[:, t, :], src[:, t, :])
                link(last)
                for t in range(TT):
                    last = dve.bn_aggr(mv[:, t, :], st[:, t, :])
                return last

            def maxima(e, k):
                heads, q, w = bank_of(e, k)
                g = banks_before(e) + k
                if k == 0 and e:
                    dve.wait_ge(mhl, e)
                dve.wait_ge(mx_scores, g + 1)
                dve.tensor_reduce(out=NEGM[:, q, heads[0]:heads[-1] + 1],
                                  in_=MX[g % 2][:, 0:len(heads) * w].rearrange("p (h t) -> p h t", t=w),
                                  axis=AX.X, op=ALU.max, negate=True).then_inc(mx_taken, 1)

            def values(b):
                dve.wait_ge(v_ps, b + 1)
                dve.wait_ge(va_zero, 4 * (b % RING) + 2)
                dve.wait_ge(ld["rows"], 16)
                if b >= RING:
                    dve.wait_ge(pv, BEATS * (b - RING + 1))
                for s in range(2):
                    for t in range(TT):
                        last = dve.tensor_tensor(
                            VA[b % RING][:, t, :, 8 * s:8 * s + 8]
                            .rearrange("p (r s j) c -> p r s j c", s=2, j=4)[:, :, s, :, :],
                            MS[:, C * t:C * t + C].rearrange("p (r s j c) -> p r s j c", s=2, j=4, c=HD)[:, :, s, :, :],
                            ROW[:, R_VB:R_VB + C].rearrange("p (r s j c) -> p r s j c", s=2, j=4, c=HD)[:, :, s, :, :],
                            ALU.add)
                last.then_inc(va, 1)

            for k in range(SLOTS):
                for i in range(BEATS):
                    if i == 0 and has(k, B):
                        b = k
                        dve.wait_ge(ld["x1" if b else "x0"], 16)
                        if b:
                            dve.wait_ge(rstd1, b)
                        statistics(X[:, TT * b:TT * b + TT, :], ST, MV1).then_inc(mv1, 1)
                    if has(k - 1):
                        for kk in range(3 * i, min(3 * i + 3, nbanks(k - 1))):
                            maxima(k - 1, kk)
                    if i == 0 and has(k, B):
                        b = k
                        dve.wait_ge(rstd1, b + 1)
                        if b:
                            dve.wait_ge(xn_t, b)
                        for t in range(TT):
                            last = dve.tensor_scalar(XN[:, t, :], X[:, TT * b + t, :], MV1[:, t, 0:1],
                                                     SM1[:, 0, t:t + 1], ALU.subtract, ALU.mult)
                        last.then_inc(xn, 1)
                    if i == 3 and has(k, B):
                        values(k)
                    if i == 0 and has(k - 8, B):
                        b = k - 8
                        dve.wait_ge(wo_ps, b + 1)
                        dve.wait_ge(z_ready, b + 1)
                        if b:
                            dve.wait_ge(h2, b)
                            dve.wait_ge(rr, b)
                            dve.wait_ge(ss3, b)
                        dve.tensor_tensor(XP[:, :, :], MS[:, 0:T].rearrange("p (t c) -> p t c", t=TT),
                                          ZB[:, TT * b:TT * b + TT, :], ALU.add).then_inc(xp, 1)
                    if i == 2 and has(k - 8, B):
                        b = k - 8
                        dve.wait_ge(rstd3, b + 1)
                        if b:
                            dve.wait_ge(h2_t, b)
                        for t in range(TT):
                            last = dve.tensor_scalar(H2[:, t, :], XP[:, t, :], SS3[:, 1, t:t + 1], None, ALU.mult)
                        last.then_inc(h2, 1)
                    if i == 2 and has(k - 3):
                        n_ = k - 3
                        dve.wait_ge(o_t, n_ + 1)
                        if n_:
                            dve.wait_ge(on_t, n_)
                        v = MS[:, :].rearrange("p (a c) -> p a c", c=32)
                        link(dve.reciprocal(RC[:, :, :], v[:, :, 16:18]))
                        dve.tensor_tensor(ON[:, :, :].rearrange("p a (s c) -> p a s c", s=2),
                                          v[:, :, 0:16].rearrange("p a (s c) -> p a s c", s=2),
                                          RC[:, :, :, None].broadcast_to([P, 16, 2, HD]), ALU.mult).then_inc(on, 1)
                    if i == 5 and has(k - 3, B):
                        b = k - 3
                        dve.wait_ge(pj, b + 1)
                        dve.wait_ge(xb_ready, 1)
                        if b:
                            dve.wait_ge(z_ready, b)
                        link(dve.tensor_tensor(X1[:, TT * b:TT * b + TT, :],
                                               MS[:, 0:T].rearrange("p (t c) -> p t c", t=TT),
                                               XB[:, TT * b:TT * b + TT, :], ALU.add))
                        statistics(X1[:, TT * b:TT * b + TT, :], ST2, MV2).then_inc(mv2, 1)
                        dve.wait_ge(rstd2, b + 1)
                        if b:
                            dve.wait_ge(hz_t, b)
                        for t in range(TT):
                            last = dve.tensor_scalar(HZ[:, t, :], X1[:, TT * b + t, :], MV2[:, t, 0:1],
                                                     SM2[:, 3, t:t + 1], ALU.subtract, ALU.mult)
                        last.then_inc(hz, 1)
                    if i == 1 and has(k - 4, B):
                        b = k - 4
                        dve.wait_ge(qkv_ps, b + 1)
                        if b:
                            dve.wait_ge(sq, b)
                            dve.wait_ge(vb, 2 * b)
                        dve.tensor_tensor(QKVS[:, :, :], MS[:, 0:TT * QKV].rearrange("p (t c) -> p t c", t=TT),
                                          ROW[:, None, R_BQKV:R_BQKV + QKV].broadcast_to([P, TT, QKV]), ALU.add)                            .then_inc(qkvs, 1)
                        dve.wait_ge(qkvs, b + 1)
                        dve.wait_ge(ld["rope"], 16)
                        qk = QKVS[:, :, 0:NH2 * HD].rearrange("p t (h c) -> p t h c", c=HD)
                        hh = HD // 2
                        dve.tensor_tensor(ROT[:, :, :, :], qk,
                                          ROPE[:, :, 0:1, :].broadcast_to([P, TT, NH2, HD]), ALU.mult)
                        dve.tensor_tensor(ROTS[:, :, :, 0:hh], qk[:, :, :, hh:HD],
                                          ROPE[:, :, 1:2, 0:hh].broadcast_to([P, TT, NH2, hh]), ALU.mult)
                        link(dve.tensor_tensor(ROTS[:, :, :, hh:HD], qk[:, :, :, 0:hh],
                                               ROPE[:, :, 1:2, hh:HD].broadcast_to([P, TT, NH2, hh]), ALU.mult))
                        link(dve.tensor_tensor(ROT[:, :, :, :], ROT[:, :, :, :], ROTS[:, :, :, :], ALU.add))
                        dve.wait_ge(sq, b + 1)
                        if b:
                            dve.wait_ge(rq, b)
                        dve.tensor_reduce(out=SSQ[:, :], in_=SQ[:, :, :].rearrange("p t (h c) -> p (t h) c", c=HD),
                                          axis=AX.X, op=ALU.add).then_inc(ssq, 1)
                        dve.wait_ge(rq, b + 1)
                        if b:
                            dve.wait_ge(qn_t, b)
                        dve.tensor_tensor(QN[:, :, :].rearrange("p t (h c) -> p (t h) c", c=HD),
                                          ROT[:, :, :, :].rearrange("p t h c -> p (t h) c"),
                                          RQ[:, :, None].broadcast_to([P, TT * NH2, HD]), ALU.mult).then_inc(qn, 1)
                    if i == 5 and has(k - 7, B):
                        b = k - 7
                        dve.wait_ge(th, b + 1)
                        if b:
                            dve.wait_ge(wo_ps, b)
                        dve.scalar_tensor_tensor(GT[:, :], TH[:, :], 1.0, ONT[:, :], ALU.add, ALU.mult)                            .then_inc(gated, 1)
                    if i == 6 and has(k - 1):
                        dve.wait_ge(mx_taken, banks_before(k))
                        if k > 1:
                            dve.wait_ge(m_t, k - 1)
                        link(dve.tensor_copy(MHL[:, 0, :, :], NEGM[:, :, :]))
                        dve.tensor_tensor(MHL[:, 1, :, :], NEGM[:, :, :], MHL[:, 0, :, :], ALU.subtract)                            .then_inc(mhl, 1)
                    if i == 7 and has(k - 8, B):
                        b = k - 8
                        dve.wait_ge(lg_ps, b + 1)
                        link(dve.tensor_tensor(LG[:, :, :], MS[:, 0:TT * E].rearrange("p (t e) -> p t e", t=TT),
                                               ROW[:, None, R_BR:R_BR + E].broadcast_to([P, TT, E]), ALU.add))
                        link(dve.tensor_reduce(out=MXL[:, 0, :], in_=LG[:, :, :], axis=AX.X, op=ALU.max))
                        link(dve.tensor_tensor(EQ[:, :, :], LG[:, :, :],
                                               MXL[:, 0, :, None].broadcast_to([P, TT, E]), ALU.is_equal))
                        dve.wait_ge(ld["rev"], 16)
                        link(dve.tensor_tensor(EQ[:, :, :], EQ[:, :, :],
                                               REV[:, None, :].broadcast_to([P, TT, E]), ALU.mult))
                        link(dve.tensor_reduce(out=MXL[:, 1, :], in_=EQ[:, :, :], axis=AX.X, op=ALU.max))
                        dve.tensor_tensor(OH[:, TT * b:TT * b + TT, :], REV[:, None, :].broadcast_to([P, TT, E]),
                                          MXL[:, 1, :, None].broadcast_to([P, TT, E]), ALU.is_equal).then_inc(oh, 1)

            nacc = 0
            for hf in range(2):
                def combine(e):
                    dve.wait_ge(y_ps, E * hf + e + 1)
                    for t in range(4):
                        r = RR[:, 4 * hf + t, :]
                        last = dve.scalar_tensor_tensor(r, Y[e % 2][:, C * t:C * t + C],
                                                        OH[:, 4 * hf + t, e:e + 1], r, ALU.mult, ALU.add)
                    last.then_inc(acc, 1)

                dve.wait_ge(yb_ps, hf + 1)
                dve.wait_ge(rr, B)
                dve.tensor_tensor(RR[:, 4 * hf:4 * hf + 4, :], RR[:, 4 * hf:4 * hf + 4, :],
                                  Y[1][:, :].rearrange("p (t c) -> p t c", t=4), ALU.add).then_inc(acc0, 1)
                for e in range(E):
                    for c in range(2):
                        m = 2 * (E * hf + e) + c
                        dve.wait_ge(sg, m + 1)
                        if e >= 2 or hf:
                            dve.wait_ge(y_ps, E * hf + e - 1)
                        dve.scalar_tensor_tensor(AC[e % 2][:, c, :], U[m % 3][:, 0:512],
                                                 COL[:, C_B1 + 4 * e + c:C_B1 + 4 * e + 1 + c], SG[m % 2][:, :],
                                                 ALU.add, ALU.mult).then_inc(ac, 1)
                    if e == 0:
                        dve.wait_ge(acc0, hf + 1)
                    if e:
                        if e > 1:
                            dve.wait_ge(acc, E * hf + e - 1)
                        combine(e - 1)
                dve.wait_ge(acc, E * hf + E - 1)
                combine(E - 1)

        @block.tensor
        def _(pe):
            last_reader = [None]

            def take_misc(reader, count):
                if last_reader[0]:
                    pe.wait_ge(*last_reader[0])
                last_reader[0] = (reader, count)

            def mm(out_, lhsT, rhs, start=True, stop=True, **kw):
                return nc.tensor.matmul(out_, lhsT, rhs, start=start, stop=stop, **kw)

            def transposes(done, src, w=C):
                for t in range(TT):
                    last = nc.tensor.transpose(MS[:, P * t:P * t + P], src[:, t, :], ID[:, :])
                last.then_inc(done, 1)

            def score_beat(e, i):
                u, kt = i // 2, i % 2
                g = BEATS * e + i
                if i == 0:
                    pe.wait_ge(m_rows[e % RING], 64 * ring_uses(e))
                    if e == B:
                        pe.wait_ge(ld["tri"], 16)
                if g >= 2:
                    pe.wait_ge(probs, g - 1)
                qa, ka = QA[e % RING], KA[e % RING]
                for j in range(4):
                    if e < B:
                        last = mm(S[g % 2][:, T * j:T * j + T], ka[:, 4 * u + j, P * kt:P * kt + P], qa[:, 4 * u + j, :])
                    elif kt == 0:
                        if j % 2 == 0:
                            last = mm(S[g % 2][:, T * j:T * j + 2 * T], ka[:, u, 0:P],
                                      qa[:, 4 * u + j:4 * u + j + 2, :])
                    elif j == 0:
                        last = mm(S[g % 2][:, 0:4 * P], ka[:, u, P:T], qa[:, 4 * u:4 * u + 4, P:T])
                last.then_inc(scores, 1)

            def max_bank(e, k):
                heads, q, w = bank_of(e, k)
                g = banks_before(e) + k
                if k == 0:
                    pe.wait_ge(stacked[e % RING], stacked_total(e))
                    if e == 0:
                        pe.wait_ge(ld["pad"], 32 * RING)
                if g >= 2:
                    pe.wait_ge(mx_taken, g - 1)
                qa, ka, m = QA[e % RING], KA[e % RING], MX[g % 2]
                causal = e >= B
                for n_, h in enumerate(heads):
                    last = mm(m[:, w * n_:w * n_ + w], qa[:, h, P * q:P * q + P], ka[:, h if e < B else h // 4, 0:w],
                              stop=not causal, skip_group_check=causal, start=not causal or n_ == 0)
                if causal:
                    if e == B and k == 0:
                        pe.wait_ge(cst, 8)
                    nh = len(heads)
                    last = mm(m[:, 0:nh * w].rearrange("p (h t) -> p h t", t=w)[:, :, w - P:w], IDB[:, :],
                              TRIB[:, 0:nh, :], start=False, skip_group_check=True)
                last.then_inc(mx_scores, 1)

            def pv_beat(e, i):
                u, kt = i // 2, i % 2
                g = BEATS * e + i
                r, s = u // 2, u % 2
                if i == 0:
                    if e < B:
                        pe.wait_ge(va, e + 1)
                    else:
                        pe.wait_ge(vb, 2 * (e - B + 1))
                    if e:
                        pe.wait_ge(o_sb, e)
                if e < B:
                    pe.wait_ge(probs, g + 1)
                else:
                    pe.wait_ge(masked, g - BEATS * B + 1)
                w, q0 = (T, 0) if e < B or kt == 0 else (P, P)
                for j in range(4):
                    V_ = VA[e % RING][:, kt, 4 * u + j, :] if e < B else VB[(e - B) % RING][:, kt, u, :]
                    last = mm(O[32 * j:32 * j + 32, T * r + q0:T * r + q0 + w], V_,
                              EX[g % PRING][:, w * j:w * j + w], start=s == 0 and kt == 0, stop=s == 1 and kt == 1,
                              tile_position=(0, 32 * j), skip_group_check=True)
                last.then_inc(pv, 1)

            def stacked_total(e):
                return sum(16 * 2 * NPART * NPART for x_ in range(e + 1) if x_ % RING == e % RING)

            for k in range(SLOTS):
                for i in range(BEATS):
                    if has(k - 2):
                        score_beat(k - 2, i)
                    if has(k - 1):
                        for kk in range(3 * i, min(3 * i + 3, nbanks(k - 1))):
                            max_bank(k - 1, kk)
                    g = BEATS * (k - 2) + i - 2
                    if 0 <= g < BEATS * NE:
                        pv_beat(g // BEATS, g % BEATS)
                    if i == 0 and has(k, B):
                        if k == 0:
                            pe.wait_ge(ld["id"], 16)
                        take_misc(xnt, k + 1)
                        pe.wait_ge(xn, k + 1)
                        transposes(xn_t, XN)
                    if i == 1 and has(k, B):
                        if k == 0:
                            pe.wait_ge(ld["wqk"], 32)
                            pe.wait_ge(ld["ctx"], 16)
                        take_misc(qkf, k + 1)
                        mm(MS[:, 0:T], WQ[:, :], XNT[:, :])
                        mm(MS[:, T:2 * T], WK[:, :], CT[:, T * k:T * k + T]).then_inc(qk_ps, 1)
                    if i == 3 and has(k, B):
                        if k == 0:
                            pe.wait_ge(ld["wv"], 16)
                        take_misc(va, k + 1)
                        for t in range(TT):
                            last = mm(MS[:, C * t:C * t + C], CT[:, T * k + P * t:T * k + P * t + P], WV[:, :])
                        last.then_inc(v_ps, 1)
                    if i == 0 and has(k - 4, B):
                        take_misc(ht, k - 3)
                        pe.wait_ge(hz, k - 3)
                        transposes(hz_t, HZ)
                    if i == 1 and has(k - 4, B):
                        if k == 4:
                            pe.wait_ge(ld["wqkv"], 16)
                        take_misc(qkvs, k - 3)
                        for t in range(TT):
                            last = mm(MS[:, QKV * t:QKV * t + QKV], HT[:, P * t:P * t + P], WQKV[:, :])
                        last.then_inc(qkv_ps, 1)
                    if i == 0 and has(k - 8, B):
                        b = k - 8
                        take_misc(xp, b + 1)
                        pe.wait_ge(gated, b + 1)
                        if b == 0:
                            pe.wait_ge(ocst, 1)
                        for t in range(TT):
                            last = mm(MS[:, C * t:C * t + C], GT[:, P * t:P * t + P], WO[:, :])
                        last.then_inc(wo_ps, 1)
                    if i == 2 and has(k - 3):
                        n_ = k - 3
                        take_misc(on, n_ + 1)
                        pe.wait_ge(o_sb, n_ + 1)
                        for t in range(TT):
                            for r in range(2):
                                last = nc.tensor.transpose(MS[:, P * (2 * t + r):P * (2 * t + r) + P],
                                                           OS[:, T * r + P * t:T * r + P * t + P], ID[:, :])
                        last.then_inc(o_t, 1)
                    if i == 3 and has(k - 4, B):
                        take_misc(qkf, k + 1)
                        pe.wait_ge(qn, k - 3)
                        for t in range(TT):
                            nc.tensor.transpose(MS[:, P * t:P * t + P], QN[:, t, 0:C], ID[:, :])
                            last = nc.tensor.transpose(MS[0:G * HD, T + P * t:T + P * t + P],
                                                       QN[:, t, C:C + G * HD], ID[:, :])
                        last.then_inc(qn_t, 1)
                    if i == 3 and has(k - 8, B):
                        take_misc(h2t, k - 7)
                        pe.wait_ge(h2, k - 7)
                        transposes(h2_t, H2)
                    if i == 4 and has(k - 3):
                        n_ = k - 3
                        take_misc(ont, n_ + 1)
                        pe.wait_ge(on, n_ + 1)
                        for t in range(TT):
                            last = nc.tensor.transpose(MS[:, P * t:P * t + P],
                                                       ON[:, 8 * t:8 * t + 8, :].rearrange("p a c -> p (a c)"), ID[:, :])
                        last.then_inc(on_t, 1)
                    if i == 5 and has(k - 3, B):
                        if k == 3:
                            pe.wait_ge(ld["wp"], 16)
                        take_misc(mv2, k - 2)
                        pe.wait_ge(ont, k - 2)
                        for t in range(TT):
                            last = mm(MS[:, C * t:C * t + C], ONT[:, P * t:P * t + P], WP[:, :])
                        last.then_inc(pj, 1)
                    if i == 5 and has(k - 7, B):
                        if k == 7:
                            pe.wait_ge(ld["wg"], 16)
                        take_misc(th, k - 6)
                        pe.wait_ge(ont, k - 2)
                        mm(MS[:, 0:T], WG[:, :], ONT[:, :]).then_inc(gate_ps, 1)
                    if i == 6 and has(k - 1):
                        take_misc(mts, k)
                        pe.wait_ge(mhl, k)
                        if k == 1:
                            pe.wait_ge(cst, 4)
                        nc.tensor.transpose(MSB[0:2 * TT * H, 0:P], MHL[:, :, :, :].rearrange("p a t h -> p (a t h)"),
                                            IDB[:, :]).then_inc(m_t, 1)
                    if i == 7 and has(k - 8, B):
                        b = k - 8
                        if b == 0:
                            pe.wait_ge(ld["wr"], 16)
                        take_misc(oh, b + 1)
                        pe.wait_ge(h2t, b + 1)
                        for t in range(TT):
                            last = mm(MS[:, E * t:E * t + E], H2T[:, T * b + P * t:T * b + P * t + P], WR[:, :])
                        last.then_inc(lg_ps, 1)

            pe.wait_ge(oh, B)
            pe.wait_ge(ld["w1"], 16)
            pe.wait_ge(ld["w2"], 16)
            pe.wait_ge(ld["b2"], 16)

            def outer(hf, e):
                pe.wait_ge(ac, 2 * (E * hf + e) + 2)
                yn = E * hf + e
                if e >= 2:
                    pe.wait_ge(acc, yn - 1)
                elif hf:
                    pe.wait_ge(acc, E * hf)
                    pe.wait_ge(acc0, hf + 1)
                elif e == 1:
                    pe.wait_ge(acc0, 1)
                for t in range(4):
                    for c in range(2):
                        last = mm(Y[e % 2][:, C * t:C * t + C], AC[e % 2][:, c, P * t:P * t + P], W2[:, e, c, :],
                                  start=c == 0, stop=c == 1)
                last.then_inc(y_ps, 1)

            for hf in range(2):
                if hf:
                    pe.wait_ge(acc, E * hf)
                for t in range(4):
                    last = nc.tensor.transpose(OHP[0:E, P * t:P * t + P], OH[:, 4 * hf + t, :], ID[:, :])
                last.then_inc(oh_t, 1)
                pe.wait_ge(oht, hf + 1)
                for t in range(4):
                    last = mm(Y[1][:, C * t:C * t + C], OHT[:, 4 * P * hf + P * t:4 * P * hf + P * t + P], B2[:, :])
                last.then_inc(yb_ps, 1)
                for e in range(E):
                    for c in range(2):
                        m = 2 * (E * hf + e) + c
                        if m >= 3:
                            pe.wait_ge(ac, m - 2)
                        for half in range(2):
                            f = HID * half + P * c
                            last = mm(U[m % 3][:, 512 * half:512 * half + 512], W1[:, e, f:f + P],
                                      H2T[:, 512 * hf:512 * hf + 512])
                        last.then_inc(u_ps, 1)
                    if e:
                        outer(hf, e - 1)
                outer(hf, E - 1)


_INS = ("x", "ctxT", "cols", "rows", "wq", "wk", "wv", "wp", "wqkv", "wg", "wo", "wr", "w1", "w2", "b2",
        "ident", "tri", "rope", "revs", "ones_row", "zero_row")


def rope_table():
    inv = (1.0 / 10000.0 ** (np.arange(0, HD, 2, dtype=np.float32) / HD)).astype(np.float32)
    f = np.arange(T, dtype=np.float32)[:, None] * inv[None, :]
    c, s = np.cos(f).astype(np.float32), np.sin(f).astype(np.float32)
    return np.stack([np.concatenate([c, c], 1), np.concatenate([-s, s], 1)], 1)


def layout(x, ctx_768, L0_xattn_q_w, L0_xattn_q_b, L0_xattn_kv_w, L0_xattn_kv_b, L0_xattn_proj_w,
           L0_xattn_proj_b, L0_ffn_ln1_w, L0_ffn_ln2_w, L0_ffn_Wq, L0_ffn_bq, L0_ffn_Wk, L0_ffn_bk,
           L0_ffn_Wv, L0_ffn_bv, L0_ffn_qn_w, L0_ffn_kn_w, L0_ffn_Wg, L0_ffn_bg, L0_ffn_Wo, L0_ffn_bo,
           L0_ffn_Wr, L0_ffn_br, L0_ffn_W1, L0_ffn_b1, L0_ffn_W2, L0_ffn_b2):
    f = np.float32
    def by_quadrant(w):
        return np.ascontiguousarray(np.asarray(w).reshape(2, 2, 4, HD, C).transpose(0, 2, 1, 3, 4).reshape(C, C))

    cols = np.zeros((P, NCOL), f)
    cols[:, C_QB] = L0_xattn_q_b
    cols[:, C_KB] = L0_xattn_kv_b[:C]
    cols[:, C_LN1] = L0_ffn_ln1_w
    cols[:, C_LN2] = L0_ffn_ln2_w
    cols[:, C_QN] = np.tile(L0_ffn_qn_w, H)
    cols[:, C_KN] = np.tile(L0_ffn_kn_w, H)
    cols[:, C_BG] = np.tile(L0_ffn_bg, H)
    cols[:, C_B1:] = np.asarray(L0_ffn_b1).reshape(E * 4, P).T
    rows = np.concatenate([L0_xattn_kv_b[C:], L0_xattn_proj_b, L0_ffn_bq, L0_ffn_bk, L0_ffn_bv, L0_ffn_bo,
                           L0_ffn_br])[None, :].astype(f)
    wg = np.zeros((C, C), f)
    for h in range(H):
        wg[HD * h:HD * h + HD, HD * h:HD * h + HD] = L0_ffn_Wg
    ii = np.arange(P)
    d = {
        "x": np.asarray(x).reshape(NT, P, C).transpose(1, 0, 2),
        "ctxT": np.asarray(ctx_768).reshape(B * T, CD).T,
        "cols": cols, "rows": rows,
        "wq": L0_xattn_q_w, "wk": L0_xattn_kv_w[:, :C], "wv": L0_xattn_kv_w[:, C:],
        "wp": by_quadrant(L0_xattn_proj_w),
        "wqkv": np.concatenate([L0_ffn_Wq, L0_ffn_Wk, L0_ffn_Wv], 1),
        "wg": wg, "wo": by_quadrant(L0_ffn_Wo), "wr": L0_ffn_Wr,
        "w1": np.asarray(L0_ffn_W1).transpose(1, 0, 2),
        "w2": np.asarray(L0_ffn_W2).reshape(E, 2, P, C).transpose(2, 0, 1, 3),
        "b2": L0_ffn_b2,
        "ident": np.eye(P, dtype=f),
        "tri": np.where(ii[None, :] > ii[:, None], -1e30, 0.0).astype(f),
        "rope": rope_table().reshape(TT, P, 2, HD).transpose(1, 0, 2, 3),
        "revs": np.arange(E, 0, -1, dtype=f)[None, :],
        "ones_row": np.full((1, H * T // 2), 0x3F803F80, np.uint32).view(f),
        "zero_row": np.zeros((1, H * T // 2), f),
    }
    return {k: np.ascontiguousarray(v) for k, v in d.items()}


def program(nc, shapes):
    aps = [nc.dram_tensor(f"in_{k}", s, d, kind="ExternalInput").ap() for k, s, d in shapes]
    parts = nc.dram_tensor("parts", [2 * B, NPART, P, 2, T], mybir.dt.bfloat16, kind="Internal").ap()
    out = nc.dram_tensor("out_0", [NT, P, C], mybir.dt.float32, kind="ExternalOutput").ap()
    tuned(nc, *aps, parts, out)


def kernel(**inputs):
    import concourse.bacc as bacc
    from concourse.bass_utils import run_bass_kernel_spmd
    arrays = layout(**{k: np.asarray(v) for k, v in inputs.items()})
    nc = bacc.Bacc("TRN2", target_bir_lowering=False, num_devices=1)
    program(nc, [(k, arrays[k].shape, mybir.dt.from_np(arrays[k].dtype)) for k in _INS])
    r = run_bass_kernel_spmd(nc, [{f"in_{k}": arrays[k] for k in _INS}], core_ids=[0])
    return r.results[0]["out_0"].reshape(B, T, C)
```

```python
import numpy as np
import concourse.bass as bass
from concourse import mybir
from contextlib import ExitStack

B, T, C = 4, 256, 128
CD = 96
H, HD = 16, 8
G = 4
E, HID = 8, 256
P = 128
TT = T // P
NT = B * TT
QKV = C + 2 * G * HD
NPART = 3
ROWS = NPART * NPART * HD
KROWS = 96
RING = 3
PRING = 4
UNITS, BEATS = 4, 8
SCALE = HD ** -0.5
NEWTON = 3

GROUPS = 1
GT_ = NT // GROUPS
ET = GT_ + E - 1
NET = GROUPS * ET
BIAS = 2 * HID + C
SKIP = 1 << 20
C_QB, C_KB, C_LN1, C_LN2, C_QN, C_KN, C_BG, C_P = 0, 1, 2, 3, 4, 5, 6, 7
NCOL = C_P + 1
N_I, N_IP, N_BEF = 0, P, 2 * P
NNUM = N_BEF + E * E
R_VB, R_PB, R_BQKV, R_BO, R_BR = 0, C, 2 * C, 2 * C + QKV, 3 * C + QKV
NROW = R_BR + E


def tuned(nc, x, ctxT, cols, rows, wq, wk, wv, wp, wqkv, wg, wo, wr, w1, w2, bias, ident, tri, rope,
          revs, numbers, ones_row, zero_row, q_rows, k_rows, k2_rows, h_rows, out):
    i32 = mybir.dt.int32
    fp32, bf16 = mybir.dt.float32, mybir.dt.bfloat16
    ALU, ACT, AX = mybir.AluOpType, mybir.ActivationFunctionType, mybir.AxisListType
    ctx = ExitStack()
    with ctx:
        def sb(name, shape, dt=fp32):
            return ctx.enter_context(nc.sbuf_tensor(name, shape, dt))

        def ps(name, cols):
            return ctx.enter_context(nc.psum_tensor(name, [P, cols], fp32))

        def sem(name):
            return ctx.enter_context(nc.semaphore(name))

        X = sb("X", [P, NT, C])
        CT = sb("CT", [CD, B * T])
        COL = sb("COL", [P, NCOL])
        ROW = sb("ROW", [P, NROW])
        WQ, WK, WV = sb("WQ", [C, C]), sb("WK", [CD, C]), sb("WV", [CD, C])
        WP, WQKV = sb("WP", [C, C]), sb("WQKV", [C, QKV])
        WG, WO, WR = sb("WG", [C, C]), sb("WO", [C, C]), sb("WR", [C, E])
        W1 = sb("W1", [C, E, 2 * HID])
        W2 = sb("W2", [P, E, 2, C])
        BF = sb("BF", [E, BIAS])
        BPT = sb("BPT", [E, NPART, BIAS], bf16)
        BROW = sb("BROW", [KROWS, E * BIAS], bf16)
        ID = sb("ID", [P, P])
        IDB = sb("IDB", [P, P], bf16)
        TRI = sb("TRI", [P, P])
        TRIB = sb("TRIB", [P, 4, P], bf16)
        ROPE = sb("ROPE", [P, TT, 2, HD])
        REV = sb("REV", [P, E])
        NEGHALF = sb("NEGHALF", [P, 64])
        QBS = sb("QBS", [P, 1])
        QNS = sb("QNS", [P, 1])
        BGH = sb("BGH", [P, 1])
        NUM = sb("NUM", [P, NNUM])
        BEFB = sb("BEFB", [P, P], bf16)
        PARTB = sb("PARTB", [P, P], bf16)
        ONEB = sb("ONEB", [P, P], bf16)
        XB = sb("XB", [P, NT, C])
        X1 = sb("X1", [P, NT, C])
        Z = sb("Z", [P, TT, C])
        ZB = sb("ZB", [P, NT, C])
        HR = sb("HR", [P, NT, 2, C])
        MV1 = sb("MV1", [P, TT, 2])
        ST = sb("ST", [P, TT, 6])
        SM1 = sb("SM1", [P, 8, TT])
        XN = sb("XN", [P, TT, C])
        XNT = sb("XNT", [C, T])
        QKF = sb("QKF", [P, 2, T])
        R1 = sb("R1", [P, 2, T])
        PT = sb("PT", [P, NPART, 2, T], bf16)
        QA = [sb(f"QA{i}", [KROWS, H, T], bf16) for i in range(RING)]
        KA = [sb(f"KA{i}", [KROWS, H, T], bf16) for i in range(RING)]
        VA = [sb(f"VA{i}", [P, TT, H, 32]) for i in range(RING)]
        VB = [sb(f"VB{i}", [P, TT, G, 32]) for i in range(B)]
        NEGM = sb("NEGM", [P, TT, H])
        MHL = sb("MHL", [P, 2, H, TT], bf16)
        MTS = sb("MTS", [2 * TT * H, P], bf16)
        EX = [sb(f"EX{i}", [P, 4 * T]) for i in range(PRING)]
        OS = sb("OS", [P, 2 * T])
        RC = sb("RC", [P, 16, 2])
        ON = sb("ON", [P, 16, 16])
        ONT = sb("ONT", [C, T])
        ST2 = sb("ST2", [P, TT, 6])
        MV2 = sb("MV2", [P, TT, 2])
        SM2 = sb("SM2", [P, 8, TT])
        HZ = XN
        HT = sb("HT", [C, T])
        QKVS = sb("QKVS", [P, TT, QKV])
        NH2 = H + G
        SQ = sb("SQ", [P, TT, NH2 * HD])
        SSQ = sb("SSQ", [P, TT * NH2])
        RQ = sb("RQ", [P, TT * NH2])
        RT = sb("RT", [P, TT * NH2])
        ROT = sb("ROT", [P, TT, HD, NH2])
        ROTS = sb("ROTS", [P, TT, HD, NH2])
        QN = sb("QN", [P, TT, NH2 * HD])
        TH = sb("TH", [C, T])
        GT = sb("GT", [C, T])
        XP = sb("XP", [P, TT, C])
        SS3 = sb("SS3", [P, 4, TT])
        XPT = sb("XPT", [C, T])
        LG = sb("LG", [P, TT, E])
        MXL = sb("MXL", [P, 2, TT])
        EQ = sb("EQ", [P, TT, E])
        OH = sb("OH", [P, NT, E], bf16)
        CNT = sb("CNT", [P, E])
        OVER = sb("OVER", [P, E, GT_])
        TILES = sb("TILES", [P, E])
        BEFT = sb("BEFT", [P, E, E])
        FIRST = sb("FIRST", [P, E])
        AFTER = sb("AFTER", [P, ET, E - 1])
        EJ = sb("EJ", [P, ET])
        EJI = [sb(f"EJI{i}", [1, ET], i32) for i in range(GROUPS)]
        PICK = sb("PICK", [P, 2, GT_, E])
        RANK = sb("RANK", [P, 2, GT_])
        PAST = sb("PAST", [P, GT_, GT_ - 1])
        SLOT = sb("SLOT", [P, 2, GT_])
        INROW = sb("INROW", [P, GT_, P], bf16)
        INTILE = sb("INTILE", [P, GT_, 3, ET], bf16)
        IDS = sb("IDS", [P, 3, ET])
        IDF = sb("IDF", [P, 2, ET])
        IDX = [sb(f"IDX{i}", [P, 2, ET], mybir.dt.uint32) for i in range(GROUPS)]
        GR = sb("GR", [P, 8, 2 * C])
        HJ = [sb(f"HJ{i}", [C, P]) for i in range(2)]
        TJ = [sb(f"TJ{i}", [P, HID]) for i in range(2)]
        AJ = [sb(f"AJ{i}", [P, HID]) for i in range(2)]
        AT = [sb(f"AT{i}", [P, HID]) for i in range(2)]

        S = [ps(f"S{i}", 1024) for i in range(2)]
        MXX = ps("MXX", 1024)
        MX = [MXX[:, 512 * i:512 * i + 512] for i in range(2)]
        O = ps("O", 512)
        MS = ps("MS", 512)
        MSB = MS[:, :].bitcast(bf16)
        U = [S[0][:, 512 * i:512 * i + 512] for i in range(2)]
        TRJ, TA = S[1][:, 0:P], S[1][:, 512:512 + HID]
        Y = O[:, 0:C]

        ld = {k: sem(f"ld_{k}") for k in ("x0", "x1", "ctx", "cols", "rows", "id", "wqk", "wv", "wp", "wqkv",
                                          "tri", "rope", "wg", "wo", "wr", "w1", "w2", "bias", "rev", "num", "pad")}
        cst = sem("constants_ready")
        route_cst = sem("route_cst")
        bias_rows = sem("bias_rows")
        xb_ready = sem("xb_ready")
        va_zero = sem("va_zero")
        dve_step = sem("dve_step")
        pool_step = sem("pool_step")
        act_step = sem("act_step")
        scores = sem("scores")
        probs = sem("probs")
        masked = sem("masked")
        pv = sem("pv")
        mx_scores = sem("mx_scores")
        mx_taken = sem("mx_taken")
        mhl = sem("mhl")
        m_t = sem("m_t")
        mts = sem("mts")
        m_rows = [sem(f"m_rows{i}") for i in range(RING)]
        m_sent = sem("m_sent")
        mv1 = sem("mv1")
        rstd1 = sem("rstd1")
        xn = sem("xn")
        xn_t = sem("xn_t")
        xnt = sem("xnt")
        qk_ps = sem("qk_ps")
        v_ps = sem("v_ps")
        va = sem("va")
        vb = sem("vb")
        qkf = sem("qkf")
        part1, rest1, part2, part3 = sem("part1"), sem("rest1"), sem("part2"), sem("part3")
        q_out, k_out = sem("q_out"), sem("k_out")
        stacked = [sem(f"stacked{i}") for i in range(RING)]
        o_sb = sem("o_sb")
        o_t = sem("o_t")
        on = sem("on")
        on_t = sem("on_t")
        ont = sem("ont")
        pj = sem("pj")
        x1 = sem("x1")
        mv2 = sem("mv2")
        rstd2 = sem("rstd2")
        hz = sem("hz")
        hz_t = sem("hz_t")
        ht = sem("ht")
        qkv_ps = sem("qkv_ps")
        qkvs = sem("qkvs")
        sq = sem("sq")
        ssq = sem("ssq")
        qn = sem("qn")
        qn_t = sem("qn_t")
        gate_ps = sem("gate_ps")
        th = sem("th")
        gated = sem("gated")
        wo_ps = sem("wo_ps")
        xp = sem("xp")
        ss3 = sem("ss3")
        rstd3 = sem("rstd3")
        h2 = sem("h2")
        xp_t = sem("xp_t")
        xpt = sem("xpt")
        lg_ps = sem("lg_ps")
        oh = sem("oh")
        z_ready = sem("z_ready")
        rr = sem("rr")
        h_stored = [sem(f"h_stored{b}") for b in range(B)]
        ranks = sem("ranks")
        experts_of = sem("experts_of")
        places = sem("places")
        ids = sem("ids")
        idx = sem("idx")
        idx_out = sem("idx_out")
        gathered = [sem(f"gathered{j}") for j in range(ET)]
        tr_ps = sem("tr_ps")
        hj = sem("hj")
        u_ps = sem("u_ps")
        tj = sem("tj")
        aj = sem("aj")
        ta_ps = sem("ta_ps")
        at_sb = sem("at_sb")
        y_ps = sem("y_ps")
        done = sem("done")
        scattered = sem("scattered")
        block = ctx.enter_context(nc.Block())

        NE = 2 * B
        SLOTS = NE + 6
        HALVES = [i / 2 for i in range(2 * BEATS)]
        PAUSE = 4

        def has(i, n=NE):
            return 0 <= i < n

        AT1 = {"pj": 7, "hz": 8, "hz_t": 9, "qkv": 10, "squares": 11, "newton1": 11,
               "newton2": 11.5, "newton3": 12, "qn_t": 13.5, "split2": 14}
        AT2 = {"gate": 7, "wo": 9, "xp_t": 10, "h2": 11, "router": 12}
        BOTH = {"o_sb": 4.5, "o_t": 5, "on_t": 6}

        def start(e):
            return BEATS * e + (PAUSE if e >= B else 0)

        def at(step, k, i):
            for table, first, n in ((AT1, 0, B), (AT2, B, B), (BOTH, 0, NE)):
                if step in table:
                    for b in range(n):
                        if BEATS * k + i == start(b + first) + 3 * BEATS + table[step]:
                            return b
                    return None

        ROUTE = [start(B + B * (g + 1) // GROUPS - 1) + 3 * BEATS + AT2["router"] + 1 for g in range(GROUPS)]
        ROUTE = [int(r) for r in ROUTE]
        PACE = 1
        START = (ROUTE[0] + 4,)
        GATHER_LAG = 3
        LAST = SLOTS * BEATS

        LAG = 3

        def attention_at(k, i, behind=0):
            for e in range(NE):
                beat = BEATS * k + i - behind - start(e) - 2 * BEATS - LAG
                if beat in range(BEATS):
                    return e, int(beat)
            return None

        A_STATS, A_XN, A_QK, A_SPLIT, A_V = 0, 1, 2, 3, 7

        def project_at(k, i, step):
            if step == A_V:
                return k if i == A_V and has(k, B) else None
            for b in range(B):
                if BEATS * k + i == (2 * b if b < 2 else BEATS * (b - 1)) + step:
                    return b
            return None

        def banks_at(k, i):
            for e in range(NE):
                beat = BEATS * k + i - start(e) - BEATS
                if 0 <= beat < BEATS:
                    return e, list(range(int(nbanks(e) * beat / BEATS), int(nbanks(e) * (beat + 0.5) / BEATS)))
            return None, []

        def maxima_done(k, i, lag=0):
            for e in range(NE):
                if BEATS * k + i == start(e) + 2 * BEATS + lag:
                    return e
            return None

        def routing(k, i, lag=0):
            for g in range(GROUPS):
                if BEATS * k + i == ROUTE[g] + lag:
                    return g
            return None

        def expert_steps(k, i):
            now = BEATS * k + i
            all_steps = [(START[g] + PACE * s, g, s) for g in range(GROUPS) for s in range(-1, ET + 3)]
            return [(g, s) for time, g, s in sorted(all_steps) if time == now or now == LAST <= time]

        def rows_of(n, lo, hi):
            if n < 8:
                return GR[:, n, lo:hi]
            j = n - 8
            return EX[j // 4][:, 2 * C * (j % 4) + lo:2 * C * (j % 4) + hi]

        def has_tile(j):
            return 0 <= j < ET

        def nbanks(e):
            return 16 if e < B else 12

        def bank_of(e, k):
            if e < B:
                u, q, half = k // 4, k // 2 % 2, k % 2
                return range(4 * u + 2 * half, 4 * u + 2 * half + 2), q, T
            u, w = k // 3, k % 3
            if w == 0:
                return range(4 * u, 4 * u + 4), 0, P
            return range(4 * u + 2 * (w - 1), 4 * u + 2 * w), 1, T

        def banks_before(e):
            return sum(nbanks(i) for i in range(e))

        def ring_uses(e, per=1):
            return (e // RING + 1) * per

        @block.sync
        def _(sp):
            sp.dma_start(X[:, 0:TT, :], x[:, 0:TT, :]).then_inc(ld["x0"], 16)
            sp.dma_start(CT[:, :], ctxT).then_inc(ld["ctx"], 16)
            sp.dma_start(COL[:, :], cols).then_inc(ld["cols"], 16)
            sp.dma_start(WK[:, :], wk).then_inc(ld["wqk"], 16)
            sp.dma_start(WV[:, :], wv).then_inc(ld["wv"], 16)
            sp.dma_start(X[:, TT:NT, :], x[:, TT:NT, :]).then_inc(ld["x1"], 16)
            for i in range(RING):
                sp.dma_start(KA[i][ROWS:KROWS, :, :].rearrange("p h t -> p (h t)").bitcast(fp32),
                             ones_row.broadcast_to([KROWS - ROWS, H * T // 2])).then_inc(ld["pad"], 16)
                sp.dma_start(QA[i][ROWS:KROWS, :, :].rearrange("p h t -> p (h t)").bitcast(fp32),
                             zero_row.broadcast_to([KROWS - ROWS, H * T // 2])).then_inc(ld["pad"], 16)

            def parts_out(e):
                nk = H if e < B else G
                k_e = k_rows[e] if e < B else k2_rows[e - B]
                for c, ready in enumerate((part1, part2, part3)):
                    sp.wait_ge(ready, e + 1)
                    sp.dma_start(q_rows[e, c].rearrange("j p t -> p j t"),
                                 PT[:, c, 0, None, :].broadcast_to([P, NPART, T])).then_inc(q_out, 16)
                    sp.dma_start(k_e[:, c].rearrange("i p t -> p i t"),
                                 PT[0:nk * HD, c, 1, None, :].broadcast_to([nk * HD, NPART, T])).then_inc(k_out, 16)

            def stacks_in(e):
                nk = H if e < B else G
                k_e = k_rows[e] if e < B else k2_rows[e - B]
                if e >= RING:
                    sp.wait_ge(scores, BEATS * (e - RING + 1))
                sp.wait_ge(q_out, 16 * NPART * (e + 1))
                sp.dma_start(QA[e % RING][0:ROWS, :, :].rearrange("p h t -> p (h t)"),
                             q_rows[e].rearrange("i j (d h) t -> (i j d) (h t)", h=H)).then_inc(stacked[e % RING], 16)
                sp.wait_ge(k_out, 16 * NPART * (e + 1))
                sp.dma_start(KA[e % RING][0:ROWS, 0:nk, :].rearrange("p h t -> p (h t)"),
                             k_e.rearrange("i j (d h) t -> (i j d) (h t)", h=nk)).then_inc(stacked[e % RING], 16)

            sp.dma_start(TRI[:, :], tri).then_inc(ld["tri"], 16)
            sp.dma_start(WP[:, :], wp).then_inc(ld["wp"], 16)
            sp.dma_start(WQKV[:, :], wqkv).then_inc(ld["wqkv"], 16)
            sp.dma_start(ROPE[:, :, :, :], rope).then_inc(ld["rope"], 16)
            def expert_weights(e):
                sp.dma_start(W1[:, e, :], w1[:, e, :]).then_inc(ld["w1"], 16)
                sp.dma_start(W2[:, e, :, :], w2[:, e, :, :]).then_inc(ld["w2"], 16)

            def maxima_in(e):
                sp.wait_ge(mts, e + 1)
                for part in range(2):
                    r = ROWS + part
                    sp.dma_start(QA[e % RING][r:r + 1, :, :].rearrange("p h (q t) -> p (h q) t", q=TT),
                                 MTS[part * TT * H:(part + 1) * TT * H, :]).then_inc(m_rows[e % RING], 16)

            parts_out(0)
            stacks_in(0)
            sp.dma_start(WG[:, :], wg).then_inc(ld["wg"], 16)
            sp.dma_start(WO[:, :], wo).then_inc(ld["wo"], 16)
            sp.dma_start(WR[:, :], wr).then_inc(ld["wr"], 16)
            sp.dma_start(REV[:, :], revs.broadcast_to([P, E])).then_inc(ld["rev"], 16)
            sp.dma_start(BF[:, :], bias).then_inc(ld["bias"], 16)
            sp.dma_start(NUM[:, :], numbers.broadcast_to([P, NNUM])).then_inc(ld["num"], 16)
            parts_out(1)
            stacks_in(1)
            parts_out(2)
            stacks_in(2)
            maxima_in(0)
            expert_weights(0)
            parts_out(3)
            maxima_in(1)
            expert_weights(1)
            stacks_in(3)
            maxima_in(2)
            expert_weights(2)
            parts_out(4)
            maxima_in(3)
            stacks_in(4)
            expert_weights(3)
            for e in range(5, NE):
                parts_out(e)
                stacks_in(e)
                maxima_in(e - 1)
                expert_weights(e - 1)
            maxima_in(NE - 1)
            expert_weights(NE - 1)
            for b in range(B):
                sp.wait_ge(h2, b + 1)
                sp.wait_ge(rr, b + 1)
                at_row = T * (b % (B // GROUPS))
                sp.dma_start(h_rows[b // (B // GROUPS)][at_row:at_row + T].rearrange("(t p) c -> p t c", p=P),
                             HR[:, TT * b:TT * b + TT, :, :].rearrange("p t a c -> p t (a c)"))\
                    .then_inc(h_stored[b], 16)
            sp.wait_ge(scattered, 16 * NET)

        @block.gpsimd
        def _(pool):
            n = [0]

            def link(ins):
                n[0] += 1
                ins.then_inc(pool_step, 1)
                pool.wait_ge(pool_step, n[0])

            def rsqrt(out_, in_, w, mult, eps):
                link(pool.tensor_scalar(out_, in_, mult, eps, ALU.mult, ALU.add))
                return pool.tensor_tensor(out_, out_, NEGHALF[:, 0:w], ALU.pow)

            link(pool.memset(NEGHALF[:, :], -0.5))

            def query_constants():
                pool.wait_ge(ld["cols"], 16)
                pool.tensor_scalar(QBS[:, :], COL[:, C_QB:C_QB + 1], SCALE, None, ALU.mult).then_inc(cst, 1)
                pool.tensor_scalar(QNS[:, :], COL[:, C_QN:C_QN + 1], SCALE, None, ALU.mult).then_inc(cst, 1)
                pool.tensor_scalar(BGH[:, :], COL[:, C_BG:C_BG + 1], 0.5, None, ALU.mult).then_inc(cst, 1)

            def ln1_rstd(b):
                pool.wait_ge(mv1, b + 1)
                if b:
                    pool.wait_ge(xn, b)
                rsqrt_last = rsqrt(SM1[:, 0, :], MV1[:, :, 1], TT, 1.0, 1e-5)
                rsqrt_last.then_inc(rstd1, 1)

            def split_rest(e):
                pool.wait_ge(part1, e + 1)
                pool.tensor_tensor(R1[:, :, :], QKF[:, :, :], PT[:, 0, :, :], ALU.subtract).then_inc(rest1, 1)

            def split_last(e):
                pool.wait_ge(rest1, e + 1)
                pool.wait_ge(part2, e + 1)
                pool.tensor_tensor(PT[:, 2, :, :], R1[:, :, :], PT[:, 1, :, :], ALU.subtract).then_inc(part3, 1)

            ln1_rstd(0)
            query_constants()
            ln1_rstd(1)
            pool.wait_ge(ld["id"], 16)
            pool.tensor_copy(IDB[:, :], ID[:, :]).then_inc(cst, 1)

            def zero_values(i):
                for V_, nh in (((VA[i], H),) if i < RING else ()) + ((VB[i], G),):
                    link(pool.memset(V_[:, :, :, :], 0.0))
                    v = V_[:, :, :, :].rearrange("p k (r s j) c -> p (k r) s j c", s=2, j=nh // 4)
                    for s in range(2):
                        pool.memset(v[:, :, s, :, 16 + s:17 + s], 1.0).then_inc(va_zero, 1)

            def causal_masks():
                pool.wait_ge(ld["tri"], 16)
                for j in range(4):
                    pool.tensor_copy(TRIB[:, j, :], TRI[:, :]).then_inc(cst, 1)

            def projected_bias():
                pool.wait_ge(ld["x0"], 16)
                pool.wait_ge(ld["x1"], 16)
                pool.wait_ge(ld["rows"], 16)
                pool.tensor_tensor(XB[:, :, :], X[:, :, :],
                                   ROW[:, None, R_PB:R_PB + C].broadcast_to([P, NT, C]), ALU.add).then_inc(xb_ready, 1)

            def routing_constants():
                pool.tensor_scalar(BEFB[:, :], TRI[:, :], -1.0, 1.0 / P, ALU.mult, ALU.min).then_inc(route_cst, 1)
                pool.memset(ONEB[:, :], 1.0).then_inc(route_cst, 1)
                pool.memset(PARTB[:, :], 1.0 / P).then_inc(route_cst, 1)

            def bias_part(step):
                if step == 0:
                    link(pool.memset(BROW[:, :], 0.0))
                elif step == 1:
                    pool.wait_ge(ld["bias"], 16)
                    link(pool.tensor_scalar(BF[:, 2 * HID:BIAS], BF[:, 2 * HID:BIAS], 2.0, None, ALU.mult))
                elif step % 2 == 0:
                    link(pool.tensor_copy(BPT[:, step // 2 - 1, :], BF[:, :]))
                elif step < 2 * NPART:
                    link(pool.tensor_tensor(BF[:, :], BF[:, :], BPT[:, step // 2 - 1, :], ALU.subtract))
                else:
                    for c in range(NPART):
                        pool.dma_start(BROW[c:c + 1, :], BPT[:, c, :]).then_inc(bias_rows, 16)

            def ln2_rstd(b):
                pool.wait_ge(mv2, b + 1)
                if b:
                    pool.wait_ge(hz, b)
                pool.tensor_tensor(SM2[:, 2:4, :], SM2[:, 0:2, :],
                                   NEGHALF[:, 0:2 * TT].rearrange("p (a t) -> p a t", a=2), ALU.pow).then_inc(rstd2, 1)
                pool.wait_ge(rstd2, b + 1)
                if b:
                    pool.wait_ge(z_ready, b)
                for t in range(TT):
                    link(pool.tensor_scalar(Z[:, t, :], X1[:, TT * b + t, :],
                                            MV2[:, t, 0:1], SM2[:, 2, t:t + 1], ALU.subtract, ALU.mult))
                pool.tensor_tensor(ZB[:, TT * b:TT * b + TT, :], Z[:, :, :],
                                   ROW[:, None, R_BO:R_BO + C].broadcast_to([P, TT, C]), ALU.add)\
                    .then_inc(z_ready, 1)

            def head_squares(b):
                pool.wait_ge(qkvs, b + 1)
                if b:
                    pool.wait_ge(ssq, b)
                pool.tensor_tensor(SQ[:, :, :], QKVS[:, :, 0:NH2 * HD], QKVS[:, :, 0:NH2 * HD], ALU.mult)\
                    .then_inc(sq, 1)
                for s in range(2):
                    pool.tensor_copy(
                        VB[b][:, :, :, 8 * s:8 * s + 8].rearrange("p k (r s) c -> p k r s c", s=2)[:, :, :, s, :],
                        QKVS[:, :, NH2 * HD:QKV].rearrange("p k (r s c) -> p k r s c", s=2, c=HD)[:, :, :, s, :])\
                        .then_inc(vb, 1)

            def rms3(b):
                pool.wait_ge(ss3, b + 1)
                if b:
                    pool.wait_ge(h2, b)
                    pool.wait_ge(oh, b)
                rsqrt(SS3[:, 1, :], SS3[:, 0, :], TT, 1.0 / C, 1e-6).then_inc(rstd3, 1)

            def causal(e, i):
                u, kt = i // 2, i % 2
                w = T if kt == 0 else P
                g = BEATS * e + i
                pool.wait_ge(probs, g + 1)
                v = EX[g % PRING][:, 0:4 * w].rearrange("p (j t) -> p j t", j=4)[:, :, 0:P]
                pool.affine_select(out=v, in_=v, pattern=[[0, 4], [1, P]], compare_op=ALU.is_ge, fill=0.0,
                                   base=0, channel_multiplier=-1).then_inc(masked, 1)

            gathered_in_slots = [[] for _ in range(GROUPS)]

            def gathers_at(g, n0):
                js = [j for j in range(2 * n0, 2 * n0 + 2) if n0 >= 0 and has_tile(j)]
                gathered_in_slots[g] += js
                return js

            def gather(g, j):
                if j == 0:
                    pool.wait_ge(idx, g + 1)
                    if True:
                        pool.wait_ge(pv, BEATS * NE)
                    for b in range(B * g // GROUPS, B * (g + 1) // GROUPS):
                        pool.wait_ge(h_stored[b], 16)
                pool.indirect_dma_start(rows_of(ET * g + j, 0, 2 * C), None, h_rows[g],
                                        bass.IndirectOffsetOnAxis(IDX[g][:, 0, j:j + 1], 0))\
                    .then_inc(gathered[j], 16)

            def scatter(g, j):
                pool.wait_ge(idx_out, g + 1)
                pool.wait_ge(done, ET * g + j + 1)
                pool.indirect_dma_start(out, bass.IndirectOffsetOnAxis(IDX[g][:, 1, j:j + 1], 0),
                                        rows_of(ET * g + j, C, 2 * C), None, bounds_check=B * T - 1, oob_is_err=False)\
                    .then_inc(scattered, 16)

            for k in range(SLOTS):
                for i in HALVES:
                    b = project_at(k, i, A_STATS)
                    if b is not None and b > 1:
                        ln1_rstd(b)
                    now = attention_at(k, i)
                    if now and now[0] >= B:
                        causal(*now)
                    b = at("qkv", k, i)
                    if b is not None:
                        head_squares(b)
                    b = project_at(k, i, A_QK)
                    if b is not None and b >= 2:
                        split_rest(b)
                    b = project_at(k, i, A_SPLIT)
                    if b is not None and b >= 2:
                        split_last(b)
                    b = at("qn_t", k, i)
                    if b is not None:
                        split_rest(b + B)
                    b = at("split2", k, i)
                    if b is not None:
                        split_last(b + B)
                    b = at("pj", k, i)
                    if b is not None:
                        ln2_rstd(b)
                    b = at("wo", k, i)
                    if b is not None:
                        pool.wait_ge(xp, b + 1)
                        pool.tensor_tensor(HR[:, TT * b:TT * b + TT, 1, :], X1[:, TT * b:TT * b + TT, :],
                                           XP[:, :, :], ALU.add).then_inc(rr, 1)
                        rms3(b)
                    once = {5: lambda: zero_values(0), 12.5: lambda: zero_values(1), 14: lambda: zero_values(2),
                            17: projected_bias, 18: causal_masks, 19: routing_constants,
                            20.5: lambda: zero_values(3)}.get(BEATS * k + i)
                    if once:
                        once()
                    if k == 3 and i in range(BEATS):
                        bias_part(int(i))
                    for g in range(GROUPS):
                        n0 = BEATS * k + i - ROUTE[g] - GATHER_LAG
                        for j in (gathers_at(g, int(n0)) if i in range(BEATS) else ()):
                            gather(g, j)
                    for g, s in expert_steps(k, i):
                        if has_tile(s - 3):
                            scatter(g, s - 3)
            for j in range(ET):
                if j not in gathered_in_slots[GROUPS - 1]:
                    gather(GROUPS - 1, j)
            for g, s in expert_steps(SLOTS, 0):
                if has_tile(s - 3):
                    scatter(g, s - 3)

        @block.scalar
        def _(act):
            n = [0]

            def link(ins):
                n[0] += 1
                ins.then_inc(act_step, 1)
                act.wait_ge(act_step, n[0])

            act.dma_start(ID[:, :], ident).then_inc(ld["id"], 16)
            act.dma_start(WQ[:, :], wq).then_inc(ld["wqk"], 16)
            act.dma_start(ROW[:, :], rows.broadcast_to([P, NROW])).then_inc(ld["rows"], 16)
            def split(e):
                if e:
                    act.wait_ge(q_out, 16 * NPART * e)
                    act.wait_ge(k_out, 16 * NPART * e)
                act.wait_ge(qkf, e + 1)
                act.activation(PT[:, 0, :, :], QKF[:, :, :], ACT.Copy).then_inc(part1, 1)

            def split_second(e):
                act.wait_ge(rest1, e + 1)
                act.activation(PT[:, 1, :, :], R1[:, :, :], ACT.Copy).then_inc(part2, 1)

            def expert_step(g, s):
                if has_tile(s + 1):
                    n = ET * g + s + 1
                    act.wait_ge(tr_ps, n + 1)
                    if n >= 2:
                        act.wait_ge(u_ps, n - 1)
                    act.activation(HJ[n % 2][:, :], TRJ, ACT.Copy, scale=COL[:, C_LN2:C_LN2 + 1])\
                        .then_inc(hj, 1)
                if has_tile(s):
                    n = ET * g + s
                    act.wait_ge(u_ps, n + 1)
                    if n >= 2:
                        act.wait_ge(aj, n - 1)
                    act.activation(TJ[n % 2][:, :], U[n % 2][:, HID:2 * HID], ACT.Tanh, scale=0.5).then_inc(tj, 1)

            def qkf_free(e):
                if e:
                    act.wait_ge(rest1, e)
                    act.wait_ge(part1, e)

            for k in range(SLOTS):
                for i in HALVES:
                    if attention_at(k, i):
                        e, beat = attention_at(k, i)
                        g = BEATS * e + beat
                        w = 4 * T if e < B or beat % 2 == 0 else 4 * P
                        act.wait_ge(scores, g + 1)
                        if g >= PRING:
                            act.wait_ge(pv, g - PRING + 1)
                        act.activation(EX[g % PRING][:, 0:w], S[g % 2][:, 0:w], ACT.Exp).then_inc(probs, 1)
                    b = at("o_sb", k, i)
                    if b is not None:
                        act.wait_ge(pv, BEATS * (b + 1))
                        if b:
                            act.wait_ge(o_t, b)
                        act.activation(OS[:, :], O[:, :], ACT.Copy).then_inc(o_sb, 1)
                    e = maxima_done(k, i, 0.5)
                    if e is not None:
                        act.wait_ge(m_t, e + 1)
                        if e:
                            act.wait_ge(m_rows[(e - 1) % RING], 32 * ring_uses(e - 1))
                        act.activation(MTS[:, :], MSB[0:2 * TT * H, 0:P], ACT.Copy).then_inc(mts, 1)
                    b = project_at(k, i, A_XN)
                    if b is not None:
                        act.wait_ge(xn_t, b + 1)
                        if b:
                            act.wait_ge(qk_ps, b)
                        act.activation(XNT[:, :], MS[:, 0:T], ACT.Copy).then_inc(xnt, 1)
                    b = project_at(k, i, A_QK)
                    if b is not None:
                        act.wait_ge(qk_ps, b + 1)
                        act.wait_ge(cst, 1)
                        act.wait_ge(ld["cols"], 16)
                        qkf_free(b)
                        act.activation(QKF[:, 0, :], MS[:, 0:T], ACT.Identity, bias=QBS[:, :], scale=SCALE)
                        act.activation(QKF[:, 1, :], MS[:, T:2 * T], ACT.Identity,
                                       bias=COL[:, C_KB:C_KB + 1]).then_inc(qkf, 1)
                        split(b)
                    b = at("hz_t", k, i)
                    if b is not None:
                        act.wait_ge(hz_t, b + 1)
                        if b:
                            act.wait_ge(qkv_ps, b)
                        act.activation(HT[:, :], MS[:, 0:T], ACT.Copy, scale=COL[:, C_LN1:C_LN1 + 1]).then_inc(ht, 1)
                    b = at("qn_t", k, i)
                    if b is not None:
                        act.wait_ge(qn_t, b + 1)
                        qkf_free(b + 4)
                        act.activation(QKF[:, 0, :], MS[:, 0:T], ACT.Copy, scale=QNS[:, :])
                        act.activation(QKF[0:G * HD, 1, :], MS[0:G * HD, T:2 * T], ACT.Copy,
                                       scale=COL[0:G * HD, C_KN:C_KN + 1]).then_inc(qkf, 1)
                        split(b + B)
                    b = at("split2", k, i)
                    if b is not None:
                        split_second(b + B)
                    b = project_at(k, i, A_SPLIT)
                    if b is not None:
                        split_second(b)
                    b = at("wo", k, i)
                    if b is not None:
                        act.wait_ge(xp, b + 1)
                        if b:
                            act.wait_ge(rstd3, b)
                        for t in range(TT):
                            last = act.activation(TH[:, P * t:P * t + P], XP[:, t, :], ACT.Square,
                                                  accum_out=SS3[:, 0, t:t + 1])
                        last.then_inc(ss3, 1)
                    b = at("xp_t", k, i)
                    if b is not None:
                        act.wait_ge(xp_t, b + 1)
                        if b:
                            act.wait_ge(lg_ps, b)
                        act.activation(XPT[:, :], MS[:, 0:T], ACT.Copy,
                                       scale=COL[:, C_LN2:C_LN2 + 1]).then_inc(xpt, 1)
                    b = at("on_t", k, i)
                    if b is not None:
                        act.wait_ge(on_t, b + 1)
                        if 0 < b <= B:
                            act.wait_ge(pj, b)
                        elif b > B:
                            act.wait_ge(gated, b - 4)
                            act.wait_ge(gate_ps, b - 4)
                        act.activation(ONT[:, :], MS[:, 0:T], ACT.Copy).then_inc(ont, 1)
                    b = at("gate", k, i)
                    if b is not None:
                        act.wait_ge(gate_ps, b + 1)
                        if b:
                            act.wait_ge(gated, b)
                            act.wait_ge(ss3, b)
                        act.activation(TH[:, :], MS[:, 0:T], ACT.Tanh, bias=BGH[:, :], scale=0.5).then_inc(th, 1)
                    for g, s in expert_steps(k, i):
                        expert_step(g, s)
            for g, s in expert_steps(SLOTS, 0):
                expert_step(g, s)

        @block.vector
        def _(dve):
            n = [0]

            def link(ins):
                n[0] += 1
                ins.then_inc(dve_step, 1)
                dve.wait_ge(dve_step, n[0])

            def statistics(src, st, mv):
                for t in range(TT):
                    last = dve.bn_stats(st[:, t, :], src[:, t, :])
                link(last)
                for t in range(TT):
                    last = dve.bn_aggr(mv[:, t, :], st[:, t, :])
                return last

            def maxima(e, k):
                heads, q, w = bank_of(e, k)
                g = banks_before(e) + k
                if k == 0 and e:
                    dve.wait_ge(mhl, e)
                dve.wait_ge(mx_scores, g + 1)
                dve.tensor_reduce(out=NEGM[:, q, heads[0]:heads[-1] + 1],
                                  in_=MX[g % 2][:, 0:len(heads) * w].rearrange("p (h t) -> p h t", t=w),
                                  axis=AX.X, op=ALU.max, negate=True).then_inc(mx_taken, 1)

            def minus_maxima(e):
                dve.wait_ge(mx_taken, banks_before(e + 1))
                if e:
                    dve.wait_ge(m_t, e)
                link(dve.tensor_copy(MHL[:, 0, :, :], NEGM[:, :, :].rearrange("p q h -> p h q")))
                dve.tensor_tensor(MHL[:, 1, :, :], NEGM[:, :, :].rearrange("p q h -> p h q"), MHL[:, 0, :, :],
                                  ALU.subtract).then_inc(mhl, 1)

            def split_on_dve(e):
                dve.wait_ge(part1, e + 1)
                dve.tensor_tensor(R1[:, :, :], QKF[:, :, :], PT[:, 0, :, :], ALU.subtract).then_inc(rest1, 1)
                dve.wait_ge(rest1, e + 1)
                dve.wait_ge(part2, e + 1)
                dve.tensor_tensor(PT[:, 2, :, :], R1[:, :, :], PT[:, 1, :, :], ALU.subtract).then_inc(part3, 1)

            def values(b):
                dve.wait_ge(v_ps, b + 1)
                dve.wait_ge(va_zero, 4 * (b % RING) + 2)
                dve.wait_ge(ld["rows"], 16)
                if b >= RING:
                    dve.wait_ge(pv, BEATS * (b - RING + 1))
                for s in range(2):
                    for t in range(TT):
                        last = dve.tensor_tensor(
                            VA[b % RING][:, t, :, 8 * s:8 * s + 8]
                            .rearrange("p (r s j) c -> p r s j c", s=2, j=4)[:, :, s, :, :],
                            MS[:, C * t:C * t + C].rearrange("p (r s j c) -> p r s j c", s=2, j=4, c=HD)[:, :, s, :, :],
                            ROW[:, R_VB:R_VB + C].rearrange("p (r s j c) -> p r s j c", s=2, j=4, c=HD)[:, :, s, :, :],
                            ALU.add)
                last.then_inc(va, 1)

            def total(out_, in_):
                return dve.tensor_reduce(out=out_, in_=in_, axis=AX.X, op=ALU.add)

            def route(g):
                oh_ = OH[:, GT_ * g:GT_ * g + GT_, :]
                number = NUM[:, N_I:N_I + P]
                if g == 0:
                    dve.wait_ge(ld["num"], 16)
                dve.wait_ge(ranks, g + 1)
                if g:
                    dve.wait_ge(ids, g)
                link(dve.tensor_copy(CNT[:, :], MX[0][:, GT_ * E:GT_ * E + E]))
                dve.tensor_tensor(PICK[:, 0, :, :], MX[0][:, 0:GT_ * E].rearrange("p (t e) -> p t e", e=E), oh_,
                                  ALU.mult)
                link(dve.tensor_tensor(OVER[:, :, :], CNT[:, :, None].broadcast_to([P, E, GT_]),
                                       number[:, None, 0:GT_].broadcast_to([P, E, GT_]), ALU.is_gt))
                total(RANK[:, 0, :], PICK[:, 0, :, :])
                link(total(TILES[:, :], OVER[:, :, :]))
                dve.tensor_tensor(PAST[:, :, :], RANK[:, 0, :, None].broadcast_to([P, GT_, GT_ - 1]),
                                  number[:, None, 1:GT_].broadcast_to([P, GT_, GT_ - 1]), ALU.is_ge)
                link(dve.tensor_tensor(BEFT[:, :, :],
                                       NUM[:, N_BEF:N_BEF + E * E].rearrange("p (e f) -> p e f", e=E),
                                       TILES[:, None, :].broadcast_to([P, E, E]), ALU.mult))
                total(SLOT[:, 0, :], PAST[:, :, :])
                link(total(FIRST[:, :], BEFT[:, :, :]))
                dve.tensor_tensor(SLOT[:, 1, :], RANK[:, 0, :], SLOT[:, 0, :], ALU.subtract)
                link(dve.tensor_tensor(PICK[:, 1, :, :], oh_, FIRST[:, None, :].broadcast_to([P, GT_, E]), ALU.mult))
                link(total(RANK[:, 1, :], PICK[:, 1, :, :]))
                link(dve.tensor_tensor(RANK[:, 1, :], RANK[:, 1, :], SLOT[:, 0, :], ALU.add))
                link(dve.tensor_tensor(INTILE[:, :, 0, :], number[:, None, 0:ET].broadcast_to([P, GT_, ET]),
                                       RANK[:, 1, :, None].broadcast_to([P, GT_, ET]), ALU.is_equal))
                dve.tensor_tensor(INROW[:, :, :], NUM[:, None, N_IP:N_IP + P].broadcast_to([P, GT_, P]),
                                  SLOT[:, 1, :, None].broadcast_to([P, GT_, P]), ALU.is_equal)
                dve.tensor_scalar(INTILE[:, :, 1, :], INTILE[:, :, 0, :], COL[:, C_P:C_P + 1], None, ALU.mult)
                dve.tensor_tensor(INTILE[:, :, 2, :], INTILE[:, :, 0, :],
                                  number[:, 0:GT_, None].broadcast_to([P, GT_, ET]), ALU.mult).then_inc(places, 1)
                link(dve.tensor_tensor(AFTER[:, :, :], number[:, 0:ET, None].broadcast_to([P, ET, E - 1]),
                                       FIRST[:, None, 1:E].broadcast_to([P, ET, E - 1]), ALU.is_ge))
                link(total(EJ[:, :], AFTER[:, :, :]))
                dve.tensor_copy(EJI[g][:, :], EJ[0:1, :]).then_inc(experts_of, 1)

            def indices(g):
                dve.wait_ge(ids, g + 1)
                link(dve.tensor_copy(IDS[:, :, :], MX[1][:, 0:3 * ET].rearrange("p (a j) -> p a j", a=3)))
                dve.scalar_tensor_tensor(IDX[g][:, 0, :], IDS[:, 2, :], float(P), IDS[:, 1, :], ALU.mult, ALU.add)\
                    .then_inc(idx, 1)
                link(dve.scalar_tensor_tensor(IDF[:, 0, :], IDS[:, 2, :], float(P), IDS[:, 1, :], ALU.mult, ALU.add))
                link(dve.scalar_tensor_tensor(IDF[:, 1, :], IDS[:, 0, :], float(P * GT_ * g - SKIP), IDF[:, 0, :],
                                              ALU.mult, ALU.add))
                dve.tensor_scalar(IDX[g][:, 1, :], IDF[:, 1, :], float(SKIP), None, ALU.add).then_inc(idx_out, 1)

            def expert_step(g, s):
                if has_tile(s):
                    n = ET * g + s
                    dve.wait_ge(tj, n + 1)
                    if n >= 2:
                        dve.wait_ge(ta_ps, n - 1)
                    dve.scalar_tensor_tensor(AJ[n % 2][:, :], TJ[n % 2][:, :], 1.0, U[n % 2][:, 0:HID],
                                             ALU.add, ALU.mult).then_inc(aj, 1)
                if has_tile(s - 1):
                    n = ET * g + s - 1
                    dve.wait_ge(ta_ps, n + 1)
                    if n >= 2:
                        dve.wait_ge(y_ps, n - 1)
                    dve.tensor_copy(AT[n % 2][:, :], TA).then_inc(at_sb, 1)
                if has_tile(s - 2):
                    n = ET * g + s - 2
                    dve.wait_ge(y_ps, n + 1)
                    dve.scalar_tensor_tensor(rows_of(n, C, 2 * C), Y, 0.5, rows_of(n, C, 2 * C),
                                             ALU.mult, ALU.add).then_inc(done, 1)

            for k in range(SLOTS):
                for i in HALVES:
                    b = project_at(k, i, A_STATS)
                    if b is not None:
                        dve.wait_ge(ld["x1" if b else "x0"], 16)
                        if b:
                            dve.wait_ge(rstd1, b)
                        statistics(X[:, TT * b:TT * b + TT, :], ST, MV1).then_inc(mv1, 1)
                    e = maxima_done(k, i)
                    if e is not None:
                        minus_maxima(e)
                    e, banks = banks_at(k, i)
                    for kk in banks:
                        maxima(e, kk)
                    b = project_at(k, i, A_XN)
                    if b is not None:
                        dve.wait_ge(rstd1, b + 1)
                        if b:
                            dve.wait_ge(xn_t, b)
                        for t in range(TT):
                            last = dve.tensor_scalar(XN[:, t, :], X[:, TT * b + t, :], MV1[:, t, 0:1],
                                                     SM1[:, 0, t:t + 1], ALU.subtract, ALU.mult)
                        last.then_inc(xn, 1)
                    b = project_at(k, i, A_SPLIT)
                    if b is not None and b < 2:
                        split_on_dve(b)
                    if project_at(k, i, A_V) is not None:
                        values(k)
                    b = at("qkv", k, i)
                    if b is not None:
                        dve.wait_ge(qkv_ps, b + 1)
                        if b:
                            dve.wait_ge(sq, b)
                            dve.wait_ge(vb, 2 * b)
                        dve.tensor_tensor(QKVS[:, :, :], MS[:, 0:TT * QKV].rearrange("p (t c) -> p t c", t=TT),
                                          ROW[:, None, R_BQKV:R_BQKV + QKV].broadcast_to([P, TT, QKV]), ALU.add)                            .then_inc(qkvs, 1)
                        dve.wait_ge(qkvs, b + 1)
                        dve.wait_ge(ld["rope"], 16)
                        qk = QKVS[:, :, 0:NH2 * HD].rearrange("p t (c h) -> p t c h", c=HD)
                        hh = HD // 2
                        dve.tensor_tensor(ROT[:, :, :, :], qk,
                                          ROPE[:, :, 0, :, None].broadcast_to([P, TT, HD, NH2]), ALU.mult)
                        dve.tensor_tensor(ROTS[:, :, 0:hh, :], qk[:, :, hh:HD, :],
                                          ROPE[:, :, 1, 0:hh, None].broadcast_to([P, TT, hh, NH2]), ALU.mult)
                        link(dve.tensor_tensor(ROTS[:, :, hh:HD, :], qk[:, :, 0:hh, :],
                                               ROPE[:, :, 1, hh:HD, None].broadcast_to([P, TT, hh, NH2]), ALU.mult))
                        link(dve.tensor_tensor(ROT[:, :, :, :], ROT[:, :, :, :], ROTS[:, :, :, :], ALU.add))
                    b = at("squares", k, i)
                    if b is not None:
                        dve.wait_ge(sq, b + 1)
                        dve.tensor_reduce(out=SSQ[:, :], in_=SQ[:, :, :].rearrange("p t (c h) -> p t h c", c=HD),
                                          axis=AX.X, op=ALU.add).then_inc(ssq, 1)
                        dve.wait_ge(ssq, b + 1)
                        link(dve.tensor_scalar(SSQ[:, :], SSQ[:, :], 1.0 / HD, 1e-6, ALU.mult, ALU.add))
                        link(dve.tensor_scalar(RQ[:, :].bitcast(i32), SSQ[:, :].bitcast(i32), 1, None,
                                               ALU.logical_shift_right))
                        link(dve.tensor_scalar(RQ[:, :].bitcast(i32), RQ[:, :].bitcast(i32), -1.0, float(0x5F3759DF),
                                               ALU.mult, ALU.add))
                    for step in range(1, NEWTON + 1):
                        b = at(f"newton{step}", k, i)
                        if b is not None:
                            link(dve.scalar_tensor_tensor(RT[:, :], RQ[:, :], -0.5, RQ[:, :], ALU.mult, ALU.mult))
                            link(dve.tensor_tensor(RT[:, :], RT[:, :], SSQ[:, :], ALU.mult))
                            link(dve.scalar_tensor_tensor(RQ[:, :], RT[:, :], 1.5, RQ[:, :], ALU.add, ALU.mult))
                    if b is not None:
                        if b:
                            dve.wait_ge(qn_t, b)
                        rq_ = RQ[:, :].rearrange("p (t h) -> p t h", t=TT)
                        dve.tensor_tensor(QN[:, :, 0:C].rearrange("p t (c h) -> p t c h", c=HD), ROT[:, :, :, 0:H],
                                          rq_[:, :, None, 0:H].broadcast_to([P, TT, HD, H]), ALU.mult)
                        dve.tensor_tensor(QN[:, :, C:C + G * HD].rearrange("p t (c h) -> p t c h", c=HD),
                                          ROT[:, :, :, H:NH2],
                                          rq_[:, :, None, H:NH2].broadcast_to([P, TT, HD, G]), ALU.mult).then_inc(qn, 1)
                    b = at("wo", k, i)
                    if b is not None:
                        dve.wait_ge(wo_ps, b + 1)
                        dve.wait_ge(z_ready, b + 1)
                        if b:
                            dve.wait_ge(h2, b)
                            dve.wait_ge(xp_t, b)
                            dve.wait_ge(rr, b)
                            dve.wait_ge(ss3, b)
                        dve.scalar_tensor_tensor(XP[:, :, :], MS[:, 0:T].rearrange("p (t c) -> p t c", t=TT), 0.5,
                                                 ZB[:, TT * b:TT * b + TT, :], ALU.mult, ALU.add).then_inc(xp, 1)
                    b = at("h2", k, i)
                    if b is not None:
                        dve.wait_ge(rstd3, b + 1)
                        for t in range(TT):
                            last = dve.tensor_scalar(HR[:, TT * b + t, 0, :], XP[:, t, :], SS3[:, 1, t:t + 1], None, ALU.mult)
                        last.then_inc(h2, 1)
                    b = at("router", k, i)
                    if b is not None:
                        dve.wait_ge(lg_ps, b + 1)
                        dve.wait_ge(rstd3, b + 1)
                        for t in range(TT):
                            last = dve.scalar_tensor_tensor(LG[:, t, :], MS[:, E * t:E * t + E], SS3[:, 1, t:t + 1],
                                                            ROW[:, R_BR:R_BR + E], ALU.mult, ALU.add)
                        link(last)
                        link(dve.tensor_reduce(out=MXL[:, 0, :], in_=LG[:, :, :], axis=AX.X, op=ALU.max))
                        link(dve.tensor_tensor(EQ[:, :, :], LG[:, :, :],
                                               MXL[:, 0, :, None].broadcast_to([P, TT, E]), ALU.is_equal))
                        dve.wait_ge(ld["rev"], 16)
                        link(dve.tensor_tensor(EQ[:, :, :], EQ[:, :, :],
                                               REV[:, None, :].broadcast_to([P, TT, E]), ALU.mult))
                        link(dve.tensor_reduce(out=MXL[:, 1, :], in_=EQ[:, :, :], axis=AX.X, op=ALU.max))
                        dve.tensor_tensor(OH[:, TT * b:TT * b + TT, :], REV[:, None, :].broadcast_to([P, TT, E]),
                                          MXL[:, 1, :, None].broadcast_to([P, TT, E]), ALU.is_equal).then_inc(oh, 1)
                    b = at("o_t", k, i)
                    if b is not None:
                        dve.wait_ge(o_t, b + 1)
                        if b:
                            dve.wait_ge(on_t, b)
                        v = MS[:, :].rearrange("p (a c) -> p a c", c=32)
                        link(dve.reciprocal(RC[:, :, :], v[:, :, 16:18]))
                        dve.tensor_tensor(ON[:, :, :].rearrange("p a (s c) -> p a s c", s=2),
                                          v[:, :, 0:16].rearrange("p a (s c) -> p a s c", s=2),
                                          RC[:, :, :, None].broadcast_to([P, 16, 2, HD]), ALU.mult).then_inc(on, 1)
                    b = at("pj", k, i)
                    if b is not None:
                        dve.wait_ge(pj, b + 1)
                        dve.wait_ge(xb_ready, 1)
                        if b:
                            dve.wait_ge(z_ready, b)
                        dve.tensor_tensor(X1[:, TT * b:TT * b + TT, :],
                                          MS[:, 0:T].rearrange("p (t c) -> p t c", t=TT),
                                          XB[:, TT * b:TT * b + TT, :], ALU.add).then_inc(x1, 1)
                        dve.wait_ge(x1, b + 1)
                        link(statistics(X1[:, TT * b:TT * b + TT, :], ST2, MV2))
                        var = MV2[:, :, 1]
                        link(dve.tensor_scalar(SM2[:, 1, :], var, 1e-5, 1e-6, ALU.add, ALU.mult))
                        dve.tensor_scalar(SM2[:, 0, :], var, 1e-5, None, ALU.add)
                        dve.tensor_tensor(SM2[:, 1, :], SM2[:, 1, :], var, ALU.add).then_inc(mv2, 1)
                    b = at("hz", k, i)
                    if b is not None:
                        dve.wait_ge(rstd2, b + 1)
                        if b:
                            dve.wait_ge(hz_t, b)
                        else:
                            dve.wait_ge(xn_t, B)
                        for t in range(TT):
                            last = dve.tensor_scalar(HZ[:, t, :], X1[:, TT * b + t, :], MV2[:, t, 0:1],
                                                     SM2[:, 3, t:t + 1], ALU.subtract, ALU.mult)
                        last.then_inc(hz, 1)
                    b = at("gate", k, i)
                    if b is not None:
                        dve.wait_ge(th, b + 1)
                        if b:
                            dve.wait_ge(wo_ps, b)
                        dve.scalar_tensor_tensor(GT[:, :], TH[:, :], 1.0, ONT[:, :], ALU.add, ALU.mult)                            .then_inc(gated, 1)
                    g = routing(k, i)
                    if g is not None:
                        route(g)
                    g = routing(k, i, 3)
                    if g is not None:
                        indices(g)
                    for g, s in expert_steps(k, i):
                        expert_step(g, s)
            for g, s in expert_steps(SLOTS, 0):
                expert_step(g, s)

        @block.tensor
        def _(pe):
            last_reader = [None]

            def take_misc(reader, count):
                if last_reader[0]:
                    pe.wait_ge(*last_reader[0])
                last_reader[0] = (reader, count)

            def mm(out_, lhsT, rhs, start=True, stop=True, **kw):
                return nc.tensor.matmul(out_, lhsT, rhs, start=start, stop=stop, **kw)

            def transposes(done, src, w=C):
                for t in range(TT):
                    last = nc.tensor.transpose(MS[:, P * t:P * t + P], src[:, t, :], ID[:, :])
                last.then_inc(done, 1)

            def score_beat(e, i):
                u, kt = i // 2, i % 2
                g = BEATS * e + i
                if i == 0:
                    pe.wait_ge(m_rows[e % RING], 32 * ring_uses(e))
                    if e == B:
                        pe.wait_ge(ld["tri"], 16)
                if g >= 2:
                    pe.wait_ge(probs, g - 1)
                qa, ka = QA[e % RING], KA[e % RING]
                for j in range(4):
                    if e < B:
                        last = mm(S[g % 2][:, T * j:T * j + T], ka[:, 4 * u + j, P * kt:P * kt + P], qa[:, 4 * u + j, :])
                    elif kt == 0:
                        if j % 2 == 0:
                            last = mm(S[g % 2][:, T * j:T * j + 2 * T], ka[:, u, 0:P],
                                      qa[:, 4 * u + j:4 * u + j + 2, :])
                    elif j == 0:
                        last = mm(S[g % 2][:, 0:4 * P], ka[:, u, P:T], qa[:, 4 * u:4 * u + 4, P:T])
                last.then_inc(scores, 1)

            def max_bank(e, k):
                heads, q, w = bank_of(e, k)
                g = banks_before(e) + k
                if k == 0:
                    pe.wait_ge(stacked[e % RING], 32 * ring_uses(e))
                    if e == 0:
                        pe.wait_ge(ld["pad"], 32 * RING)
                if g >= 2:
                    pe.wait_ge(mx_taken, g - 1)
                qa, ka, m = QA[e % RING], KA[e % RING], MX[g % 2]
                causal = e >= B
                for n_, h in enumerate(heads):
                    last = mm(m[:, w * n_:w * n_ + w], qa[:, h, P * q:P * q + P], ka[:, h if e < B else h // 4, 0:w],
                              stop=not causal, skip_group_check=causal, start=not causal or n_ == 0)
                if causal:
                    if e == B and k == 0:
                        pe.wait_ge(cst, 8)
                    nh = len(heads)
                    last = mm(m[:, 0:nh * w].rearrange("p (h t) -> p h t", t=w)[:, :, w - P:w], IDB[:, :],
                              TRIB[:, 0:nh, :], start=False, skip_group_check=True)
                last.then_inc(mx_scores, 1)

            def pv_beat(e, i):
                u, kt = i // 2, i % 2
                g = BEATS * e + i
                r, s = u // 2, u % 2
                if i == 0:
                    if e < B:
                        pe.wait_ge(va, e + 1)
                    else:
                        pe.wait_ge(vb, 2 * (e - B + 1))
                    if e:
                        pe.wait_ge(o_sb, e)
                if e < B:
                    pe.wait_ge(probs, g + 1)
                else:
                    pe.wait_ge(masked, g - BEATS * B + 1)
                w, q0 = (T, 0) if e < B or kt == 0 else (P, P)
                for j in range(4):
                    V_ = VA[e % RING][:, kt, 4 * u + j, :] if e < B else VB[e - B][:, kt, u, :]
                    last = mm(O[32 * j:32 * j + 32, T * r + q0:T * r + q0 + w], V_,
                              EX[g % PRING][:, w * j:w * j + w], start=s == 0 and kt == 0, stop=s == 1 and kt == 1,
                              tile_position=(0, 32 * j), skip_group_check=True)
                last.then_inc(pv, 1)

            def rank_tokens(g):
                if g == 0:
                    pe.wait_ge(route_cst, 3)
                    pe.wait_ge(mx_taken, banks_before(NE))
                else:
                    pe.wait_ge(places, g)
                pe.wait_ge(oh, B * (g + 1) // GROUPS)
                rank = MX[0][:, 0:GT_ * E].rearrange("p (t e) -> p t e", e=E)
                mm(rank, BEFB[:, :], OH[:, GT_ * g:GT_ * g + GT_, :], stop=False, skip_group_check=True)
                for t in range(GT_):
                    oh_ = OH[:, GT_ * g + t:GT_ * g + t + 1, :]
                    if t < GT_ - 1:
                        later = GT_ - 1 - t
                        mm(rank[:, t + 1:GT_, :], PARTB[:, :], oh_.broadcast_to([P, later, E]), start=False,
                           skip_group_check=True)
                    last = mm(MX[0][:, GT_ * E:GT_ * E + E], PARTB[:, :], oh_[:, 0, :], start=False,
                              skip_group_check=True)
                last.then_inc(ranks, 1)

            def name_slots(g):
                pe.wait_ge(places, g + 1)
                if g:
                    pe.wait_ge(idx, g)
                for t in range(GT_):
                    last = mm(MX[1][:, 0:3 * ET], INROW[:, t, :], INTILE[:, t, :, :].rearrange("p a j -> p (a j)"),
                              start=t == 0, stop=t == GT_ - 1)
                last.then_inc(ids, 1)

            expert = {}

            def load_expert(g, j):
                if j == 0:
                    pe.wait_ge(experts_of, g + 1)
                expert[ET * g + j] = pe.value_load(EJI[g][0:1, j:j + 1], min_val=0, max_val=E - 1)

            W1F = W1[:, :, :].rearrange("p e f -> p (e f)")
            W2F = W2[:, :, :, :].rearrange("p e k c -> p (e k c)")

            def expert_step(g, s):
                if s == -1:
                    load_expert(g, 0)
                    load_expert(g, 1)
                    if g == 0:
                        pe.wait_ge(ld["w1"], 16 * E)
                        pe.wait_ge(ld["w2"], 16 * E)
                        pe.wait_ge(bias_rows, 16 * NPART)
                        pe.wait_ge(probs, BEATS * NE)
                if has_tile(s + 2) and s >= 0:
                    load_expert(g, s + 2)
                if has_tile(s + 1):
                    n = ET * g + s + 1
                    pe.wait_ge(gathered[s + 1], 16 * (g + 1))
                    if n:
                        pe.wait_ge(hj, n)
                    nc.tensor.transpose(TRJ, rows_of(n, 0, C), ID[:, :]).then_inc(tr_ps, 1)
                if has_tile(s):
                    n = ET * g + s
                    pe.wait_ge(hj, n + 1)
                    if n >= 2:
                        pe.wait_ge(aj, n - 1)
                    mm(U[n % 2], ONEB[0:KROWS, :], BROW[:, bass.ds(expert[n] * BIAS, 2 * HID)], stop=False)
                    mm(U[n % 2], HJ[n % 2][:, :], W1F[:, bass.ds(expert[n] * (2 * HID), 2 * HID)], start=False)\
                        .then_inc(u_ps, 1)
                if has_tile(s - 1):
                    n = ET * g + s - 1
                    pe.wait_ge(aj, n + 1)
                    if n:
                        pe.wait_ge(at_sb, n)
                    for c in range(2):
                        last = nc.tensor.transpose(TA[:, P * c:P * c + P], AJ[n % 2][:, P * c:P * c + P],
                                                   ID[:, :])
                    last.then_inc(ta_ps, 1)
                if has_tile(s - 2):
                    n = ET * g + s - 2
                    pe.wait_ge(at_sb, n + 1)
                    if n:
                        pe.wait_ge(done, n)
                    else:
                        pe.wait_ge(o_sb, NE)
                    mm(Y, ONEB[0:KROWS, :], BROW[:, bass.ds(expert[n] * BIAS + 2 * HID, C)], stop=False)
                    for c in range(2):
                        last = mm(Y, AT[n % 2][:, P * c:P * c + P],
                                  W2F[:, bass.ds(expert[n] * (2 * C) + C * c, C)], start=False, stop=c == 1)
                    last.then_inc(y_ps, 1)

            for k in range(SLOTS):
                for i in HALVES:
                    e, banks = banks_at(k, i)
                    for kk in banks:
                        max_bank(e, kk)
                    if attention_at(k, i):
                        score_beat(*attention_at(k, i))
                    if attention_at(k, i, 2.5):
                        pv_beat(*attention_at(k, i, 2.5))
                    e = maxima_done(k, i, 0.5)
                    if e is not None:
                        take_misc(mts, e + 1)
                        pe.wait_ge(mhl, e + 1)
                        if e == 0:
                            pe.wait_ge(cst, 4)
                        nc.tensor.transpose(MSB[0:2 * TT * H, 0:P], MHL[:, :, :, :].rearrange("p a h t -> p (a h t)"),
                                            IDB[:, :]).then_inc(m_t, 1)
                    b = project_at(k, i, A_XN)
                    if b is not None:
                        if b == 0:
                            pe.wait_ge(ld["id"], 16)
                        take_misc(xnt, b + 1)
                        pe.wait_ge(xn, b + 1)
                        transposes(xn_t, XN)
                    b = project_at(k, i, A_QK)
                    if b is not None:
                        if b == 0:
                            pe.wait_ge(ld["wqk"], 32)
                            pe.wait_ge(ld["ctx"], 16)
                        take_misc(qkf, b + 1)
                        mm(MS[:, 0:T], WQ[:, :], XNT[:, :])
                        mm(MS[:, T:2 * T], WK[:, :], CT[:, T * b:T * b + T]).then_inc(qk_ps, 1)
                    if project_at(k, i, A_V) is not None:
                        if k == 0:
                            pe.wait_ge(ld["wv"], 16)
                        take_misc(va, k + 1)
                        for t in range(TT):
                            last = mm(MS[:, C * t:C * t + C], CT[:, T * k + P * t:T * k + P * t + P], WV[:, :])
                        last.then_inc(v_ps, 1)
                    b = at("hz_t", k, i)
                    if b is not None:
                        take_misc(ht, b + 1)
                        pe.wait_ge(hz, b + 1)
                        transposes(hz_t, HZ)
                    b = at("qkv", k, i)
                    if b is not None:
                        if b == 0:
                            pe.wait_ge(ld["wqkv"], 16)
                        take_misc(qkvs, b + 1)
                        for t in range(TT):
                            last = mm(MS[:, QKV * t:QKV * t + QKV], HT[:, P * t:P * t + P], WQKV[:, :])
                        last.then_inc(qkv_ps, 1)
                    b = at("qn_t", k, i)
                    if b is not None:
                        take_misc(qkf, b + B + 1)
                        pe.wait_ge(qn, b + 1)
                        for t in range(TT):
                            nc.tensor.transpose(MS[:, P * t:P * t + P], QN[:, t, 0:C], ID[:, :])
                            last = nc.tensor.transpose(MS[0:G * HD, T + P * t:T + P * t + P],
                                                       QN[:, t, C:C + G * HD], ID[:, :])
                        last.then_inc(qn_t, 1)
                    b = at("wo", k, i)
                    if b is not None:
                        take_misc(xp, b + 1)
                        pe.wait_ge(gated, b + 1)
                        if b == 0:
                            pe.wait_ge(ld["wo"], 16)
                        for t in range(TT):
                            last = mm(MS[:, C * t:C * t + C], GT[:, P * t:P * t + P], WO[:, :])
                        last.then_inc(wo_ps, 1)
                    b = at("xp_t", k, i)
                    if b is not None:
                        take_misc(xpt, b + 1)
                        pe.wait_ge(xp, b + 1)
                        transposes(xp_t, XP)
                    b = at("router", k, i)
                    if b is not None:
                        if b == 0:
                            pe.wait_ge(ld["wr"], 16)
                        take_misc(oh, b + 1)
                        pe.wait_ge(xpt, b + 1)
                        for t in range(TT):
                            last = mm(MS[:, E * t:E * t + E], XPT[:, P * t:P * t + P], WR[:, :])
                        last.then_inc(lg_ps, 1)
                    b = at("o_t", k, i)
                    if b is not None:
                        take_misc(on, b + 1)
                        pe.wait_ge(o_sb, b + 1)
                        for t in range(TT):
                            for r in range(2):
                                last = nc.tensor.transpose(MS[:, P * (2 * t + r):P * (2 * t + r) + P],
                                                           OS[:, T * r + P * t:T * r + P * t + P], ID[:, :])
                        last.then_inc(o_t, 1)
                    b = at("on_t", k, i)
                    if b is not None:
                        take_misc(ont, b + 1)
                        pe.wait_ge(on, b + 1)
                        for t in range(TT):
                            last = nc.tensor.transpose(MS[:, P * t:P * t + P],
                                                       ON[:, 8 * t:8 * t + 8, :].rearrange("p a c -> p (a c)"), ID[:, :])
                        last.then_inc(on_t, 1)
                    b = at("pj", k, i)
                    if b is not None:
                        if b == 0:
                            pe.wait_ge(ld["wp"], 16)
                        take_misc(x1, b + 1)
                        pe.wait_ge(ont, b + 1)
                        for t in range(TT):
                            last = mm(MS[:, C * t:C * t + C], ONT[:, P * t:P * t + P], WP[:, :])
                        last.then_inc(pj, 1)
                    b = at("gate", k, i)
                    if b is not None:
                        if b == 0:
                            pe.wait_ge(ld["wg"], 16)
                        take_misc(th, b + 1)
                        pe.wait_ge(ont, b + 5)
                        mm(MS[:, 0:T], WG[:, :], ONT[:, :]).then_inc(gate_ps, 1)
                    g = routing(k, i)
                    if g is not None:
                        rank_tokens(g)
                    g = routing(k, i, 2)
                    if g is not None:
                        name_slots(g)
                    for g, s in expert_steps(k, i):
                        expert_step(g, s)
            for g, s in expert_steps(SLOTS, 0):
                expert_step(g, s)


_INS = ("x", "ctxT", "cols", "rows", "wq", "wk", "wv", "wp", "wqkv", "wg", "wo", "wr", "w1", "w2", "bias",
        "ident", "tri", "rope", "revs", "numbers", "ones_row", "zero_row")


def rope_table():
    inv = (1.0 / 10000.0 ** (np.arange(0, HD, 2, dtype=np.float32) / HD)).astype(np.float32)
    f = np.arange(T, dtype=np.float32)[:, None] * inv[None, :]
    c, s = np.cos(f).astype(np.float32), np.sin(f).astype(np.float32)
    return np.stack([np.concatenate([c, c], 1), np.concatenate([-s, s], 1)], 1)


def layout(x, ctx_768, L0_xattn_q_w, L0_xattn_q_b, L0_xattn_kv_w, L0_xattn_kv_b, L0_xattn_proj_w,
           L0_xattn_proj_b, L0_ffn_ln1_w, L0_ffn_ln2_w, L0_ffn_Wq, L0_ffn_bq, L0_ffn_Wk, L0_ffn_bk,
           L0_ffn_Wv, L0_ffn_bv, L0_ffn_qn_w, L0_ffn_kn_w, L0_ffn_Wg, L0_ffn_bg, L0_ffn_Wo, L0_ffn_bo,
           L0_ffn_Wr, L0_ffn_br, L0_ffn_W1, L0_ffn_b1, L0_ffn_W2, L0_ffn_b2):
    f = np.float32
    def by_quadrant(w):
        return np.ascontiguousarray(np.asarray(w).reshape(2, 2, 4, HD, C).transpose(0, 2, 1, 3, 4).reshape(C, C))

    def by_column(w):
        w = np.asarray(w)
        return w.reshape(*w.shape[:-1], -1, HD).swapaxes(-1, -2)

    def flat(w):
        return w.reshape(*w.shape[:-2], -1)

    def joint(q, k, v):
        return np.concatenate([flat(np.concatenate([by_column(q), by_column(k)], -1)), v], -1)

    cols = np.zeros((P, NCOL), f)
    cols[:, C_QB] = flat(by_column(L0_xattn_q_b))
    cols[:, C_KB] = flat(by_column(L0_xattn_kv_b[:C]))
    cols[:, C_LN1] = L0_ffn_ln1_w
    cols[:, C_LN2] = L0_ffn_ln2_w
    cols[:, C_QN] = np.repeat(L0_ffn_qn_w, H)
    cols[:G * HD, C_KN] = np.repeat(L0_ffn_kn_w, G)
    cols[:, C_BG] = np.tile(L0_ffn_bg, H)
    cols[:, C_P] = np.arange(P)
    rows = np.concatenate([L0_xattn_kv_b[C:], L0_xattn_proj_b, joint(L0_ffn_bq, L0_ffn_bk, L0_ffn_bv), L0_ffn_bo,
                           L0_ffn_br])[None, :].astype(f)
    wg = np.zeros((C, C), f)
    for h in range(H):
        wg[HD * h:HD * h + HD, HD * h:HD * h + HD] = L0_ffn_Wg
    ii = np.arange(P)
    d = {
        "x": np.asarray(x).reshape(NT, P, C).transpose(1, 0, 2),
        "ctxT": np.asarray(ctx_768).reshape(B * T, CD).T,
        "cols": cols, "rows": rows,
        "wq": flat(by_column(L0_xattn_q_w)), "wk": flat(by_column(L0_xattn_kv_w[:, :C])), "wv": L0_xattn_kv_w[:, C:],
        "wp": by_quadrant(L0_xattn_proj_w),
        "wqkv": joint(L0_ffn_Wq, L0_ffn_Wk, L0_ffn_Wv),
        "wg": wg, "wo": by_quadrant(L0_ffn_Wo), "wr": L0_ffn_Wr,
        "w1": np.asarray(L0_ffn_W1).transpose(1, 0, 2),
        "w2": np.asarray(L0_ffn_W2).reshape(E, 2, P, C).transpose(2, 0, 1, 3),
        "bias": np.concatenate([L0_ffn_b1, L0_ffn_b2], 1),
        "ident": np.eye(P, dtype=f),
        "tri": np.where(ii[None, :] > ii[:, None], -1e30, 0.0).astype(f),
        "rope": rope_table().reshape(TT, P, 2, HD).transpose(1, 0, 2, 3),
        "revs": np.arange(E, 0, -1, dtype=f)[None, :],
        "numbers": np.concatenate([ii, ii / P, (ii[None, :E] < ii[:E, None]).ravel()]).astype(f)[None, :],
        "ones_row": np.full((1, H * T // 2), 0x3F803F80, np.uint32).view(f),
        "zero_row": np.zeros((1, H * T // 2), f),
    }
    return {k: np.ascontiguousarray(v) for k, v in d.items()}


def program(nc, shapes):
    aps = [nc.dram_tensor(f"in_{k}", s, d, kind="ExternalInput").ap() for k, s, d in shapes]
    bf16 = mybir.dt.bfloat16
    q_rows = nc.dram_tensor("q_rows", [2 * B, NPART, NPART, H * HD, T], bf16, kind="Internal").ap()
    k_rows = nc.dram_tensor("k_rows", [B, NPART, NPART, H * HD, T], bf16, kind="Internal").ap()
    k2_rows = nc.dram_tensor("k2_rows", [B, NPART, NPART, G * HD, T], bf16, kind="Internal").ap()
    h_rows = [nc.dram_tensor(f"h_rows{g}", [P * GT_, 2 * C], mybir.dt.float32, kind="Internal").ap()
              for g in range(GROUPS)]
    out = nc.dram_tensor("out_0", [B * T, C], mybir.dt.float32, kind="ExternalOutput").ap()
    tuned(nc, *aps, q_rows, k_rows, k2_rows, h_rows, out)


def kernel(**inputs):
    import concourse.bacc as bacc
    from concourse.bass_utils import run_bass_kernel_spmd
    arrays = layout(**{k: np.asarray(v) for k, v in inputs.items()})
    nc = bacc.Bacc("TRN2", target_bir_lowering=False, num_devices=1)
    program(nc, [(k, arrays[k].shape, mybir.dt.from_np(arrays[k].dtype)) for k in _INS])
    r = run_bass_kernel_spmd(nc, [{f"in_{k}": arrays[k] for k in _INS}], core_ids=[0])
    return r.results[0]["out_0"].reshape(B, T, C)
```

```python
import numpy as np
import concourse.bass as bass
from concourse import mybir
from contextlib import ExitStack

B, T, C = 4, 256, 128
CD = 96
H, HD = 16, 8
G = 4
E, HID = 8, 256
P = 128
TT = T // P
NT = B * TT
QKV = C + 2 * G * HD
NPART = 3
ROWS = NPART * NPART * HD
KROWS = 96
RING = 3
WRING = 3
PRING = 4
BEATS = H // 4 * TT
SCALE = HD ** -0.5
NEWTON = 3
ET = NT + E - 1
SKIP = 1 << 20
W1_B = 2 * HID
W1C = W1_B + 2 * HID // P
C_QB, C_KB, C_LN1, C_LN2, C_QN, C_KN, C_BG, C_P = 0, 1, 2, 3, 4, 5, 6, 7
NCOL = C_P + 1
N_I, N_IP, N_BEF = 0, P, 2 * P
NNUM = N_BEF + E * E
R_VB, R_PB, R_BQKV, R_BO, R_BR = 0, C, 2 * C, 2 * C + QKV, 3 * C + QKV
NROW = R_BR + E


def transformer(nc, x, ctxT, cols, rows, wq, wk, wv, wp, wqkv, wg, wo, wr, w1, w2, b2, ident, tri, rope,
          revs, numbers, ones_row, zero_row, q_rows, k_rows, k2_rows, h_rows, out):
    i32 = mybir.dt.int32
    fp32, bf16 = mybir.dt.float32, mybir.dt.bfloat16
    ALU, ACT, AX = mybir.AluOpType, mybir.ActivationFunctionType, mybir.AxisListType
    ctx = ExitStack()
    with ctx:
        def sb(name, shape, dt=fp32):
            return ctx.enter_context(nc.sbuf_tensor(name, shape, dt))

        def ps(name, cols):
            return ctx.enter_context(nc.psum_tensor(name, [P, cols], fp32))

        def sem(name):
            return ctx.enter_context(nc.semaphore(name))

        X = sb("X", [P, NT, C])
        CT = sb("CT", [CD, B * T])
        COL = sb("COL", [P, NCOL])
        ROW = sb("ROW", [P, NROW])
        WQ, WK, WV = sb("WQ", [C, C]), sb("WK", [CD, C]), sb("WV", [CD, C])
        WP, WQKV = sb("WP", [C, C]), sb("WQKV", [C, QKV])
        WG, WO, WR = sb("WG", [C, C]), sb("WO", [C, C]), sb("WR", [C, E])
        W1 = sb("W1", [C, E, W1C])
        W2 = sb("W2", [P, E, 2, C])
        BF = sb("BF", [E, C])
        BPT = sb("BPT", [E, NPART, C], bf16)
        BROW = sb("BROW", [KROWS, E * C], bf16)
        ID = sb("ID", [P, P])
        IDB = sb("IDB", [P, P], bf16)
        TRI = sb("TRI", [P, P])
        TRIB = sb("TRIB", [P, 4, P], bf16)
        ROPE = sb("ROPE", [P, TT, 2, HD])
        REV = sb("REV", [P, E])
        NEGHALF = sb("NEGHALF", [P, 64])
        QBS = sb("QBS", [P, 1])
        QNS = sb("QNS", [P, 1])
        BGH = sb("BGH", [P, 1])
        NUM = sb("NUM", [P, NNUM])
        BEFB = sb("BEFB", [P, P], bf16)
        PARTB = sb("PARTB", [P, P], bf16)
        ONEB = sb("ONEB", [P, P], bf16)
        XB = sb("XB", [P, NT, C])
        X1 = sb("X1", [P, NT, C])
        Z = sb("Z", [P, TT, C])
        ZB = sb("ZB", [P, NT, C])
        HR = sb("HR", [P, NT, 2, C])
        MV1 = sb("MV1", [P, TT, 2])
        ST = sb("ST", [P, TT, 6])
        SM1 = sb("SM1", [P, 8, TT])
        XN = sb("XN", [P, TT, C])
        XNT = sb("XNT", [C, T])
        QKF = sb("QKF", [P, 2, T])
        R1 = sb("R1", [P, 2, T])
        PT = sb("PT", [P, NPART, 2, T], bf16)
        QA = [sb(f"QA{i}", [KROWS, H, T], bf16) for i in range(RING)]
        KA = [sb(f"KA{i}", [KROWS, H, T], bf16) for i in range(RING)]
        VA = [sb(f"VA{i}", [P, TT, H, 32]) for i in range(RING)]
        VB = [sb(f"VB{i}", [P, TT, G, 32]) for i in range(B)]
        NEGM = sb("NEGM", [P, TT, H])
        MHL = sb("MHL", [P, 2, H, TT], bf16)
        MTS = sb("MTS", [2 * TT * H, P], bf16)
        EX = [sb(f"EX{i}", [P, 4 * T]) for i in range(PRING)]
        OS = sb("OS", [P, 2 * T])
        RC = sb("RC", [P, 16, 2])
        ON = sb("ON", [P, 16, 16])
        ONT = sb("ONT", [C, T])
        ST2 = sb("ST2", [P, TT, 6])
        MV2 = sb("MV2", [P, TT, 2])
        SM2 = sb("SM2", [P, 8, TT])
        HZ = XN
        HT = sb("HT", [C, T])
        QKVS = sb("QKVS", [P, TT, QKV])
        NH2 = H + G
        SQ = sb("SQ", [P, TT, NH2 * HD])
        SSQ = sb("SSQ", [P, TT * NH2])
        RQ = sb("RQ", [P, TT * NH2])
        RT = sb("RT", [P, TT * NH2])
        ROT = sb("ROT", [P, TT, HD, NH2])
        ROTS = sb("ROTS", [P, TT, HD, NH2])
        QN = sb("QN", [P, TT, NH2 * HD])
        TH = sb("TH", [C, T])
        GT = sb("GT", [C, T])
        XP = sb("XP", [P, TT, C])
        SS3 = sb("SS3", [P, 4, TT])
        XPT = sb("XPT", [C, T])
        LG = sb("LG", [P, TT, E])
        MXL = sb("MXL", [P, 2, TT])
        EQ = sb("EQ", [P, TT, E])
        OH = sb("OH", [P, NT, E], bf16)
        CNT = sb("CNT", [P, E])
        OVER = sb("OVER", [P, E, NT])
        TILES = sb("TILES", [P, E])
        BEFT = sb("BEFT", [P, E, E])
        FIRST = sb("FIRST", [P, E])
        AFTER = sb("AFTER", [P, ET, E - 1])
        EJ = sb("EJ", [P, ET])
        EJI = sb("EJI", [1, ET], i32)
        PICK = sb("PICK", [P, 2, NT, E])
        RANK = sb("RANK", [P, 2, NT])
        PAST = sb("PAST", [P, NT, NT - 1])
        SLOT = sb("SLOT", [P, 2, NT])
        INROW = sb("INROW", [P, NT, P], bf16)
        INTILE = sb("INTILE", [P, NT, 3, ET], bf16)
        IDS = sb("IDS", [P, 3, ET])
        IDF = sb("IDF", [P, 2, ET])
        IDX = sb("IDX", [P, 2, ET], mybir.dt.uint32)
        GR = sb("GR", [P, NT, 2 * C])
        HJ = [sb(f"HJ{i}", [C, P]) for i in range(2)]
        WJ = [sb(f"WJ{i}", [C, W1C]) for i in range(WRING)]
        SJ = [sb(f"SJ{i}", [P, HID]) for i in range(2)]
        AJ = [sb(f"AJ{i}", [P, HID]) for i in range(2)]
        WARM = sb("WARM", [P, 1])

        S = [ps(f"S{i}", 1024) for i in range(2)]
        MXX = ps("MXX", 1024)
        MX = [MXX[:, 512 * i:512 * i + 512] for i in range(2)]
        O = ps("O", 512)
        MS = ps("MS", 512)
        MSB = MS[:, :].bitcast(bf16)
        U = [S[0][:, 512 * i:512 * i + 512] for i in range(2)]
        TRJ = S[1][:, 0:P]
        Y = O[:, 0:C]

        ld = {k: sem(f"ld_{k}") for k in ("x0", "x1", "ctx", "cols", "rows", "id", "wqk", "wv", "wp", "wqkv",
                                          "tri", "rope", "wg", "wo", "wr", "w1", "w2", "b2", "rev", "num", "pad")}
        cst = sem("constants_ready")
        route_cst = sem("route_cst")
        bias_rows = sem("bias_rows")
        xb_ready = sem("xb_ready")
        va_zero = sem("va_zero")
        dve_step = sem("dve_step")
        pool_step = sem("pool_step")
        scores = sem("scores")
        probs = sem("probs")
        masked = sem("masked")
        pv = sem("pv")
        mx_scores = sem("mx_scores")
        mx_taken = sem("mx_taken")
        mhl = sem("mhl")
        m_t = sem("m_t")
        mts = sem("mts")
        m_rows = [sem(f"m_rows{i}") for i in range(RING)]
        mv1 = sem("mv1")
        rstd1 = sem("rstd1")
        xn = sem("xn")
        xn_t = sem("xn_t")
        xnt = sem("xnt")
        qk_ps = sem("qk_ps")
        v_ps = sem("v_ps")
        va = sem("va")
        vb = sem("vb")
        qkf = sem("qkf")
        part1, rest1, part2, part3 = sem("part1"), sem("rest1"), sem("part2"), sem("part3")
        q_out, k_out = sem("q_out"), sem("k_out")
        stacked = [sem(f"stacked{i}") for i in range(RING)]
        o_sb = sem("o_sb")
        o_t = sem("o_t")
        on = sem("on")
        on_t = sem("on_t")
        ont = sem("ont")
        pj = sem("pj")
        x1 = sem("x1")
        mv2 = sem("mv2")
        rstd2 = sem("rstd2")
        hz = sem("hz")
        hz_t = sem("hz_t")
        ht = sem("ht")
        qkv_ps = sem("qkv_ps")
        qkvs = sem("qkvs")
        sq = sem("sq")
        rots = sem("rots")
        ssq = sem("ssq")
        qn = sem("qn")
        qn_t = sem("qn_t")
        gate_ps = sem("gate_ps")
        th = sem("th")
        gated = sem("gated")
        wo_ps = sem("wo_ps")
        xp = sem("xp")
        ss3 = sem("ss3")
        rstd3 = sem("rstd3")
        h2 = sem("h2")
        xp_t = sem("xp_t")
        xpt = sem("xpt")
        lg_ps = sem("lg_ps")
        oh = sem("oh")
        z_ready = sem("z_ready")
        rr = sem("rr")
        h_stored = [sem(f"h_stored{b}") for b in range(B)]
        ranks = sem("ranks")
        experts_of = sem("experts_of")
        places = sem("places")
        ids = sem("ids")
        idx = sem("idx")
        idx_out = sem("idx_out")
        gathered = [sem(f"gathered{j}") for j in range(ET)]
        tr_ps = sem("tr_ps")
        hj = sem("hj")
        wj = sem("wj")
        u_ps = sem("u_ps")
        sj = sem("sj")
        aj = sem("aj")
        y_ps = sem("y_ps")
        done = sem("done")
        scattered = sem("scattered")
        block = ctx.enter_context(nc.Block())

        NE = 2 * B
        SLOTS = NE + 6
        HALVES = [i / 2 for i in range(2 * BEATS)]
        PAUSE = 4

        def has(i, n):
            return 0 <= i < n

        AT1 = {"pj": 7, "hz": 8, "hz_t": 9, "qkv": 10, "squares": 11, "newton1": 11,
               "newton2": 11.5, "newton3": 12, "qn_t": 13.5, "split2": 14.5}
        AT2 = {"gate": 7.5, "wo": 9, "xp_t": 10, "h2": 11, "router": 11.5}
        BOTH = {"o_sb": 4.5, "o_t": 5, "on_t": 6}

        def start(e):
            return BEATS * e + (PAUSE if e >= B else 0)

        def at(step, k, i):
            for table, first, n in ((AT1, 0, B), (AT2, B, B), (BOTH, 0, NE)):
                if step in table:
                    for b in range(n):
                        if BEATS * k + i == start(b + first) + 3 * BEATS + table[step]:
                            return b
                    return None

        ROUTE = start(NE - 1) + 3 * BEATS + int(AT2["router"]) + 1
        START = ROUTE + 4
        GATHERS = ROUTE + 3
        LAST = SLOTS * BEATS

        LAG = 3

        def attention_at(k, i, behind=0):
            for e in range(NE):
                beat = BEATS * k + i - behind - start(e) - 2 * BEATS - LAG
                if beat in range(BEATS):
                    return e, int(beat)
            return None

        A_STATS, A_XN, A_QK, A_SPLIT, A_V = 0, 1, 2, 3, 7.5

        def project_at(k, i, step):
            if step == A_V:
                return k if i == A_V and has(k, B) else None
            for b in range(B):
                if BEATS * k + i == (2 * b if b < 2 else BEATS * (b - 1)) + step:
                    return b
            return None

        def banks_at(k, i):
            for e in range(NE):
                beat = BEATS * k + i - start(e) - BEATS
                if 0 <= beat < BEATS:
                    return e, list(range(int(nbanks(e) * beat / BEATS), int(nbanks(e) * (beat + 0.5) / BEATS)))
            return None, []

        def maxima_done(k, i, lag=0):
            for e in range(NE):
                if BEATS * k + i == start(e) + 2 * BEATS + lag:
                    return e
            return None

        def routing(k, i, lag=0):
            return BEATS * k + i == ROUTE + lag

        def expert_steps(k, i):
            now = BEATS * k + i
            return [s for s in range(-1, ET + 2) if START + s == now or now == LAST <= START + s]

        def rows_of(n, lo, hi):
            if n < NT:
                return GR[:, n, lo:hi]
            j = n - NT
            return EX[j // 4][:, 2 * C * (j % 4) + lo:2 * C * (j % 4) + hi]

        def has_tile(j):
            return 0 <= j < ET

        def nbanks(e):
            return 16 if e < B else 12

        def bank_of(e, k):
            if e < B:
                u, q, half = k // 4, k // 2 % 2, k % 2
                return range(4 * u + 2 * half, 4 * u + 2 * half + 2), q, T
            u, w = k // 3, k % 3
            if w == 0:
                return range(4 * u, 4 * u + 4), 0, P
            return range(4 * u + 2 * (w - 1), 4 * u + 2 * w), 1, T

        def banks_before(e):
            return sum(nbanks(i) for i in range(e))

        def ring_uses(e):
            return e // RING + 1

        @block.sync
        def _(sp):
            sp.dma_start(X[:, 0:TT, :], x[:, 0:TT, :]).then_inc(ld["x0"], 16)
            sp.dma_start(CT[:, :], ctxT).then_inc(ld["ctx"], 16)
            sp.dma_start(COL[:, :], cols).then_inc(ld["cols"], 16)
            sp.dma_start(WK[:, :], wk).then_inc(ld["wqk"], 16)
            sp.dma_start(WV[:, :], wv).then_inc(ld["wv"], 16)
            sp.dma_start(X[:, TT:NT, :], x[:, TT:NT, :]).then_inc(ld["x1"], 16)
            for i in range(RING):
                sp.dma_start(KA[i][ROWS:KROWS, :, :].rearrange("p h t -> p (h t)").bitcast(fp32),
                             ones_row.broadcast_to([KROWS - ROWS, H * T // 2])).then_inc(ld["pad"], 16)
                sp.dma_start(QA[i][ROWS:KROWS, :, :].rearrange("p h t -> p (h t)").bitcast(fp32),
                             zero_row.broadcast_to([KROWS - ROWS, H * T // 2])).then_inc(ld["pad"], 16)

            def parts_out(e):
                nk = H if e < B else G
                k_e = k_rows[e] if e < B else k2_rows[e - B]
                for c, ready in enumerate((part1, part2, part3)):
                    sp.wait_ge(ready, e + 1)
                    sp.dma_start(q_rows[e, c].rearrange("j p t -> p j t"),
                                 PT[:, c, 0, None, :].broadcast_to([P, NPART, T])).then_inc(q_out, 16)
                    sp.dma_start(k_e[:, c].rearrange("i p t -> p i t"),
                                 PT[0:nk * HD, c, 1, None, :].broadcast_to([nk * HD, NPART, T])).then_inc(k_out, 16)

            def stacks_in(e):
                nk = H if e < B else G
                k_e = k_rows[e] if e < B else k2_rows[e - B]
                if e >= RING:
                    sp.wait_ge(scores, BEATS * (e - RING + 1))
                sp.wait_ge(q_out, 16 * NPART * (e + 1))
                sp.dma_start(QA[e % RING][0:ROWS, :, :].rearrange("p h t -> p (h t)"),
                             q_rows[e].rearrange("i j (d h) t -> (i j d) (h t)", h=H)).then_inc(stacked[e % RING], 16)
                sp.wait_ge(k_out, 16 * NPART * (e + 1))
                sp.dma_start(KA[e % RING][0:ROWS, 0:nk, :].rearrange("p h t -> p (h t)"),
                             k_e.rearrange("i j (d h) t -> (i j d) (h t)", h=nk)).then_inc(stacked[e % RING], 16)

            sp.dma_start(TRI[:, :], tri).then_inc(ld["tri"], 16)
            sp.dma_start(WP[:, :], wp).then_inc(ld["wp"], 16)
            sp.dma_start(WQKV[:, :], wqkv).then_inc(ld["wqkv"], 16)
            sp.dma_start(ROPE[:, :, :, :], rope).then_inc(ld["rope"], 16)
            def expert_weights(e):
                sp.dma_start(W1[:, e, :], w1[:, e, :]).then_inc(ld["w1"], 16)
                sp.dma_start(W2[:, e, :, :], w2[:, e, :, :]).then_inc(ld["w2"], 16)

            def maxima_in(e):
                sp.wait_ge(mts, e + 1)
                for part in range(2):
                    r = ROWS + part
                    sp.dma_start(QA[e % RING][r:r + 1, :, :].rearrange("p h (q t) -> p (h q) t", q=TT),
                                 MTS[part * TT * H:(part + 1) * TT * H, :]).then_inc(m_rows[e % RING], 16)

            parts_out(0)
            stacks_in(0)
            sp.dma_start(WG[:, :], wg).then_inc(ld["wg"], 16)
            sp.dma_start(WO[:, :], wo).then_inc(ld["wo"], 16)
            sp.dma_start(WR[:, :], wr).then_inc(ld["wr"], 16)
            sp.dma_start(REV[:, :], revs.broadcast_to([P, E])).then_inc(ld["rev"], 16)
            sp.dma_start(BF[:, :], b2).then_inc(ld["b2"], 16)
            sp.dma_start(NUM[:, :], numbers.broadcast_to([P, NNUM])).then_inc(ld["num"], 16)
            parts_out(1)
            stacks_in(1)
            parts_out(2)
            stacks_in(2)
            maxima_in(0)
            expert_weights(0)
            parts_out(3)
            maxima_in(1)
            expert_weights(1)
            stacks_in(3)
            maxima_in(2)
            expert_weights(2)
            parts_out(4)
            maxima_in(3)
            stacks_in(4)
            expert_weights(3)
            for e in range(5, NE):
                parts_out(e)
                stacks_in(e)
                maxima_in(e - 1)
                expert_weights(e - 1)
            maxima_in(NE - 1)
            expert_weights(NE - 1)
            for b in range(B):
                sp.wait_ge(h2, b + 1)
                sp.wait_ge(rr, b + 1)
                sp.dma_start(h_rows[T * b:T * b + T].rearrange("(t p) c -> p t c", p=P),
                             HR[:, TT * b:TT * b + TT, :, :].rearrange("p t a c -> p t (a c)"))\
                    .then_inc(h_stored[b], 16)
            sp.wait_ge(scattered, 16 * ET)

        @block.gpsimd
        def _(pool):
            n = [0]

            def link(ins):
                n[0] += 1
                ins.then_inc(pool_step, 1)
                pool.wait_ge(pool_step, n[0])

            def rsqrt(out_, in_, w, mult, eps):
                link(pool.tensor_scalar(out_, in_, mult, eps, ALU.mult, ALU.add))
                return pool.tensor_tensor(out_, out_, NEGHALF[:, 0:w], ALU.pow)

            link(pool.memset(NEGHALF[:, :], -0.5))

            def query_constants():
                pool.wait_ge(ld["cols"], 16)
                pool.tensor_scalar(QBS[:, :], COL[:, C_QB:C_QB + 1], SCALE, None, ALU.mult).then_inc(cst, 1)
                pool.tensor_scalar(QNS[:, :], COL[:, C_QN:C_QN + 1], SCALE, None, ALU.mult).then_inc(cst, 1)
                pool.tensor_scalar(BGH[:, :], COL[:, C_BG:C_BG + 1], 0.5, None, ALU.mult).then_inc(cst, 1)

            def ln1_rstd(b):
                pool.wait_ge(mv1, b + 1)
                if b:
                    pool.wait_ge(xn, b)
                rsqrt_last = rsqrt(SM1[:, 0, :], MV1[:, :, 1], TT, 1.0, 1e-5)
                rsqrt_last.then_inc(rstd1, 1)

            def split_rest(e):
                pool.wait_ge(part1, e + 1)
                pool.tensor_tensor(R1[:, :, :], QKF[:, :, :], PT[:, 0, :, :], ALU.subtract).then_inc(rest1, 1)

            def split_last(e):
                pool.wait_ge(rest1, e + 1)
                pool.wait_ge(part2, e + 1)
                pool.tensor_tensor(PT[:, 2, :, :], R1[:, :, :], PT[:, 1, :, :], ALU.subtract).then_inc(part3, 1)

            ln1_rstd(0)
            query_constants()
            ln1_rstd(1)
            pool.wait_ge(ld["id"], 16)
            pool.tensor_copy(IDB[:, :], ID[:, :]).then_inc(cst, 1)

            def zero_values(i):
                for V_, nh in (((VA[i], H),) if i < RING else ()) + ((VB[i], G),):
                    link(pool.memset(V_[:, :, :, :], 0.0))
                    v = V_[:, :, :, :].rearrange("p k (r s j) c -> p (k r) s j c", s=2, j=nh // 4)
                    for s in range(2):
                        pool.memset(v[:, :, s, :, 16 + s:17 + s], 1.0).then_inc(va_zero, 1)

            def causal_masks():
                pool.wait_ge(ld["tri"], 16)
                for j in range(4):
                    pool.tensor_copy(TRIB[:, j, :], TRI[:, :]).then_inc(cst, 1)

            def projected_bias():
                pool.wait_ge(ld["x0"], 16)
                pool.wait_ge(ld["x1"], 16)
                pool.wait_ge(ld["rows"], 16)
                pool.tensor_tensor(XB[:, :, :], X[:, :, :],
                                   ROW[:, None, R_PB:R_PB + C].broadcast_to([P, NT, C]), ALU.add).then_inc(xb_ready, 1)

            def routing_constants():
                pool.tensor_scalar(BEFB[:, :], TRI[:, :], -1.0, 1.0 / P, ALU.mult, ALU.min).then_inc(route_cst, 1)
                pool.memset(ONEB[:, :], 1.0).then_inc(route_cst, 1)
                pool.memset(PARTB[:, :], 1.0 / P).then_inc(route_cst, 1)

            def bias_part(step):
                if step == 0:
                    link(pool.memset(BROW[:, :], 0.0))
                elif step == 1:
                    pool.wait_ge(ld["b2"], 16)
                elif step % 2 == 0:
                    link(pool.tensor_copy(BPT[:, step // 2 - 1, :], BF[:, :]))
                elif step < 2 * NPART:
                    link(pool.tensor_tensor(BF[:, :], BF[:, :], BPT[:, step // 2 - 1, :], ALU.subtract))
                else:
                    for c in range(NPART):
                        pool.dma_start(BROW[c:c + 1, :], BPT[:, c, :]).then_inc(bias_rows, 16)

            def ln2_rstd(b):
                pool.wait_ge(mv2, b + 1)
                if b:
                    pool.wait_ge(hz, b)
                pool.tensor_tensor(SM2[:, 2:4, :], SM2[:, 0:2, :],
                                   NEGHALF[:, 0:2 * TT].rearrange("p (a t) -> p a t", a=2), ALU.pow).then_inc(rstd2, 1)
                pool.wait_ge(rstd2, b + 1)
                if b:
                    pool.wait_ge(z_ready, b)
                for t in range(TT):
                    link(pool.tensor_scalar(Z[:, t, :], X1[:, TT * b + t, :],
                                            MV2[:, t, 0:1], SM2[:, 2, t:t + 1], ALU.subtract, ALU.mult))
                pool.tensor_tensor(ZB[:, TT * b:TT * b + TT, :], Z[:, :, :],
                                   ROW[:, None, R_BO:R_BO + C].broadcast_to([P, TT, C]), ALU.add)\
                    .then_inc(z_ready, 1)

            def head_squares(b):
                pool.wait_ge(qkvs, b + 1)
                if b:
                    pool.wait_ge(ssq, b)
                pool.tensor_tensor(SQ[:, :, :], QKVS[:, :, 0:NH2 * HD], QKVS[:, :, 0:NH2 * HD], ALU.mult)\
                    .then_inc(sq, 1)
                pool.wait_ge(ld["rope"], 16)
                if b:
                    pool.wait_ge(qn, b)
                hh = HD // 2
                qk = QKVS[:, :, 0:NH2 * HD].rearrange("p t (c h) -> p t c h", c=HD)
                pool.tensor_tensor(ROTS[:, :, 0:hh, :], qk[:, :, hh:HD, :],
                                   ROPE[:, :, 1, 0:hh, None].broadcast_to([P, TT, hh, NH2]), ALU.mult)
                pool.tensor_tensor(ROTS[:, :, hh:HD, :], qk[:, :, 0:hh, :],
                                   ROPE[:, :, 1, hh:HD, None].broadcast_to([P, TT, hh, NH2]), ALU.mult)\
                    .then_inc(rots, 1)
                for s in range(2):
                    pool.tensor_copy(
                        VB[b][:, :, :, 8 * s:8 * s + 8].rearrange("p k (r s) c -> p k r s c", s=2)[:, :, :, s, :],
                        QKVS[:, :, NH2 * HD:QKV].rearrange("p k (r s c) -> p k r s c", s=2, c=HD)[:, :, :, s, :])\
                        .then_inc(vb, 1)

            def rms3(b):
                pool.wait_ge(ss3, b + 1)
                if b:
                    pool.wait_ge(h2, b)
                    pool.wait_ge(oh, b)
                rsqrt(SS3[:, 1, :], SS3[:, 0, :], TT, 1.0 / C, 1e-6).then_inc(rstd3, 1)

            def causal(e, i):
                u, kt = i // 2, i % 2
                w = T if kt == 0 else P
                g = BEATS * e + i
                pool.wait_ge(probs, g + 1)
                v = EX[g % PRING][:, 0:4 * w].rearrange("p (j t) -> p j t", j=4)[:, :, 0:P]
                pool.affine_select(out=v, in_=v, pattern=[[0, 4], [1, P]], compare_op=ALU.is_ge, fill=0.0,
                                   base=0, channel_multiplier=-1).then_inc(masked, 1)

            for k in range(SLOTS):
                for i in HALVES:
                    b = project_at(k, i, A_STATS)
                    if b is not None and b > 1:
                        ln1_rstd(b)
                    now = attention_at(k, i)
                    if now and now[0] >= B:
                        causal(*now)
                    b = at("qkv", k, i)
                    if b is not None:
                        head_squares(b)
                    b = project_at(k, i, A_QK)
                    if b is not None and b >= 2:
                        split_rest(b)
                    b = project_at(k, i, A_SPLIT)
                    if b is not None and b >= 2:
                        split_last(b)
                    b = at("qn_t", k, i)
                    if b is not None:
                        split_rest(b + B)
                    b = at("split2", k, i)
                    if b is not None:
                        split_last(b + B)
                    b = at("pj", k, i)
                    if b is not None:
                        ln2_rstd(b)
                    b = at("wo", k, i)
                    if b is not None:
                        pool.wait_ge(xp, b + 1)
                        pool.tensor_tensor(HR[:, TT * b:TT * b + TT, 1, :], X1[:, TT * b:TT * b + TT, :],
                                           XP[:, :, :], ALU.add).then_inc(rr, 1)
                        rms3(b)
                    if (k, i) == (0, 5):
                        zero_values(0)
                    if (k, i) == (1, 4.5):
                        zero_values(1)
                    if (k, i) == (1, 6):
                        zero_values(2)
                    if (k, i) == (2, 1):
                        projected_bias()
                    if (k, i) == (2, 2):
                        causal_masks()
                    if (k, i) == (2, 3):
                        routing_constants()
                    if (k, i) == (2, 4.5):
                        zero_values(3)
                    if k == 3 and i in range(BEATS):
                        bias_part(int(i))
                    if BEATS * k + i == GATHERS:
                        pool.wait_ge(idx, 1)
                        pool.wait_ge(pv, BEATS * NE)
                        for b in range(B):
                            pool.wait_ge(h_stored[b], 16)
                        for j in range(ET):
                            pool.indirect_dma_start(rows_of(j, 0, 2 * C), None, h_rows,
                                                    bass.IndirectOffsetOnAxis(IDX[:, 0, j:j + 1], 0))\
                                .then_inc(gathered[j], 16)
            pool.wait_ge(idx_out, 1)
            for j in range(ET):
                pool.wait_ge(done, j + 1)
                pool.indirect_dma_start(out, bass.IndirectOffsetOnAxis(IDX[:, 1, j:j + 1], 0),
                                        rows_of(j, C, 2 * C), None, bounds_check=B * T - 1, oob_is_err=False)\
                    .then_inc(scattered, 16)

        @block.scalar
        def _(act):
            act.dma_start(ID[:, :], ident).then_inc(ld["id"], 16)
            act.dma_start(WQ[:, :], wq).then_inc(ld["wqk"], 16)
            act.dma_start(ROW[:, :], rows.broadcast_to([P, NROW])).then_inc(ld["rows"], 16)

            def split(e):
                if e:
                    act.wait_ge(q_out, 16 * NPART * e)
                    act.wait_ge(k_out, 16 * NPART * e)
                act.wait_ge(qkf, e + 1)
                act.activation(PT[:, 0, :, :], QKF[:, :, :], ACT.Copy).then_inc(part1, 1)

            def split_second(e):
                act.wait_ge(rest1, e + 1)
                act.activation(PT[:, 1, :, :], R1[:, :, :], ACT.Copy).then_inc(part2, 1)

            def load_expert(n):
                act.wait_ge(experts_of, 1)
                return act.value_load(EJI[0:1, n:n + 1], min_val=0, max_val=E - 1)

            def copy_expert(n):
                expert = load_expert(n)
                if n >= WRING:
                    act.wait_ge(aj, n - WRING + 1)
                act.activation(WJ[n % WRING][:, :], W1[:, :, :].rearrange("p e f -> p (e f)")
                               [:, bass.ds(expert * W1C, W1C)], ACT.Copy).then_inc(wj, 1)

            def expert_step(s):
                if s == -1:
                    act.wait_ge(ld["w1"], 16 * E)
                    copy_expert(0)
                    copy_expert(1)
                if has_tile(s):
                    n = s
                    act.wait_ge(wj, n + 1)
                    act.wait_ge(u_ps, n + 1)
                    for c in range(2):
                        last = act.activation(SJ[n % 2][:, P * c:P * c + P], U[n % 2][:, HID + P * c:HID + P * c + P],
                                              ACT.Sigmoid, bias=WJ[n % WRING][:, W1_B + 2 + c:W1_B + 3 + c])
                    last.then_inc(sj, 1)
                    if has_tile(n + 2):
                        copy_expert(n + 2)

            def qkf_free(e):
                if e:
                    act.wait_ge(rest1, e)
                    act.wait_ge(part1, e)

            for k in range(SLOTS):
                for i in HALVES:
                    if attention_at(k, i):
                        e, beat = attention_at(k, i)
                        g = BEATS * e + beat
                        w = 4 * T if e < B or beat % 2 == 0 else 4 * P
                        act.wait_ge(scores, g + 1)
                        if g >= PRING:
                            act.wait_ge(pv, g - PRING + 1)
                        act.activation(EX[g % PRING][:, 0:w], S[g % 2][:, 0:w], ACT.Exp).then_inc(probs, 1)
                    b = at("o_sb", k, i)
                    if b is not None:
                        act.wait_ge(pv, BEATS * (b + 1))
                        if b:
                            act.wait_ge(o_t, b)
                        act.activation(OS[:, :], O[:, :], ACT.Copy).then_inc(o_sb, 1)
                    e = maxima_done(k, i, 0.5)
                    if e is not None:
                        act.wait_ge(m_t, e + 1)
                        if e:
                            act.wait_ge(m_rows[(e - 1) % RING], 32 * ring_uses(e - 1))
                        act.activation(MTS[:, :], MSB[0:2 * TT * H, 0:P], ACT.Copy).then_inc(mts, 1)
                    b = project_at(k, i, A_XN)
                    if b is not None:
                        act.wait_ge(xn_t, b + 1)
                        if b:
                            act.wait_ge(qk_ps, b)
                        act.activation(XNT[:, :], MS[:, 0:T], ACT.Copy).then_inc(xnt, 1)
                    b = project_at(k, i, A_QK)
                    if b is not None:
                        act.wait_ge(qk_ps, b + 1)
                        act.wait_ge(cst, 1)
                        act.wait_ge(ld["cols"], 16)
                        qkf_free(b)
                        act.activation(QKF[:, 0, :], MS[:, 0:T], ACT.Identity, bias=QBS[:, :], scale=SCALE)
                        act.activation(QKF[:, 1, :], MS[:, T:2 * T], ACT.Identity,
                                       bias=COL[:, C_KB:C_KB + 1]).then_inc(qkf, 1)
                        split(b)
                    b = at("hz_t", k, i)
                    if b is not None:
                        act.wait_ge(hz_t, b + 1)
                        if b:
                            act.wait_ge(qkv_ps, b)
                        act.activation(HT[:, :], MS[:, 0:T], ACT.Copy, scale=COL[:, C_LN1:C_LN1 + 1]).then_inc(ht, 1)
                    b = at("qn_t", k, i)
                    if b is not None:
                        act.wait_ge(qn_t, b + 1)
                        qkf_free(b + 4)
                        act.activation(QKF[:, 0, :], MS[:, 0:T], ACT.Copy, scale=QNS[:, :])
                        act.activation(QKF[0:G * HD, 1, :], MS[0:G * HD, T:2 * T], ACT.Copy,
                                       scale=COL[0:G * HD, C_KN:C_KN + 1]).then_inc(qkf, 1)
                        split(b + B)
                    b = at("split2", k, i)
                    if b is not None:
                        split_second(b + B)
                    b = project_at(k, i, A_SPLIT)
                    if b is not None:
                        split_second(b)
                    b = at("wo", k, i)
                    if b is not None:
                        act.wait_ge(xp, b + 1)
                        if b:
                            act.wait_ge(rstd3, b)
                        for t in range(TT):
                            last = act.activation(TH[:, P * t:P * t + P], XP[:, t, :], ACT.Square,
                                                  accum_out=SS3[:, 0, t:t + 1])
                        last.then_inc(ss3, 1)
                    b = at("xp_t", k, i)
                    if b is not None:
                        act.wait_ge(xp_t, b + 1)
                        if b:
                            act.wait_ge(lg_ps, b)
                        act.activation(XPT[:, :], MS[:, 0:T], ACT.Copy,
                                       scale=COL[:, C_LN2:C_LN2 + 1]).then_inc(xpt, 1)
                    b = at("on_t", k, i)
                    if b is not None:
                        act.wait_ge(on_t, b + 1)
                        if 0 < b <= B:
                            act.wait_ge(pj, b)
                        elif b > B:
                            act.wait_ge(gated, b - 4)
                            act.wait_ge(gate_ps, b - 4)
                        act.activation(ONT[:, :], MS[:, 0:T], ACT.Copy).then_inc(ont, 1)
                    b = at("gate", k, i)
                    if b is not None:
                        act.wait_ge(gate_ps, b + 1)
                        if b:
                            act.wait_ge(gated, b)
                            act.wait_ge(ss3, b)
                        act.activation(TH[:, :], MS[:, 0:T], ACT.Tanh, bias=BGH[:, :], scale=0.5).then_inc(th, 1)
                    if routing(k, i):
                        act.wait_ge(ld["cols"], 16)
                        act.activation(WARM[:, :], COL[:, C_QB:C_QB + 1], ACT.Sigmoid)
                    for s in expert_steps(k, i):
                        expert_step(s)
            for s in expert_steps(SLOTS, 0):
                expert_step(s)

        @block.vector
        def _(dve):
            n = [0]

            def link(ins):
                n[0] += 1
                ins.then_inc(dve_step, 1)
                dve.wait_ge(dve_step, n[0])

            def statistics(src, st, mv):
                for t in range(TT):
                    last = dve.bn_stats(st[:, t, :], src[:, t, :])
                link(last)
                for t in range(TT):
                    last = dve.bn_aggr(mv[:, t, :], st[:, t, :])
                return last

            def maxima(e, k):
                heads, q, w = bank_of(e, k)
                g = banks_before(e) + k
                if k == 0 and e:
                    dve.wait_ge(mhl, e)
                dve.wait_ge(mx_scores, g + 1)
                dve.tensor_reduce(out=NEGM[:, q, heads[0]:heads[-1] + 1],
                                  in_=MX[g % 2][:, 0:len(heads) * w].rearrange("p (h t) -> p h t", t=w),
                                  axis=AX.X, op=ALU.max, negate=True).then_inc(mx_taken, 1)

            def minus_maxima(e):
                dve.wait_ge(mx_taken, banks_before(e + 1))
                if e:
                    dve.wait_ge(m_t, e)
                link(dve.tensor_copy(MHL[:, 0, :, :], NEGM[:, :, :].rearrange("p q h -> p h q")))
                dve.tensor_tensor(MHL[:, 1, :, :], NEGM[:, :, :].rearrange("p q h -> p h q"), MHL[:, 0, :, :],
                                  ALU.subtract).then_inc(mhl, 1)

            def split_on_dve(e):
                dve.wait_ge(part1, e + 1)
                dve.tensor_tensor(R1[:, :, :], QKF[:, :, :], PT[:, 0, :, :], ALU.subtract).then_inc(rest1, 1)
                dve.wait_ge(rest1, e + 1)
                dve.wait_ge(part2, e + 1)
                dve.tensor_tensor(PT[:, 2, :, :], R1[:, :, :], PT[:, 1, :, :], ALU.subtract).then_inc(part3, 1)

            def values(b):
                dve.wait_ge(v_ps, b + 1)
                dve.wait_ge(va_zero, 4 * (b % RING) + 2)
                dve.wait_ge(ld["rows"], 16)
                if b >= RING:
                    dve.wait_ge(pv, BEATS * (b - RING + 1))
                for s in range(2):
                    for t in range(TT):
                        last = dve.tensor_tensor(
                            VA[b % RING][:, t, :, 8 * s:8 * s + 8]
                            .rearrange("p (r s j) c -> p r s j c", s=2, j=4)[:, :, s, :, :],
                            MS[:, C * t:C * t + C].rearrange("p (r s j c) -> p r s j c", s=2, j=4, c=HD)[:, :, s, :, :],
                            ROW[:, R_VB:R_VB + C].rearrange("p (r s j c) -> p r s j c", s=2, j=4, c=HD)[:, :, s, :, :],
                            ALU.add)
                last.then_inc(va, 1)

            def total(out_, in_):
                return dve.tensor_reduce(out=out_, in_=in_, axis=AX.X, op=ALU.add)

            def route():
                oh_ = OH[:, :, :]
                number = NUM[:, N_I:N_I + P]
                dve.wait_ge(ld["num"], 16)
                dve.wait_ge(ranks, 1)
                link(dve.tensor_copy(CNT[:, :], MX[0][:, NT * E:NT * E + E]))
                dve.tensor_tensor(PICK[:, 0, :, :], MX[0][:, 0:NT * E].rearrange("p (t e) -> p t e", e=E), oh_,
                                  ALU.mult)
                link(dve.tensor_tensor(OVER[:, :, :], CNT[:, :, None].broadcast_to([P, E, NT]),
                                       number[:, None, 0:NT].broadcast_to([P, E, NT]), ALU.is_gt))
                total(RANK[:, 0, :], PICK[:, 0, :, :])
                link(total(TILES[:, :], OVER[:, :, :]))
                dve.tensor_tensor(PAST[:, :, :], RANK[:, 0, :, None].broadcast_to([P, NT, NT - 1]),
                                  number[:, None, 1:NT].broadcast_to([P, NT, NT - 1]), ALU.is_ge)
                link(dve.tensor_tensor(BEFT[:, :, :],
                                       NUM[:, N_BEF:N_BEF + E * E].rearrange("p (e f) -> p e f", e=E),
                                       TILES[:, None, :].broadcast_to([P, E, E]), ALU.mult))
                total(SLOT[:, 0, :], PAST[:, :, :])
                link(total(FIRST[:, :], BEFT[:, :, :]))
                dve.tensor_tensor(SLOT[:, 1, :], RANK[:, 0, :], SLOT[:, 0, :], ALU.subtract)
                link(dve.tensor_tensor(PICK[:, 1, :, :], oh_, FIRST[:, None, :].broadcast_to([P, NT, E]), ALU.mult))
                link(total(RANK[:, 1, :], PICK[:, 1, :, :]))
                link(dve.tensor_tensor(RANK[:, 1, :], RANK[:, 1, :], SLOT[:, 0, :], ALU.add))
                link(dve.tensor_tensor(INTILE[:, :, 0, :], number[:, None, 0:ET].broadcast_to([P, NT, ET]),
                                       RANK[:, 1, :, None].broadcast_to([P, NT, ET]), ALU.is_equal))
                dve.tensor_tensor(INROW[:, :, :], NUM[:, None, N_IP:N_IP + P].broadcast_to([P, NT, P]),
                                  SLOT[:, 1, :, None].broadcast_to([P, NT, P]), ALU.is_equal)
                dve.tensor_scalar(INTILE[:, :, 1, :], INTILE[:, :, 0, :], COL[:, C_P:C_P + 1], None, ALU.mult)
                dve.tensor_tensor(INTILE[:, :, 2, :], INTILE[:, :, 0, :],
                                  number[:, 0:NT, None].broadcast_to([P, NT, ET]), ALU.mult).then_inc(places, 1)
                link(dve.tensor_tensor(AFTER[:, :, :], number[:, 0:ET, None].broadcast_to([P, ET, E - 1]),
                                       FIRST[:, None, 1:E].broadcast_to([P, ET, E - 1]), ALU.is_ge))
                link(total(EJ[:, :], AFTER[:, :, :]))
                dve.tensor_copy(EJI[:, :], EJ[0:1, :]).then_inc(experts_of, 1)

            def indices():
                dve.wait_ge(ids, 1)
                link(dve.tensor_copy(IDS[:, :, :], MX[1][:, 0:3 * ET].rearrange("p (a j) -> p a j", a=3)))
                dve.scalar_tensor_tensor(IDX[:, 0, :], IDS[:, 2, :], float(P), IDS[:, 1, :], ALU.mult, ALU.add)\
                    .then_inc(idx, 1)
                link(dve.scalar_tensor_tensor(IDF[:, 0, :], IDS[:, 2, :], float(P), IDS[:, 1, :], ALU.mult, ALU.add))
                link(dve.scalar_tensor_tensor(IDF[:, 1, :], IDS[:, 0, :], -float(SKIP), IDF[:, 0, :],
                                              ALU.mult, ALU.add))
                dve.tensor_scalar(IDX[:, 1, :], IDF[:, 1, :], float(SKIP), None, ALU.add).then_inc(idx_out, 1)

            def expert_step(s):
                if has_tile(s + 1):
                    n = s + 1
                    dve.wait_ge(tr_ps, n + 1)
                    if n >= 2:
                        dve.wait_ge(u_ps, n - 1)
                    dve.tensor_scalar(HJ[n % 2][:, :], TRJ, COL[:, C_LN2:C_LN2 + 1], None, ALU.mult).then_inc(hj, 1)
                if has_tile(s):
                    n = s
                    dve.wait_ge(sj, n + 1)
                    if n >= 2:
                        dve.wait_ge(y_ps, n - 1)
                    for c in range(2):
                        last = dve.scalar_tensor_tensor(AJ[n % 2][:, P * c:P * c + P], U[n % 2][:, P * c:P * c + P],
                                                        WJ[n % WRING][:, W1_B + c:W1_B + c + 1],
                                                        SJ[n % 2][:, P * c:P * c + P], ALU.add, ALU.mult)
                    last.then_inc(aj, 1)
                if has_tile(s - 1):
                    n = s - 1
                    dve.wait_ge(y_ps, n + 1)
                    dve.tensor_tensor(rows_of(n, C, 2 * C), Y, rows_of(n, C, 2 * C), ALU.add).then_inc(done, 1)

            for k in range(SLOTS):
                for i in HALVES:
                    b = project_at(k, i, A_STATS)
                    if b is not None:
                        dve.wait_ge(ld["x1" if b else "x0"], 16)
                        if b:
                            dve.wait_ge(rstd1, b)
                        statistics(X[:, TT * b:TT * b + TT, :], ST, MV1).then_inc(mv1, 1)
                    e = maxima_done(k, i)
                    if e is not None:
                        minus_maxima(e)
                    e, banks = banks_at(k, i)
                    for kk in banks:
                        maxima(e, kk)
                    b = project_at(k, i, A_XN)
                    if b is not None:
                        dve.wait_ge(rstd1, b + 1)
                        if b:
                            dve.wait_ge(xn_t, b)
                        for t in range(TT):
                            last = dve.tensor_scalar(XN[:, t, :], X[:, TT * b + t, :], MV1[:, t, 0:1],
                                                     SM1[:, 0, t:t + 1], ALU.subtract, ALU.mult)
                        last.then_inc(xn, 1)
                    b = project_at(k, i, A_SPLIT)
                    if b is not None and b < 2:
                        split_on_dve(b)
                    if project_at(k, i, A_V) is not None:
                        values(k)
                    b = at("qkv", k, i)
                    if b is not None:
                        dve.wait_ge(qkv_ps, b + 1)
                        if b:
                            dve.wait_ge(sq, b)
                            dve.wait_ge(vb, 2 * b)
                            dve.wait_ge(rots, b)
                        dve.tensor_tensor(QKVS[:, :, :], MS[:, 0:TT * QKV].rearrange("p (t c) -> p t c", t=TT),
                                          ROW[:, None, R_BQKV:R_BQKV + QKV].broadcast_to([P, TT, QKV]), ALU.add)\
                            .then_inc(qkvs, 1)
                        dve.wait_ge(qkvs, b + 1)
                        dve.wait_ge(ld["rope"], 16)
                        qk = QKVS[:, :, 0:NH2 * HD].rearrange("p t (c h) -> p t c h", c=HD)
                        dve.tensor_tensor(ROT[:, :, :, :], qk,
                                          ROPE[:, :, 0, :, None].broadcast_to([P, TT, HD, NH2]), ALU.mult)
                    b = at("squares", k, i)
                    if b is not None:
                        dve.wait_ge(sq, b + 1)
                        dve.tensor_reduce(out=SSQ[:, :], in_=SQ[:, :, :].rearrange("p t (c h) -> p t h c", c=HD),
                                          axis=AX.X, op=ALU.add).then_inc(ssq, 1)
                        dve.wait_ge(ssq, b + 1)
                        link(dve.tensor_scalar(SSQ[:, :], SSQ[:, :], 1.0 / HD, 1e-6, ALU.mult, ALU.add))
                        link(dve.tensor_scalar(RQ[:, :].bitcast(i32), SSQ[:, :].bitcast(i32), 1, None,
                                               ALU.logical_shift_right))
                        link(dve.tensor_scalar(RQ[:, :].bitcast(i32), RQ[:, :].bitcast(i32), -1.0, float(0x5F3759DF),
                                               ALU.mult, ALU.add))
                    for step in range(1, NEWTON + 1):
                        b = at(f"newton{step}", k, i)
                        if b is not None:
                            link(dve.scalar_tensor_tensor(RT[:, :], RQ[:, :], -0.5, RQ[:, :], ALU.mult, ALU.mult))
                            link(dve.tensor_tensor(RT[:, :], RT[:, :], SSQ[:, :], ALU.mult))
                            link(dve.scalar_tensor_tensor(RQ[:, :], RT[:, :], 1.5, RQ[:, :], ALU.add, ALU.mult))
                    if b is not None:
                        if b:
                            dve.wait_ge(qn_t, b)
                        dve.wait_ge(rots, b + 1)
                        link(dve.tensor_tensor(ROT[:, :, :, :], ROT[:, :, :, :], ROTS[:, :, :, :], ALU.add))
                        rq_ = RQ[:, :].rearrange("p (t h) -> p t h", t=TT)
                        dve.tensor_tensor(QN[:, :, 0:C].rearrange("p t (c h) -> p t c h", c=HD), ROT[:, :, :, 0:H],
                                          rq_[:, :, None, 0:H].broadcast_to([P, TT, HD, H]), ALU.mult)
                        dve.tensor_tensor(QN[:, :, C:C + G * HD].rearrange("p t (c h) -> p t c h", c=HD),
                                          ROT[:, :, :, H:NH2],
                                          rq_[:, :, None, H:NH2].broadcast_to([P, TT, HD, G]), ALU.mult).then_inc(qn, 1)
                    b = at("wo", k, i)
                    if b is not None:
                        dve.wait_ge(wo_ps, b + 1)
                        dve.wait_ge(z_ready, b + 1)
                        if b:
                            dve.wait_ge(h2, b)
                            dve.wait_ge(xp_t, b)
                            dve.wait_ge(rr, b)
                            dve.wait_ge(ss3, b)
                        dve.scalar_tensor_tensor(XP[:, :, :], MS[:, 0:T].rearrange("p (t c) -> p t c", t=TT), 0.5,
                                                 ZB[:, TT * b:TT * b + TT, :], ALU.mult, ALU.add).then_inc(xp, 1)
                    b = at("h2", k, i)
                    if b is not None:
                        dve.wait_ge(rstd3, b + 1)
                        for t in range(TT):
                            last = dve.tensor_scalar(HR[:, TT * b + t, 0, :], XP[:, t, :], SS3[:, 1, t:t + 1], None, ALU.mult)
                        last.then_inc(h2, 1)
                    b = at("router", k, i)
                    if b is not None:
                        dve.wait_ge(lg_ps, b + 1)
                        dve.wait_ge(rstd3, b + 1)
                        for t in range(TT):
                            last = dve.scalar_tensor_tensor(LG[:, t, :], MS[:, E * t:E * t + E], SS3[:, 1, t:t + 1],
                                                            ROW[:, R_BR:R_BR + E], ALU.mult, ALU.add)
                        link(last)
                        link(dve.tensor_reduce(out=MXL[:, 0, :], in_=LG[:, :, :], axis=AX.X, op=ALU.max))
                        link(dve.tensor_tensor(EQ[:, :, :], LG[:, :, :],
                                               MXL[:, 0, :, None].broadcast_to([P, TT, E]), ALU.is_equal))
                        dve.wait_ge(ld["rev"], 16)
                        link(dve.tensor_tensor(EQ[:, :, :], EQ[:, :, :],
                                               REV[:, None, :].broadcast_to([P, TT, E]), ALU.mult))
                        link(dve.tensor_reduce(out=MXL[:, 1, :], in_=EQ[:, :, :], axis=AX.X, op=ALU.max))
                        dve.tensor_tensor(OH[:, TT * b:TT * b + TT, :], REV[:, None, :].broadcast_to([P, TT, E]),
                                          MXL[:, 1, :, None].broadcast_to([P, TT, E]), ALU.is_equal).then_inc(oh, 1)
                    b = at("o_t", k, i)
                    if b is not None:
                        dve.wait_ge(o_t, b + 1)
                        if b:
                            dve.wait_ge(on_t, b)
                        v = MS[:, :].rearrange("p (a c) -> p a c", c=32)
                        link(dve.reciprocal(RC[:, :, :], v[:, :, 16:18]))
                        dve.tensor_tensor(ON[:, :, :].rearrange("p a (s c) -> p a s c", s=2),
                                          v[:, :, 0:16].rearrange("p a (s c) -> p a s c", s=2),
                                          RC[:, :, :, None].broadcast_to([P, 16, 2, HD]), ALU.mult).then_inc(on, 1)
                    b = at("pj", k, i)
                    if b is not None:
                        dve.wait_ge(pj, b + 1)
                        dve.wait_ge(xb_ready, 1)
                        if b:
                            dve.wait_ge(z_ready, b)
                        dve.tensor_tensor(X1[:, TT * b:TT * b + TT, :],
                                          MS[:, 0:T].rearrange("p (t c) -> p t c", t=TT),
                                          XB[:, TT * b:TT * b + TT, :], ALU.add).then_inc(x1, 1)
                        dve.wait_ge(x1, b + 1)
                        link(statistics(X1[:, TT * b:TT * b + TT, :], ST2, MV2))
                        var = MV2[:, :, 1]
                        link(dve.tensor_scalar(SM2[:, 1, :], var, 1e-5, 1e-6, ALU.add, ALU.mult))
                        dve.tensor_scalar(SM2[:, 0, :], var, 1e-5, None, ALU.add)
                        dve.tensor_tensor(SM2[:, 1, :], SM2[:, 1, :], var, ALU.add).then_inc(mv2, 1)
                    b = at("hz", k, i)
                    if b is not None:
                        dve.wait_ge(rstd2, b + 1)
                        if b:
                            dve.wait_ge(hz_t, b)
                        else:
                            dve.wait_ge(xn_t, B)
                        for t in range(TT):
                            last = dve.tensor_scalar(HZ[:, t, :], X1[:, TT * b + t, :], MV2[:, t, 0:1],
                                                     SM2[:, 3, t:t + 1], ALU.subtract, ALU.mult)
                        last.then_inc(hz, 1)
                    b = at("gate", k, i)
                    if b is not None:
                        dve.wait_ge(th, b + 1)
                        if b:
                            dve.wait_ge(wo_ps, b)
                        dve.scalar_tensor_tensor(GT[:, :], TH[:, :], 1.0, ONT[:, :], ALU.add, ALU.mult)\
                            .then_inc(gated, 1)
                    if routing(k, i):
                        route()
                    if routing(k, i, 3):
                        indices()
                    for s in expert_steps(k, i):
                        expert_step(s)
            for s in expert_steps(SLOTS, 0):
                expert_step(s)

        @block.tensor
        def _(pe):
            last_reader = [None]

            def take_misc(reader, count):
                if last_reader[0]:
                    pe.wait_ge(*last_reader[0])
                last_reader[0] = (reader, count)

            def mm(out_, lhsT, rhs, start=True, stop=True, **kw):
                return nc.tensor.matmul(out_, lhsT, rhs, start=start, stop=stop, **kw)

            def transposes(done, src, w=C):
                for t in range(TT):
                    last = nc.tensor.transpose(MS[:, P * t:P * t + P], src[:, t, :], ID[:, :])
                last.then_inc(done, 1)

            def score_beat(e, i):
                u, kt = i // 2, i % 2
                g = BEATS * e + i
                if i == 0:
                    pe.wait_ge(m_rows[e % RING], 32 * ring_uses(e))
                    if e == B:
                        pe.wait_ge(ld["tri"], 16)
                if g >= 2:
                    pe.wait_ge(probs, g - 1)
                qa, ka = QA[e % RING], KA[e % RING]
                for j in range(4):
                    if e < B:
                        last = mm(S[g % 2][:, T * j:T * j + T], ka[:, 4 * u + j, P * kt:P * kt + P], qa[:, 4 * u + j, :])
                    elif kt == 0:
                        if j % 2 == 0:
                            last = mm(S[g % 2][:, T * j:T * j + 2 * T], ka[:, u, 0:P],
                                      qa[:, 4 * u + j:4 * u + j + 2, :])
                    elif j == 0:
                        last = mm(S[g % 2][:, 0:4 * P], ka[:, u, P:T], qa[:, 4 * u:4 * u + 4, P:T])
                last.then_inc(scores, 1)

            def max_bank(e, k):
                heads, q, w = bank_of(e, k)
                g = banks_before(e) + k
                if k == 0:
                    pe.wait_ge(stacked[e % RING], 32 * ring_uses(e))
                    if e == 0:
                        pe.wait_ge(ld["pad"], 32 * RING)
                if g >= 2:
                    pe.wait_ge(mx_taken, g - 1)
                qa, ka, m = QA[e % RING], KA[e % RING], MX[g % 2]
                causal = e >= B
                for slot, h in enumerate(heads):
                    last = mm(m[:, w * slot:w * slot + w], qa[:, h, P * q:P * q + P], ka[:, h if e < B else h // 4, 0:w],
                              stop=not causal, skip_group_check=causal, start=not causal or slot == 0)
                if causal:
                    if e == B and k == 0:
                        pe.wait_ge(cst, 8)
                    nh = len(heads)
                    last = mm(m[:, 0:nh * w].rearrange("p (h t) -> p h t", t=w)[:, :, w - P:w], IDB[:, :],
                              TRIB[:, 0:nh, :], start=False, skip_group_check=True)
                last.then_inc(mx_scores, 1)

            def pv_beat(e, i):
                u, kt = i // 2, i % 2
                g = BEATS * e + i
                r, s = u // 2, u % 2
                if i == 0:
                    if e < B:
                        pe.wait_ge(va, e + 1)
                    else:
                        pe.wait_ge(vb, 2 * (e - B + 1))
                    if e:
                        pe.wait_ge(o_sb, e)
                if e < B:
                    pe.wait_ge(probs, g + 1)
                else:
                    pe.wait_ge(masked, g - BEATS * B + 1)
                w, q0 = (T, 0) if e < B or kt == 0 else (P, P)
                for j in range(4):
                    V_ = VA[e % RING][:, kt, 4 * u + j, :] if e < B else VB[e - B][:, kt, u, :]
                    last = mm(O[32 * j:32 * j + 32, T * r + q0:T * r + q0 + w], V_,
                              EX[g % PRING][:, w * j:w * j + w], start=s == 0 and kt == 0, stop=s == 1 and kt == 1,
                              tile_position=(0, 32 * j), skip_group_check=True)
                last.then_inc(pv, 1)

            def rank_tokens():
                pe.wait_ge(route_cst, 3)
                pe.wait_ge(mx_taken, banks_before(NE))
                pe.wait_ge(oh, B)
                rank = MX[0][:, 0:NT * E].rearrange("p (t e) -> p t e", e=E)
                mm(rank, BEFB[:, :], OH[:, :, :], stop=False, skip_group_check=True)
                for t in range(NT):
                    oh_ = OH[:, t:t + 1, :]
                    if t < NT - 1:
                        later = NT - 1 - t
                        mm(rank[:, t + 1:NT, :], PARTB[:, :], oh_.broadcast_to([P, later, E]), start=False,
                           skip_group_check=True)
                    last = mm(MX[0][:, NT * E:NT * E + E], PARTB[:, :], oh_[:, 0, :], start=False,
                              skip_group_check=True)
                last.then_inc(ranks, 1)

            def name_slots():
                pe.wait_ge(places, 1)
                for t in range(NT):
                    last = mm(MX[1][:, 0:3 * ET], INROW[:, t, :], INTILE[:, t, :, :].rearrange("p a j -> p (a j)"),
                              start=t == 0, stop=t == NT - 1)
                last.then_inc(ids, 1)

            expert = {}

            def load_expert(n):
                pe.wait_ge(experts_of, 1)
                expert[n] = pe.value_load(EJI[0:1, n:n + 1], min_val=0, max_val=E - 1)

            W2F = W2[:, :, :, :].rearrange("p e k c -> p (e k c)")

            def expert_step(s):
                if s == -1:
                    pe.wait_ge(ld["w2"], 16 * E)
                    pe.wait_ge(bias_rows, 16 * NPART)
                    pe.wait_ge(probs, BEATS * NE)
                if has_tile(s + 1):
                    n = s + 1
                    pe.wait_ge(gathered[n], 16)
                    if n:
                        pe.wait_ge(hj, n)
                    nc.tensor.transpose(TRJ, rows_of(n, 0, C), ID[:, :]).then_inc(tr_ps, 1)
                if has_tile(s):
                    n = s
                    pe.wait_ge(hj, n + 1)
                    pe.wait_ge(wj, n + 1)
                    if n >= 2:
                        pe.wait_ge(aj, n - 1)
                    for c in range(2 * HID // P):
                        last = mm(U[n % 2][:, P * c:P * c + P], WJ[n % WRING][:, P * c:P * c + P], HJ[n % 2][:, :])
                    last.then_inc(u_ps, 1)
                    load_expert(n)
                if has_tile(s - 1):
                    n = s - 1
                    pe.wait_ge(aj, n + 1)
                    if n:
                        pe.wait_ge(done, n)
                    else:
                        pe.wait_ge(o_sb, NE)
                    mm(Y, ONEB[0:KROWS, :], BROW[:, bass.ds(expert[n] * C, C)], stop=False)
                    for c in range(2):
                        last = mm(Y, AJ[n % 2][:, P * c:P * c + P],
                                  W2F[:, bass.ds(expert[n] * (2 * C) + C * c, C)], start=False, stop=c == 1)
                    last.then_inc(y_ps, 1)

            for k in range(SLOTS):
                for i in HALVES:
                    e, banks = banks_at(k, i)
                    for kk in banks:
                        max_bank(e, kk)
                    if attention_at(k, i):
                        score_beat(*attention_at(k, i))
                    if attention_at(k, i, 2.5):
                        pv_beat(*attention_at(k, i, 2.5))
                    e = maxima_done(k, i, 0.5)
                    if e is not None:
                        take_misc(mts, e + 1)
                        pe.wait_ge(mhl, e + 1)
                        if e == 0:
                            pe.wait_ge(cst, 4)
                        nc.tensor.transpose(MSB[0:2 * TT * H, 0:P], MHL[:, :, :, :].rearrange("p a h t -> p (a h t)"),
                                            IDB[:, :]).then_inc(m_t, 1)
                    b = project_at(k, i, A_XN)
                    if b is not None:
                        if b == 0:
                            pe.wait_ge(ld["id"], 16)
                        take_misc(xnt, b + 1)
                        pe.wait_ge(xn, b + 1)
                        transposes(xn_t, XN)
                    b = project_at(k, i, A_QK)
                    if b is not None:
                        if b == 0:
                            pe.wait_ge(ld["wqk"], 32)
                            pe.wait_ge(ld["ctx"], 16)
                        take_misc(qkf, b + 1)
                        mm(MS[:, 0:T], WQ[:, :], XNT[:, :])
                        mm(MS[:, T:2 * T], WK[:, :], CT[:, T * b:T * b + T]).then_inc(qk_ps, 1)
                    if project_at(k, i, A_V) is not None:
                        if k == 0:
                            pe.wait_ge(ld["wv"], 16)
                        take_misc(va, k + 1)
                        for t in range(TT):
                            last = mm(MS[:, C * t:C * t + C], CT[:, T * k + P * t:T * k + P * t + P], WV[:, :])
                        last.then_inc(v_ps, 1)
                    b = at("hz_t", k, i)
                    if b is not None:
                        take_misc(ht, b + 1)
                        pe.wait_ge(hz, b + 1)
                        transposes(hz_t, HZ)
                    b = at("qkv", k, i)
                    if b is not None:
                        if b == 0:
                            pe.wait_ge(ld["wqkv"], 16)
                        take_misc(qkvs, b + 1)
                        for t in range(TT):
                            last = mm(MS[:, QKV * t:QKV * t + QKV], HT[:, P * t:P * t + P], WQKV[:, :])
                        last.then_inc(qkv_ps, 1)
                    b = at("qn_t", k, i)
                    if b is not None:
                        take_misc(qkf, b + B + 1)
                        pe.wait_ge(qn, b + 1)
                        for t in range(TT):
                            nc.tensor.transpose(MS[:, P * t:P * t + P], QN[:, t, 0:C], ID[:, :])
                            last = nc.tensor.transpose(MS[0:G * HD, T + P * t:T + P * t + P],
                                                       QN[:, t, C:C + G * HD], ID[:, :])
                        last.then_inc(qn_t, 1)
                    b = at("wo", k, i)
                    if b is not None:
                        take_misc(xp, b + 1)
                        pe.wait_ge(gated, b + 1)
                        if b == 0:
                            pe.wait_ge(ld["wo"], 16)
                        for t in range(TT):
                            last = mm(MS[:, C * t:C * t + C], GT[:, P * t:P * t + P], WO[:, :])
                        last.then_inc(wo_ps, 1)
                    b = at("xp_t", k, i)
                    if b is not None:
                        take_misc(xpt, b + 1)
                        pe.wait_ge(xp, b + 1)
                        transposes(xp_t, XP)
                    b = at("router", k, i)
                    if b is not None:
                        if b == 0:
                            pe.wait_ge(ld["wr"], 16)
                        take_misc(oh, b + 1)
                        pe.wait_ge(xpt, b + 1)
                        for t in range(TT):
                            last = mm(MS[:, E * t:E * t + E], XPT[:, P * t:P * t + P], WR[:, :])
                        last.then_inc(lg_ps, 1)
                    b = at("o_t", k, i)
                    if b is not None:
                        take_misc(on, b + 1)
                        pe.wait_ge(o_sb, b + 1)
                        for t in range(TT):
                            for r in range(2):
                                last = nc.tensor.transpose(MS[:, P * (2 * t + r):P * (2 * t + r) + P],
                                                           OS[:, T * r + P * t:T * r + P * t + P], ID[:, :])
                        last.then_inc(o_t, 1)
                    b = at("on_t", k, i)
                    if b is not None:
                        take_misc(ont, b + 1)
                        pe.wait_ge(on, b + 1)
                        for t in range(TT):
                            last = nc.tensor.transpose(MS[:, P * t:P * t + P],
                                                       ON[:, 8 * t:8 * t + 8, :].rearrange("p a c -> p (a c)"), ID[:, :])
                        last.then_inc(on_t, 1)
                    b = at("pj", k, i)
                    if b is not None:
                        if b == 0:
                            pe.wait_ge(ld["wp"], 16)
                        take_misc(x1, b + 1)
                        pe.wait_ge(ont, b + 1)
                        for t in range(TT):
                            last = mm(MS[:, C * t:C * t + C], ONT[:, P * t:P * t + P], WP[:, :])
                        last.then_inc(pj, 1)
                    b = at("gate", k, i)
                    if b is not None:
                        if b == 0:
                            pe.wait_ge(ld["wg"], 16)
                        take_misc(th, b + 1)
                        pe.wait_ge(ont, b + 5)
                        mm(MS[:, 0:T], WG[:, :], ONT[:, :]).then_inc(gate_ps, 1)
                    if routing(k, i):
                        rank_tokens()
                    if routing(k, i, 2):
                        name_slots()
                    for s in expert_steps(k, i):
                        expert_step(s)
            for s in expert_steps(SLOTS, 0):
                expert_step(s)


_INS = ("x", "ctxT", "cols", "rows", "wq", "wk", "wv", "wp", "wqkv", "wg", "wo", "wr", "w1", "w2", "b2",
        "ident", "tri", "rope", "revs", "numbers", "ones_row", "zero_row")


def rope_table():
    inv = (1.0 / 10000.0 ** (np.arange(0, HD, 2, dtype=np.float32) / HD)).astype(np.float32)
    f = np.arange(T, dtype=np.float32)[:, None] * inv[None, :]
    c, s = np.cos(f).astype(np.float32), np.sin(f).astype(np.float32)
    return np.stack([np.concatenate([c, c], 1), np.concatenate([-s, s], 1)], 1)


def layout(x, ctx_768, L0_xattn_q_w, L0_xattn_q_b, L0_xattn_kv_w, L0_xattn_kv_b, L0_xattn_proj_w,
           L0_xattn_proj_b, L0_ffn_ln1_w, L0_ffn_ln2_w, L0_ffn_Wq, L0_ffn_bq, L0_ffn_Wk, L0_ffn_bk,
           L0_ffn_Wv, L0_ffn_bv, L0_ffn_qn_w, L0_ffn_kn_w, L0_ffn_Wg, L0_ffn_bg, L0_ffn_Wo, L0_ffn_bo,
           L0_ffn_Wr, L0_ffn_br, L0_ffn_W1, L0_ffn_b1, L0_ffn_W2, L0_ffn_b2):
    f = np.float32
    def by_quadrant(w):
        return np.ascontiguousarray(np.asarray(w).reshape(2, 2, 4, HD, C).transpose(0, 2, 1, 3, 4).reshape(C, C))

    def by_column(w):
        w = np.asarray(w)
        return w.reshape(*w.shape[:-1], -1, HD).swapaxes(-1, -2)

    def flat(w):
        return w.reshape(*w.shape[:-2], -1)

    def joint(q, k, v):
        return np.concatenate([flat(np.concatenate([by_column(q), by_column(k)], -1)), v], -1)

    cols = np.zeros((P, NCOL), f)
    cols[:, C_QB] = flat(by_column(L0_xattn_q_b))
    cols[:, C_KB] = flat(by_column(L0_xattn_kv_b[:C]))
    cols[:, C_LN1] = L0_ffn_ln1_w
    cols[:, C_LN2] = L0_ffn_ln2_w
    cols[:, C_QN] = np.repeat(L0_ffn_qn_w, H)
    cols[:G * HD, C_KN] = np.repeat(L0_ffn_kn_w, G)
    cols[:, C_BG] = np.tile(L0_ffn_bg, H)
    cols[:, C_P] = np.arange(P)
    rows = np.concatenate([L0_xattn_kv_b[C:], L0_xattn_proj_b, joint(L0_ffn_bq, L0_ffn_bk, L0_ffn_bv), L0_ffn_bo,
                           L0_ffn_br])[None, :].astype(f)
    wg = np.zeros((C, C), f)
    for h in range(H):
        wg[HD * h:HD * h + HD, HD * h:HD * h + HD] = L0_ffn_Wg
    ii = np.arange(P)
    d = {
        "x": np.asarray(x).reshape(NT, P, C).transpose(1, 0, 2),
        "ctxT": np.asarray(ctx_768).reshape(B * T, CD).T,
        "cols": cols, "rows": rows,
        "wq": flat(by_column(L0_xattn_q_w)), "wk": flat(by_column(L0_xattn_kv_w[:, :C])), "wv": L0_xattn_kv_w[:, C:],
        "wp": by_quadrant(L0_xattn_proj_w),
        "wqkv": joint(L0_ffn_Wq, L0_ffn_Wk, L0_ffn_Wv),
        "wg": wg, "wo": by_quadrant(L0_ffn_Wo), "wr": L0_ffn_Wr,
        "w1": np.concatenate([np.asarray(L0_ffn_W1).transpose(1, 0, 2),
                              np.asarray(L0_ffn_b1).reshape(E, 2 * HID // P, P).transpose(2, 0, 1)], 2),
        "w2": np.asarray(L0_ffn_W2).reshape(E, 2, P, C).transpose(2, 0, 1, 3),
        "b2": L0_ffn_b2,
        "ident": np.eye(P, dtype=f),
        "tri": np.where(ii[None, :] > ii[:, None], -1e30, 0.0).astype(f),
        "rope": rope_table().reshape(TT, P, 2, HD).transpose(1, 0, 2, 3),
        "revs": np.arange(E, 0, -1, dtype=f)[None, :],
        "numbers": np.concatenate([ii, ii / P, (ii[None, :E] < ii[:E, None]).ravel()]).astype(f)[None, :],
        "ones_row": np.full((1, H * T // 2), 0x3F803F80, np.uint32).view(f),
        "zero_row": np.zeros((1, H * T // 2), f),
    }
    return {k: np.ascontiguousarray(v) for k, v in d.items()}


def program(nc, shapes):
    aps = [nc.dram_tensor(f"in_{k}", s, d, kind="ExternalInput").ap() for k, s, d in shapes]
    bf16 = mybir.dt.bfloat16
    q_rows = nc.dram_tensor("q_rows", [2 * B, NPART, NPART, H * HD, T], bf16, kind="Internal").ap()
    k_rows = nc.dram_tensor("k_rows", [B, NPART, NPART, H * HD, T], bf16, kind="Internal").ap()
    k2_rows = nc.dram_tensor("k2_rows", [B, NPART, NPART, G * HD, T], bf16, kind="Internal").ap()
    h_rows = nc.dram_tensor("h_rows", [B * T, 2 * C], mybir.dt.float32, kind="Internal").ap()
    out = nc.dram_tensor("out_0", [B * T, C], mybir.dt.float32, kind="ExternalOutput").ap()
    transformer(nc, *aps, q_rows, k_rows, k2_rows, h_rows, out)


def kernel(**inputs):
    import concourse.bacc as bacc
    from concourse.bass_utils import run_bass_kernel_spmd
    arrays = layout(**{k: np.asarray(v) for k, v in inputs.items()})
    nc = bacc.Bacc("TRN2", target_bir_lowering=False, num_devices=1)
    program(nc, [(k, arrays[k].shape, mybir.dt.from_np(arrays[k].dtype)) for k in _INS])
    r = run_bass_kernel_spmd(nc, [{f"in_{k}": arrays[k] for k in _INS}], core_ids=[0])
    return r.results[0]["out_0"].reshape(B, T, C)
```
